# Optimizing a Trainium2 kernel written in Bass

```python
import numpy as np
import jax
import jax.numpy as jnp

def _softmax(x, axis=-1):
    return jax.nn.softmax(x, axis=axis)

def _gelu(x):
    return jax.nn.gelu(x, approximate=True)

def _silu(x):
    return jax.nn.silu(x)

def _sigmoid(x):
    return jax.nn.sigmoid(x)

def _layernorm(x, axis=-1, eps=1e-05):
    m = jnp.mean(x, axis=axis, keepdims=True)
    v = jnp.var(x, axis=axis, keepdims=True)
    return (x - m) / jnp.sqrt(v + eps)

def _scatter_add(tgt, idx, src, axis=0):
    return tgt.at[idx].add(src)

def _segment_sum(src, seg, n):
    return jax.ops.segment_sum(src, seg, n)
kernel_name = 'mk_prb_d1_jaxref_r2_779b83'

def setup_inputs(seed: int=0):
    np.random.seed(seed)
    _w = jnp.asarray

    def _L0_attn_setup():
        import jax, jax.numpy as jnp
        import numpy as np
        D_MODEL = 512
        D_STATE = 128
        D_CONV = 4
        EXPAND = 2
        HEADDIM = 64
        D_INNER = EXPAND * D_MODEL
        NHEADS = D_INNER // HEADDIM
        CONV_DIM = D_INNER + 2 * D_STATE
        D_IN_PROJ = 2 * D_INNER + 2 * D_STATE + NHEADS
        BATCH, SEQLEN = (4, 1024)
        EPS = 1e-05

        def _layernorm(u, w, b):
            mu = u.mean(-1, keepdims=True)
            var = ((u - mu) ** 2).mean(-1, keepdims=True)
            return (u - mu) * jax.lax.rsqrt(var + EPS) * w + b

        def _mamba2_block(x, ln_w, ln_b, in_proj_w, conv_w, conv_b, A_log, D, dt_bias, gamma, out_proj_w):
            Bsz, L, _ = x.shape
            u = _layernorm(x, ln_w, ln_b)
            zxbcdt = u @ in_proj_w.T
            z = zxbcdt[..., :D_INNER]
            xBC = zxbcdt[..., D_INNER:D_INNER + CONV_DIM]
            dt = jax.nn.softplus(zxbcdt[..., -NHEADS:] + dt_bias)
            xc = jnp.pad(xBC.transpose(0, 2, 1), ((0, 0), (0, 0), (D_CONV - 1, 0)))
            xc = jax.lax.conv_general_dilated(xc, conv_w[:, None, :], (1,), 'VALID', feature_group_count=CONV_DIM, dimension_numbers=('NCH', 'OIH', 'NCH'))
            xBC = jax.nn.silu(xc.transpose(0, 2, 1) + conv_b)
            xs = xBC[..., :D_INNER].reshape(Bsz, L, NHEADS, HEADDIM)
            Bm = xBC[..., D_INNER:D_INNER + D_STATE]
            Cm = xBC[..., D_INNER + D_STATE:]
            A = -jnp.exp(A_log)
            dA = jnp.exp(dt * A)

            def step(state, inp):
                dA_t, dt_t, x_t, B_t, C_t = inp
                state = state * dA_t[:, :, None, None] + (dt_t[:, :, None] * x_t)[..., None] * B_t[:, None, None, :]
                y = jnp.einsum('bhpn,bn->bhp', state, C_t)
                return (state, y)
            init = jnp.zeros((Bsz, NHEADS, HEADDIM, D_STATE), x.dtype)
            xs_scan = (dA.transpose(1, 0, 2), dt.transpose(1, 0, 2), xs.transpose(1, 0, 2, 3), Bm.transpose(1, 0, 2), Cm.transpose(1, 0, 2))
            _, ys = jax.lax.scan(step, init, xs_scan)
            y = ys.transpose(1, 0, 2, 3) + D[None, None, :, None] * xs
            y = y.reshape(Bsz, L, D_INNER)
            y = y * jax.nn.silu(z)
            y = y * jax.lax.rsqrt(jnp.mean(y * y, -1, keepdims=True) + EPS) * gamma
            return x + y @ out_proj_w.T
        key = jax.random.key(seed)
        ks = jax.random.split(key, 8)
        x = jax.random.normal(ks[0], (BATCH, SEQLEN, D_MODEL), jnp.float32)
        ln_w = jnp.ones((D_MODEL,), jnp.float32)
        ln_b = jnp.zeros((D_MODEL,), jnp.float32)
        in_proj_w = jax.random.normal(ks[1], (D_IN_PROJ, D_MODEL), jnp.float32) * 0.02
        conv_w = jax.random.normal(ks[2], (CONV_DIM, D_CONV), jnp.float32) * 0.1
        conv_b = jnp.zeros((CONV_DIM,), jnp.float32)
        A_log = jnp.log(jax.random.uniform(ks[3], (NHEADS,), jnp.float32, 1.0, 16.0))
        D = jnp.ones((NHEADS,), jnp.float32)
        dt = jax.random.uniform(ks[4], (NHEADS,), jnp.float32, 0.001, 0.1)
        dt_bias = dt + jnp.log(-jnp.expm1(-dt))
        gamma = jnp.ones((D_INNER,), jnp.float32)
        out_proj_w = jax.random.normal(ks[5], (D_MODEL, D_INNER), jnp.float32) * 0.02
        return dict(x=x, ln_w=ln_w, ln_b=ln_b, in_proj_w=in_proj_w, conv_w=conv_w, conv_b=conv_b, A_log=A_log, D=D, dt_bias=dt_bias, gamma=gamma, out_proj_w=out_proj_w)
    _L0_attn_in = _L0_attn_setup()

    def _L0_ffn_setup():
        import jax, jax.numpy as jnp
        import numpy as np
        NQ, NK, H, DH = (512, 256, 8, 64)
        key = jax.random.key(seed)
        ks = jax.random.split(key, 8)
        b, n, d, g = (4, 2048, 512, 4)
        di = H * DH
        s = lambda fan: 1.0 / np.sqrt(fan)
        return {'x': jax.random.normal(ks[0], (b, n, d), jnp.float32), 'w_qr': jax.random.normal(ks[1], (g, d), jnp.float32) * s(d), 'w_kvr': jax.random.normal(ks[2], (g, d), jnp.float32) * s(d), 'w_q': jax.random.normal(ks[3], (g, di, d), jnp.float32) * s(d), 'w_kv': jax.random.normal(ks[4], (g, 2 * di, d), jnp.float32) * s(d), 'w_out': jax.random.normal(ks[5], (g, d, di), jnp.float32) * s(di), 'null_kv': jax.random.normal(ks[6], (2, g, H, 1, DH), jnp.float32), 'null_token': jax.random.normal(ks[7], (1, 1, d), jnp.float32)}
    _L0_ffn_in = _L0_ffn_setup()
    _d = {'L0_attn_x': _L0_attn_in['x'], 'L0_attn_ln_w': _L0_attn_in['ln_w'], 'L0_attn_ln_b': _L0_attn_in['ln_b'], 'L0_attn_in_proj_w': _L0_attn_in['in_proj_w'], 'L0_attn_conv_w': _L0_attn_in['conv_w'], 'L0_attn_conv_b': _L0_attn_in['conv_b'], 'L0_attn_A_log': _L0_attn_in['A_log'], 'L0_attn_D': _L0_attn_in['D'], 'L0_attn_dt_bias': _L0_attn_in['dt_bias'], 'L0_attn_gamma': _L0_attn_in['gamma'], 'L0_attn_out_proj_w': _L0_attn_in['out_proj_w'], 'L0_ffn_w_qr': _L0_ffn_in['w_qr'], 'L0_ffn_w_kvr': _L0_ffn_in['w_kvr'], 'L0_ffn_w_q': _L0_ffn_in['w_q'], 'L0_ffn_w_kv': _L0_ffn_in['w_kv'], 'L0_ffn_w_out': _L0_ffn_in['w_out'], 'L0_ffn_null_kv': _L0_ffn_in['null_kv'], 'L0_ffn_null_token': _L0_ffn_in['null_token']}
    _x0 = _d['L0_attn_x']
    _d['L0_attn_x'] = jax.random.normal(jax.random.fold_in(jax.random.key(seed), 1), (8, 1024, 512), dtype=_x0.dtype)
    del _x0
    return _d

def reference(L0_attn_x, L0_attn_ln_w, L0_attn_ln_b, L0_attn_in_proj_w, L0_attn_conv_w, L0_attn_conv_b, L0_attn_A_log, L0_attn_D, L0_attn_dt_bias, L0_attn_gamma, L0_attn_out_proj_w, L0_ffn_w_qr, L0_ffn_w_kvr, L0_ffn_w_q, L0_ffn_w_kv, L0_ffn_w_out, L0_ffn_null_kv, L0_ffn_null_token):

    def _L0_attn_ref(x, ln_w, ln_b, in_proj_w, conv_w, conv_b, A_log, D, dt_bias, gamma, out_proj_w):
        import jax, jax.numpy as jnp
        import numpy as np
        D_MODEL = 512
        D_STATE = 128
        D_CONV = 4
        EXPAND = 2
        HEADDIM = 64
        D_INNER = EXPAND * D_MODEL
        NHEADS = D_INNER // HEADDIM
        CONV_DIM = D_INNER + 2 * D_STATE
        D_IN_PROJ = 2 * D_INNER + 2 * D_STATE + NHEADS
        BATCH, SEQLEN = (4, 1024)
        EPS = 1e-05

        def _layernorm(u, w, b):
            mu = u.mean(-1, keepdims=True)
            var = ((u - mu) ** 2).mean(-1, keepdims=True)
            return (u - mu) * jax.lax.rsqrt(var + EPS) * w + b

        def _mamba2_block(x, ln_w, ln_b, in_proj_w, conv_w, conv_b, A_log, D, dt_bias, gamma, out_proj_w):
            Bsz, L, _ = x.shape
            u = _layernorm(x, ln_w, ln_b)
            zxbcdt = u @ in_proj_w.T
            z = zxbcdt[..., :D_INNER]
            xBC = zxbcdt[..., D_INNER:D_INNER + CONV_DIM]
            dt = jax.nn.softplus(zxbcdt[..., -NHEADS:] + dt_bias)
            xc = jnp.pad(xBC.transpose(0, 2, 1), ((0, 0), (0, 0), (D_CONV - 1, 0)))
            xc = jax.lax.conv_general_dilated(xc, conv_w[:, None, :], (1,), 'VALID', feature_group_count=CONV_DIM, dimension_numbers=('NCH', 'OIH', 'NCH'))
            xBC = jax.nn.silu(xc.transpose(0, 2, 1) + conv_b)
            xs = xBC[..., :D_INNER].reshape(Bsz, L, NHEADS, HEADDIM)
            Bm = xBC[..., D_INNER:D_INNER + D_STATE]
            Cm = xBC[..., D_INNER + D_STATE:]
            A = -jnp.exp(A_log)
            dA = jnp.exp(dt * A)

            def step(state, inp):
                dA_t, dt_t, x_t, B_t, C_t = inp
                state = state * dA_t[:, :, None, None] + (dt_t[:, :, None] * x_t)[..., None] * B_t[:, None, None, :]
                y = jnp.einsum('bhpn,bn->bhp', state, C_t)
                return (state, y)
            init = jnp.zeros((Bsz, NHEADS, HEADDIM, D_STATE), x.dtype)
            xs_scan = (dA.transpose(1, 0, 2), dt.transpose(1, 0, 2), xs.transpose(1, 0, 2, 3), Bm.transpose(1, 0, 2), Cm.transpose(1, 0, 2))
            _, ys = jax.lax.scan(step, init, xs_scan)
            y = ys.transpose(1, 0, 2, 3) + D[None, None, :, None] * xs
            y = y.reshape(Bsz, L, D_INNER)
            y = y * jax.nn.silu(z)
            y = y * jax.lax.rsqrt(jnp.mean(y * y, -1, keepdims=True) + EPS) * gamma
            return x + y @ out_proj_w.T
        return _mamba2_block(x, ln_w, ln_b, in_proj_w, conv_w, conv_b, A_log, D, dt_bias, gamma, out_proj_w)

    def _L0_ffn_ref(x, w_qr, w_kvr, w_q, w_kv, w_out, null_kv, null_token):
        import jax, jax.numpy as jnp
        import numpy as np
        NQ, NK, H, DH = (512, 256, 8, 64)
        b, n, d = x.shape
        g = w_qr.shape[0]
        bidx = jnp.arange(b)[:, None, None]
        q_logits = jnp.einsum('bnd,gd->bgn', x, w_qr)
        q_top, q_idx = jax.lax.top_k(q_logits, NQ)
        q_scores = jax.nn.sigmoid(q_top)[..., None]
        queries = x[bidx, q_idx]
        kv_logits = jnp.einsum('bnd,gd->bgn', x, w_kvr)
        kv_top, kv_idx = jax.lax.top_k(kv_logits, NK)
        kv_scores = jax.nn.sigmoid(kv_top)[:, :, None, :, None]
        key_values = x[bidx, kv_idx]
        q = jnp.einsum('bgnd,ged->bgne', queries, w_q)
        kv = jnp.einsum('bgnd,ged->bgne', key_values, w_kv)
        k, v = jnp.split(kv, 2, axis=-1)
        heads = lambda t: t.reshape(b, g, -1, H, DH).transpose(0, 1, 3, 2, 4)
        q, k, v = (heads(q), heads(k), heads(v))
        v = v * kv_scores
        nk = jnp.broadcast_to(null_kv[0][None], (b, g, H, 1, DH))
        nv = jnp.broadcast_to(null_kv[1][None], (b, g, H, 1, DH))
        k = jnp.concatenate([nk, k], axis=-2)
        v = jnp.concatenate([nv, v], axis=-2)
        attn = jax.nn.softmax(jnp.einsum('bghid,bghjd->bghij', q, k) * DH ** (-0.5), axis=-1)
        o = jnp.einsum('bghij,bghjd->bghid', attn, v)
        o = o.transpose(0, 1, 3, 2, 4).reshape(b, g, NQ, H * DH)
        o = jnp.einsum('bgne,gde->bgnd', o, w_out)
        o = o * q_scores
        flat_idx = q_idx.reshape(b, g * NQ)
        flat_o = o.reshape(b, g * NQ, d)
        b2 = jnp.arange(b)[:, None]
        summed = jnp.zeros_like(x).at[b2, flat_idx].add(flat_o)
        counts = jnp.zeros((b, n), x.dtype).at[b2, flat_idx].add(1.0)[..., None]
        meaned = summed / jnp.clip(counts, 1e-05)
        return jnp.where(counts > 0, meaned, null_token)
    x = L0_attn_x
    xn = _layernorm(x, axis=-1)
    x = x + _L0_attn_ref(xn, L0_attn_ln_w, L0_attn_ln_b, L0_attn_in_proj_w, L0_attn_conv_w, L0_attn_conv_b, L0_attn_A_log, L0_attn_D, L0_attn_dt_bias, L0_attn_gamma, L0_attn_out_proj_w) + _L0_ffn_ref(xn, L0_ffn_w_qr, L0_ffn_w_kvr, L0_ffn_w_q, L0_ffn_w_kv, L0_ffn_w_out, L0_ffn_null_kv, L0_ffn_null_token)
    return x

_drawn_inputs = setup_inputs


def setup_inputs(seed=0):
    import zlib

    import numpy as np

    out = dict(_drawn_inputs(seed))
    spreads = {'L0_attn_ln_w': (1.0, 0.2),
     'L0_attn_ln_b': (0.0, 0.1),
     'L0_attn_conv_b': (0.0, 0.1),
     'L0_attn_D': (1.0, 0.2),
     'L0_attn_gamma': (1.0, 0.2)}
    factors = {'L0_attn_A_log': 8.0,
     'L0_attn_dt_bias': 8.0,
     'L0_ffn_w_kvr': 2.949,
     'L0_ffn_w_q': 3.408,
     'L0_ffn_null_kv': 8.0}
    for name, (base, spread) in spreads.items():
        noise = np.random.default_rng([zlib.crc32(name.encode()), seed]).standard_normal(out[name].shape)
        drawn = base * np.exp(spread * noise) if base else spread * noise
        out[name] = jnp.asarray(drawn.astype(out[name].dtype))
    for name, factor in factors.items():
        out[name] = (out[name] * factor).astype(out[name].dtype)
    return out
```

```python
from contextlib import ExitStack

import concourse.bass as bass
from concourse import mybir
from concourse.alu_op_type import AluOpType as ALU

ACT = mybir.ActivationFunctionType
AX = mybir.AxisListType
F32 = mybir.dt.float32
F16 = mybir.dt.float16
I32 = mybir.dt.int32

P = 128
NB, L, D = 8, 1024, 512
T = NB * L
KD = D // P
DI, NS, NH, HD = 1024, 128, 16, 64
CH = DI + 2 * NS
NCT = CH // P
KI = DI // P
TAPS = 4
BLK = 512
CK = BLK // P
NBLK = T // BLK
WC = DI + CH
G, NQ, NK, H, DH = 4, 512, 256, 8, 64
QT, KT = NQ // P, NK // P
NR = NB * 2 * G
NT = T // P
TPS = L // P
ROW = D + 2 * G
EPS = 1e-5
WS = 64.0
MS = 16.0
NULLROW = G * NQ

C_ID, C_U, C_J, C_K, C_BASE, C_BATCH = 0, P, 2 * P, 2 * P + QT, 2 * P + QT + 1, 2 * P + QT + 2
C_N = C_BATCH + NB


class Engine:

    def __init__(self, eng, sem):
        self.eng, self.sem, self.n, self.seen = eng, sem, 0, {}

    def after(self, *marks):
        for m in marks:
            if m is None:
                continue
            if type(m) is list:
                self.after(*m)
                continue
            name, sem, value = m
            if self.seen.get(name, 0) < value:
                self.eng.wait_ge(sem, value)
                self.seen[name] = value

    def done(self, ins):
        self.n += 1
        ins.then_inc(self.sem, 1)
        return (id(self), self.sem, self.n)


class Slot:

    def __init__(self, t, sem=None):
        self.t, self.free, self.sem, self.n = t, [], sem, 0

    def landed(self, dma):
        self.n += 16
        dma.then_inc(self.sem, 16)
        return (id(self), self.sem, self.n)


def weave(*gens):
    live = [[g, n, 0] for g, n in gens]
    while live:
        live.sort(key=lambda e: e[2] / e[1])
        e = live[0]
        try:
            next(e[0])
            e[2] += 1
        except StopIteration:
            live.remove(e)


def program(nc, x, w_in, ln_w, ln_b, conv_w, conv_b, a_log, d_skip, dt_bias, gamma, w_out,
            w_route, wq, wkv, wo, null_k, null_v, null_tok, consts, out):
    ctx = ExitStack()
    with ctx:
        def sem(name):
            return ctx.enter_context(nc.semaphore(name))

        PE = Engine(nc.tensor, sem("pe_done"))
        V = Engine(nc.vector, sem("dve_done"))
        A = Engine(nc.scalar, sem("act_done"))
        Q = Engine(nc.gpsimd, sem("pool_done"))
        SP = Engine(nc.sync, sem("sp_done"))
        pe, ve, ac, po, sp = nc.tensor, nc.vector, nc.scalar, nc.gpsimd, nc.sync

        def scratch(name, shape, dt):
            return nc.dram_tensor(name, shape, dt, kind="Internal").ap()

        rows_d = scratch("rows", (T, ROW), F32)
        skip_d = scratch("skip", (T, D), F32)
        acc_d = scratch("acc", (T, D), F32)
        cum_d = scratch("cum", (NBLK, NH, BLK), F32)
        rank_d = scratch("rank", (NR, L), F16)
        res_d = [scratch(f"results{b}", (NULLROW + P, D), F32) for b in range(NB)]

        singles = [Slot(ctx.enter_context(nc.psum_tensor(f"bank{i}", [P, 512], F32))) for i in range(2)]
        pairs = [Slot(ctx.enter_context(nc.psum_tensor(f"pair{i}", [P, 1024], F32))) for i in range(3)]
        turn = {"single": 0, "pair": 0}

        def bank(kind):
            ring = singles if kind == "single" else pairs
            s = ring[turn[kind] % len(ring)]
            turn[kind] += 1
            PE.after(s.free)
            s.free = []
            return s

        def sb(stack, name, shape, dt):
            return stack.enter_context(nc.sbuf_tensor(name, shape, dt))

        cst = sb(ctx, "cst", [P, C_N], F32)
        id16 = sb(ctx, "id16", [P, P], F16)
        neghalf = sb(ctx, "neghalf", [P, CK], F32)
        logit = sb(ctx, "logit", [P, TPS, NB, 2 * G], F32)
        load_const, load_small, load_wout, load_null = (Slot(None, sem(f"s_load{i}")) for i in range(4))
        id32 = cst[:, C_ID:C_ID + P]
        upper = cst[:, C_U:C_U + P]

        c1 = load_const.landed(sp.dma_start(cst[:], consts))
        A.after(c1)
        m_id16 = A.done(ac.copy(id16[:], id32))
        m_half = V.done(ve.memset(neghalf[:], -0.5))
        V.after(c1)
        PE.after(c1, m_id16)
        Q.after(c1, m_half)

        mam = ExitStack()
        with mam:
            whi = sb(mam, "whi", [P, KD, WC], F16)
            wlo = sb(mam, "wlo", [P, KD, WC], F16)
            shi = sb(mam, "shi", [P, KD, 2 * G + NH], F16)
            slo = sb(mam, "slo", [P, KD, 2 * G + NH], F16)
            ohi = sb(mam, "ohi", [P, KI, D], F16)
            olo = sb(mam, "olo", [P, KI, D], F16)
            z_bias = sb(mam, "z_bias", [P, DI], F32)
            dt_b = sb(mam, "dt_b", [P, NH], F32)
            a_neg = sb(mam, "a_neg", [P, NH], F32)
            d_bc = sb(mam, "d_bc", [P, NH], F32)
            raw_bias = sb(mam, "raw_bias", [P, NCT], F32)
            taps = sb(mam, "taps", [P, NCT, TAPS], F32)
            conv_bias = sb(mam, "conv_bias", [P, NCT], F32)

            prep = ExitStack()
            with prep:
                lw = sb(prep, "lw", [P, KD], F32)
                lb = sb(prep, "lb", [P, KD], F32)
                gm = sb(prep, "gm", [P, KI], F32)
                lb_bc = sb(prep, "lb_bc", [P, KD, P], F32)
                bias_bc = sb(prep, "bias_bc", [P, WC + NH], F32)
                al = sb(prep, "al", [P, NH], F32)
                route = sb(prep, "route", [P, KD, 2 * G], F32)
                wout_f = sb(prep, "wout_f", [P, KI, D], F32)
                NC5 = 5
                CW = (WC + NH) // NC5
                stage = [Slot(sb(prep, f"stage{i}", [P, KD, CW], F32), sem(f"s_stage{i}")) for i in range(2)]
                lw64 = sb(prep, "lw64", [P, KD], F32)
                gm64 = sb(prep, "gm64", [P, KI], F32)
                for dst, src in ((lw[:], ln_w.rearrange("(k p) -> p k", p=P)),
                                 (lb[:], ln_b.rearrange("(k p) -> p k", p=P)),
                                 (gm[:], gamma.rearrange("(k p) -> p k", p=P)),
                                 (al[:], a_log.partition_broadcast(P)),
                                 (d_bc[:], d_skip.partition_broadcast(P)),
                                 (dt_b[:], dt_bias.partition_broadcast(P)),
                                 (taps[:], conv_w.rearrange("(c p) t -> p c t", p=P)),
                                 (conv_bias[:], conv_b.rearrange("(c p) -> p c", p=P)),
                                 (route[:], w_route.rearrange("(k p) r -> p k r", p=P))):
                    small = load_small.landed(sp.dma_start(dst, src, allow_slow_non_contiguous=True))
                m_wof = load_wout.landed(sp.dma_start(wout_f[:], w_out.rearrange("(k p) n -> p k n", p=P)))
                V.after(small, m_wof)
                A.after(small, m_wof)
                m = A.done(ac.activation(a_neg[:], al[:], ACT.Exp))
                V.after(m)
                V.done(ve.tensor_scalar(a_neg[:], a_neg[:], -1.0, None, ALU.mult))
                V.done(ve.tensor_scalar(taps[:], taps[:], 0.5, None, ALU.mult))
                V.done(ve.tensor_scalar(conv_bias[:], conv_bias[:], 0.5, None, ALU.mult))
                V.done(ve.tensor_scalar(lw64[:], lw[:], WS, None, ALU.mult))
                m = V.done(ve.tensor_scalar(gm64[:], gm[:], WS, None, ALU.mult))
                m_lb = V.done(ve.tensor_copy(lb_bc[:], lb[:].unsqueeze(2).to_broadcast([P, KD, P])))
                A.after(m)
                V.after(m_lb)
                m = A.done(ac.mul(shi[:, :, 0:2 * G], route[:], WS))
                V.after(m)
                V.done(ve.scalar_tensor_tensor(slo[:, :, 0:2 * G], route[:], WS, shi[:, :, 0:2 * G],
                                               ALU.mult, ALU.subtract))
                for k in range(KI):
                    m = A.done(ac.activation(ohi[:, k, :], wout_f[:, k, :], ACT.Copy, scale=gm64[:, k:k + 1]))
                    V.after(m)
                    V.done(ve.scalar_tensor_tensor(olo[:, k, :], wout_f[:, k, :], gm64[:, k:k + 1],
                                                   ohi[:, k, :], ALU.mult, ALU.subtract))
                PE.after(m_lb)
                wr = w_in.rearrange("(k p) n -> p k n", p=P)
                for n in range(NC5):
                    s = stage[n % 2]
                    SP.after(s.free)
                    got = s.landed(sp.dma_start(s.t[:], wr[:, :, n * CW:(n + 1) * CW]))
                    A.after(got)
                    V.after(got)
                    PE.after(got)
                    bk = bank("single")
                    for k in range(KD):
                        ins = pe.matmul(bk.t[:, 0:CW], lb_bc[:, k, :], s.t[:, k, :], start=k == 0, stop=k == KD - 1)
                    m_pe = PE.done(ins)
                    A.after(m_pe)
                    m_b = A.done(ac.copy(bias_bc[:, n * CW:(n + 1) * CW], bk.t[:, 0:CW]))
                    bk.free = [m_b]
                    last = n == NC5 - 1
                    for k in range(KD):
                        w = min(CW, WC - n * CW)
                        m = A.done(ac.activation(whi[:, k, n * CW:n * CW + w], s.t[:, k, 0:w], ACT.Copy,
                                                 scale=lw64[:, k:k + 1]))
                        if last:
                            m = A.done(ac.activation(shi[:, k, 2 * G:], s.t[:, k, w:CW], ACT.Copy,
                                                     scale=lw64[:, k:k + 1]))
                        V.after(m)
                        m_v = V.done(ve.scalar_tensor_tensor(wlo[:, k, n * CW:n * CW + w], s.t[:, k, 0:w],
                                                             lw64[:, k:k + 1], whi[:, k, n * CW:n * CW + w],
                                                             ALU.mult, ALU.subtract))
                        if last:
                            m_v = V.done(ve.scalar_tensor_tensor(slo[:, k, 2 * G:], s.t[:, k, w:CW],
                                                                 lw64[:, k:k + 1], shi[:, k, 2 * G:],
                                                                 ALU.mult, ALU.subtract))
                    s.free = [m_pe, m_v]
                V.after(m_b)
                V.done(ve.tensor_copy(z_bias[:], bias_bc[:, 0:DI]))
                V.done(ve.tensor_tensor(dt_b[:], dt_b[:], bias_bc[:, WC:], ALU.add))
                PE.after(m_b)
                for c in range(NCT):
                    bk = bank("single")
                    m = PE.done(pe.transpose(bk.t[:, 0:P], bias_bc[:, DI + c * P:DI + (c + 1) * P], id32))
                    V.after(m)
                    m_v = V.done(ve.tensor_copy(raw_bias[:, c:c + 1], bk.t[:, 0:1]))
                    bk.free = [m_v]
                w_ready = [m_v, m]

            for e in (PE, V, A, Q, SP):
                e.after(w_ready)

            s_x = [sem(f"s_x{i}") for i in range(1)]
            xin = [Slot(sb(mam, "xin", [P, CK, D], F32), s_x[0])]
            xn = [Slot(sb(mam, f"xn{i}", [P, D], F32)) for i in range(1)]
            rowt = Slot(sb(mam, "rowt", [P, CK, ROW], F32), sem("s_row"))
            row16 = rowt.t[:].bitcast(F16)
            xh = [Slot(sb(mam, f"xh{i}", [P, 2, D], F16)) for i in range(1)]
            xhT = [Slot(sb(mam, f"xhT{i}", [P, 2, KD, BLK], F16)) for i in range(2)]
            s_skip = sem("s_skip")
            stats = sb(mam, "stats", [P, CK, 6], F32)
            mv = sb(mam, "mv", [P, CK, 2], F32)
            nrm = sb(mam, "nrm", [P, 6, CK], F32)
            dts = sb(mam, "dts", [P, 5, CK * NH], F32)
            dt_t = [Slot(sb(mam, f"dt{i}", [P, CK, NH], F32)) for i in range(2)]
            cum_t = [Slot(sb(mam, f"cum{i}", [P, CK, NH], F32)) for i in range(2)]
            ecum = [Slot(sb(mam, f"ecum{i}", [P, CK, NH], F32)) for i in range(2)]
            cumT = Slot(sb(mam, "cumT", [NH, BLK], F32), sem("s_cumT"))
            raw = [Slot(sb(mam, f"raw{i}", [P, BLK + TAPS - 1], F32)) for i in range(2)]
            halo = sb(mam, "halo", [P, NCT, TAPS - 1], F32)
            cv = [Slot(sb(mam, f"cv{i}", [P, BLK], F32)) for i in range(2)]
            xsT = [Slot(sb(mam, f"xsT{i}", [P, NCT, BLK], F32)) for i in range(2)]

            bc = Slot(sb(mam, "bc", [P, NH, P], F32), sem("s_bc"))
            de = Slot(sb(mam, "de", [P, NH, P], F32))
            skipb = [Slot(sb(mam, f"skipb{i}", [P, D], F32), sem(f"s_skipb{i}")) for i in range(2)]
            s_acc = [sem(f"s_acc{i}") for i in range(2)]
            accw = [Slot(None, s) for s in s_acc]
            xdt = Slot(sb(mam, "xdt", [P, NH, HD], F32))
            dxs = Slot(sb(mam, "dxs", [P, NH, HD], F32))
            xw = Slot(sb(mam, "xw", [P, NH, HD], F32))
            state = [Slot(sb(mam, f"state{i}", [P, NH, HD], F32)) for i in range(2)]
            btok = Slot(sb(mam, "btok", [P, P], F32))
            gmask = Slot(sb(mam, "gmask", [P, P], F32))
            decs = Slot(sb(mam, "decs", [P, 3, NH], F32))
            zs = Slot(sb(mam, "zs", [P, DI], F32))
            yb = Slot(sb(mam, "yb", [P, NH, HD], F32))
            yn = sb(mam, "yn", [P, 3], F32)
            yhl = Slot(sb(mam, "yhl", [P, 2, DI], F16))
            yT = Slot(sb(mam, "yT", [P, 2 * KI, P], F16))
            skip_w = Slot(None, s_skip)
            skip_marks = {}
            cum_marks = {}
            row_marks = []
            front_out = {}
            acc_marks = []

            def front(i):
                b, half = divmod(i, L // BLK)
                u = i % 2
                xi = xin[0]
                SP.after(xi.free)
                got = xi.landed(sp.dma_start(xi.t[:], x[i * BLK:(i + 1) * BLK, :].rearrange("(c p) d -> p c d", p=P)))
                V.after(got)
                for c in range(CK):
                    m = V.done(ve.bn_stats(stats[:, c, :], xi.t[:, c, :]))
                    V.after(m)
                    m = V.done(ve.bn_aggr(mv[:, c, :], stats[:, c, :]))
                V.after(m)
                var, mean = mv[:, :, 1], mv[:, :, 0]
                r1, r2, q2, t0, v2 = (nrm[:, j, :] for j in range(5))
                m = V.done(ve.tensor_scalar(t0, var, EPS, None, ALU.add))
                Q.after(m)
                m = Q.done(po.tensor_tensor(r1, t0, neghalf[:], ALU.pow))
                V.after(m)
                m = V.done(ve.tensor_tensor(v2, var, r1, ALU.mult))
                V.after(m)
                m = V.done(ve.tensor_tensor(v2, v2, r1, ALU.mult))
                V.after(m)
                m = V.done(ve.tensor_scalar(v2, v2, EPS, None, ALU.add))
                Q.after(m)
                m = Q.done(po.tensor_tensor(r2, v2, neghalf[:], ALU.pow))
                V.after(m)
                m_q2 = V.done(ve.tensor_tensor(q2, v2, r2, ALU.mult))
                A.after(m_q2)
                xt = xhT[u]
                yield
                for c in range(CK):
                    n_, h_ = xn[0], xh[0]
                    V.after(n_.free)
                    m_xn = V.done(ve.tensor_scalar(n_.t[:], xi.t[:, c, :], mean[:, c:c + 1], r1[:, c:c + 1],
                                                   ALU.subtract, ALU.mult))
                    A.after(m_xn, rowt.free if c == 0 else None, h_.free)
                    hi, lo = row16[:, c, 0:D], row16[:, c, D:2 * D]
                    m_hi = A.done(ac.copy(hi, n_.t[:]))
                    m_xh = A.done(ac.activation(h_.t[:, 0, :], n_.t[:], ACT.Copy, scale=r2[:, c:c + 1]))
                    Q.after(m_hi)
                    m_lo = Q.done(po.tensor_tensor(lo, n_.t[:], hi, ALU.subtract))
                    m_sk = Q.done(po.tensor_tensor(xi.t[:, c, :], xi.t[:, c, :], n_.t[:], ALU.add))
                    V.after(m_xh)
                    m_xl = V.done(ve.scalar_tensor_tensor(h_.t[:, 1, :], n_.t[:], r2[:, c:c + 1], h_.t[:, 0, :],
                                                          ALU.mult, ALU.subtract))
                    n_.free = [m_xh, m_xl, m_sk]
                    PE.after(m_xl)
                    bk = bank("single")
                    b16 = bk.t[:].bitcast(F16)
                    for j in range(2 * KD):
                        ins = pe.transpose(b16[:, j * P:(j + 1) * P], h_.t[:, j // KD, (j % KD) * P:(j % KD + 1) * P], id16[:])
                    m_t = PE.done(ins)
                    h_.free = [m_t]
                    A.after(m_t, xt.free if c == 0 else None)
                    m_e = A.done(ac.copy(xt.t[:].bitcast(F32)[:, :, :, c * P // 2:(c + 1) * P // 2].rearrange("p h k t -> p (h k) t"),
                                         bk.t[:].rearrange("p (j t) -> p j t", j=2 * KD)))
                    bk.free = [m_e]
                    yield
                m_xhT = m_e
                SP.after(m_sk)
                skip_marks[i] = skip_w.landed(sp.dma_start(
                    skip_d[i * BLK:(i + 1) * BLK, :].rearrange("(c p) d -> p c d", p=P), xi.t[:]))
                xi.free = [skip_marks[i]]
                PE.after(m_xhT)
                bk = bank("single")
                NW = 2 * G + NH
                for c in range(CK):
                    cs = slice(c * P, (c + 1) * P)
                    n = 0
                    for k in range(KD):
                        for ha, w in ((0, shi), (0, slo), (1, shi)):
                            ins = pe.matmul(bk.t[:, c * NW:(c + 1) * NW], xt.t[:, ha, k, cs], w[:, k, :],
                                            start=n == 0, stop=n == 3 * KD - 1)
                            n += 1
                m = PE.done(ins)
                V.after(m)
                sm = bk.t[:, 0:CK * NW].rearrange("p (c n) -> p c n", c=CK)
                for c in range(CK):
                    m_lg = V.done(ve.tensor_scalar(logit[:, half * CK + c, b, :], sm[:, c, 0:2 * G], q2[:, c:c + 1],
                                                   1.0 / WS, ALU.mult, ALU.mult))
                xr, ex, sq, s2, pl = (dts[:, j, :].rearrange("p (c h) -> p c h", c=CK) for j in range(5))
                m = V.done(ve.scalar_tensor_tensor(xr, sm[:, :, 2 * G:], 1.0 / WS,
                                                   dt_b[:].unsqueeze(1).to_broadcast([P, CK, NH]), ALU.mult, ALU.add))
                bk.free = [m_lg, m]
                V.after(m)
                A.after(m_lg)
                sc = rowt.t[:, :, D:ROW]
                m_s = A.done(ac.activation(sc, logit[:, half * CK:(half + 1) * CK, b, :], ACT.Tanh, scale=0.5))
                V.after(m_s)
                m_s = V.done(ve.tensor_scalar(sc, sc, 0.5, 0.5, ALU.mult, ALU.add))
                SP.after(m_s, m_lo)
                m_row = rowt.landed(sp.dma_start(rows_d[i * BLK:(i + 1) * BLK, :].rearrange("(c p) d -> p c d", p=P), rowt.t[:]))
                rowt.free = [m_row]
                row_marks.append(m_row)
                m = V.done(ve.scalar_tensor_tensor(ex, xr, -1.0, xr, ALU.mult, ALU.max))
                A.after(m)
                m = A.done(ac.activation(ex, ex, ACT.Exp, scale=-1.0))
                V.after(m)
                m = V.done(ve.tensor_scalar(sq, ex, 2.0, None, ALU.add))
                V.after(m)
                m = V.done(ve.reciprocal(sq, sq))
                V.after(m)
                m = V.done(ve.tensor_tensor(sq, sq, ex, ALU.mult))
                V.after(m)
                m = V.done(ve.tensor_tensor(s2, sq, sq, ALU.mult))
                V.after(m)
                m = V.done(ve.tensor_scalar(pl, s2, 2.0 / 17, None, ALU.mult))
                for j in range(15, 1, -2):
                    V.after(m)
                    m = V.done(ve.scalar_tensor_tensor(pl, pl, 2.0 / j, s2, ALU.add, ALU.mult))
                V.after(m)
                m = V.done(ve.scalar_tensor_tensor(pl, pl, 2.0, sq, ALU.add, ALU.mult))
                V.after(m, dt_t[u].free)
                dt = dt_t[u].t
                m_dt = V.done(ve.scalar_tensor_tensor(dt[:], xr, 0.0, pl, ALU.max, ALU.add))
                V.after(m_dt)
                m = V.done(ve.tensor_tensor(xr, dt[:], a_neg[:].unsqueeze(1).to_broadcast([P, CK, NH]), ALU.mult))
                PE.after(m)
                bk = bank("single")
                for c in range(CK):
                    ins = pe.matmul(bk.t[:, c * NH:(c + 1) * NH], upper, xr[:, c, :], start=True, stop=True)
                m = PE.done(ins)
                V.after(m, cum_t[u].free)
                A.after(m, ecum[u].free)
                m_cum = V.done(ve.tensor_copy(cum_t[u].t[:], bk.t[:, 0:CK * NH].rearrange("p (c h) -> p c h", c=CK)))
                A.after(m_cum)
                m_ec = A.done(ac.activation(ecum[u].t[:], cum_t[u].t[:], ACT.Exp))
                bk.free = [m_cum]
                bk = bank("single")
                for c in range(CK):
                    ins = pe.matmul(bk.t[0:NH, c * P:(c + 1) * P], xr[:, c, :], upper, start=True, stop=True)
                m = PE.done(ins)
                A.after(m, cumT.free)
                m = A.done(ac.copy(cumT.t[:], bk.t[0:NH, :]))
                bk.free = [m]
                SP.after(m)
                cum_marks[i] = cumT.landed(sp.dma_start(cum_d[i], cumT.t[:]))
                cumT.free = [cum_marks[i]]
                if half == 0:
                    m_halo = V.done(ve.memset(halo[:], 0.0))
                    V.after(m_halo)
                yield
                xs = xsT[u]
                for pr in range(NCT // 2):
                    bk = bank("pair")
                    for j in range(2):
                        ct = 2 * pr + j
                        n = 0
                        for k in range(KD):
                            ws = slice(DI + ct * P, DI + (ct + 1) * P)
                            for ha, w in ((0, whi), (1, whi), (0, wlo)):
                                ins = pe.matmul(bk.t[:, j * BLK:(j + 1) * BLK], w[:, k, ws], xt.t[:, ha, k, :],
                                                start=n == 0, stop=n == 3 * KD - 1)
                                n += 1
                        m_mm = PE.done(ins)
                        r_, c_ = raw[j], cv[j]
                        A.after(m_mm, r_.free)
                        m_r = A.done(ac.activation(r_.t[:, TAPS - 1:], bk.t[:, j * BLK:(j + 1) * BLK], ACT.Identity,
                                                   bias=raw_bias[:, ct:ct + 1], scale=1.0 / WS))
                        V.after(r_.free)
                        m = V.done(ve.tensor_copy(r_.t[:, 0:TAPS - 1], halo[:, ct, :]))
                        V.after(m, m_r)
                        m_h = V.done(ve.tensor_copy(halo[:, ct, :], r_.t[:, BLK:]))
                        V.after(c_.free)
                        m = V.done(ve.tensor_scalar(c_.t[:], r_.t[:, 0:BLK], taps[:, ct, 0:1], conv_bias[:, ct:ct + 1],
                                                    ALU.mult, ALU.add))
                        for t in range(1, TAPS):
                            V.after(m, m_h)
                            m = V.done(ve.scalar_tensor_tensor(c_.t[:], r_.t[:, t:t + BLK], taps[:, ct, t:t + 1], c_.t[:],
                                                               ALU.mult, ALU.add))
                        r_.free = [m]
                        A.after(m)
                        th = bk.t[:, j * BLK:(j + 1) * BLK]
                        m_th = A.done(ac.activation(th, c_.t[:], ACT.Tanh))
                        V.after(m_th, xs.free if ct == 0 else None)
                        m_xs = V.done(ve.scalar_tensor_tensor(xs.t[:, ct, :], th, 1.0, c_.t[:], ALU.add, ALU.mult))
                        c_.free = [m_xs]
                    bk.free = [m_xs]
                    yield
                xt.free = [m_mm]
                front_out[i] = (m_xs, m_dt, m_cum, m_ec)

            def back(i):
                b, half = divmod(i, L // BLK)
                u = i % 2
                m_xs, m_dt, m_cum, m_ec = front_out[i]
                xs, xt = xsT[u], xhT[u]
                dt, cum, ec = dt_t[u].t, cum_t[u].t, ecum[u].t
                for c in range(CK):
                    ch = i * CK + c
                    cs = slice(c * P, (c + 1) * P)
                    old, new = state[ch % 2], state[(ch + 1) % 2]
                    SP.after(bc.free, cum_marks[i])
                    m_bc = bc.landed(sp.dma_start(bc.t[:], cum_d[i][:, cs].partition_broadcast(P)))
                    sk = skipb[ch % 2]
                    SP.after(sk.free, skip_marks[i])
                    m_sk = sk.landed(sp.dma_start(sk.t[:], skip_d[ch * P:(ch + 1) * P, :]))
                    if half == 0 and c == 0:
                        V.after(old.free)
                        m_old = V.done(ve.memset(old.t[:], 0.0))
                        old.ready = m_old
                    m_old = old.ready
                    PE.after(m_xs)
                    px = bank("pair")
                    for k in range(KI):
                        ins = pe.transpose(px.t[:, k * P:(k + 1) * P], xs.t[:, k, cs], id32)
                    m_px = PE.done(ins)
                    bk = bank("single")
                    pe.transpose(bk.t[:, 0:P], xs.t[:, KI, cs], id32)
                    m_g = PE.done(pe.matmul(bk.t[:, P:2 * P], xs.t[:, KI, cs], xs.t[:, KI + 1, cs], start=True, stop=True))
                    Q.after(m_bc, m_cum, de.free)
                    m = Q.done(po.tensor_tensor(de.t[:], bc.t[:], cum[:, c, :].unsqueeze(2).to_broadcast([P, NH, P]), ALU.subtract))
                    V.after(m_bc, m_cum, decs.free)
                    m_d1 = V.done(ve.tensor_tensor(decs.t[:, 0, :], bc.t[:, :, P - 1], cum[:, c, :], ALU.subtract))
                    A.after(m_d1, m_bc)
                    m_dec = A.done(ac.activation(decs.t[:, 1, :], decs.t[:, 0, :], ACT.Exp))
                    m_cd = A.done(ac.activation(decs.t[:, 2, :], bc.t[:, :, P - 1], ACT.Exp))
                    bc.free = [m, m_d1, m_cd]
                    V.after(m)
                    m = V.done(ve.tensor_scalar(de.t[:], de.t[:], 0.0, None, ALU.min))
                    A.after(m)
                    m_e = A.done(ac.activation(de.t[:], de.t[:], ACT.Exp))
                    V.after(m_px, m_dt, xdt.free)
                    p3 = px.t[:].rearrange("p (h d) -> p h d", h=NH)
                    m_xdt = V.done(ve.tensor_tensor(xdt.t[:], p3, dt[:, c, :].unsqueeze(2).to_broadcast([P, NH, HD]), ALU.mult))
                    V.after(dxs.free)
                    m_dxs = V.done(ve.tensor_tensor(dxs.t[:], p3, d_bc[:].unsqueeze(2).to_broadcast([P, NH, HD]), ALU.mult))
                    px.free = [m_dxs]
                    A.after(m_g, btok.free)
                    m_bt = A.done(ac.copy(btok.t[:], bk.t[:, 0:P]))
                    V.after(m_g, m_bt, gmask.free)
                    m_gm = V.done(ve.tensor_tensor(gmask.t[:], bk.t[:, P:2 * P], upper, ALU.mult))
                    bk.free = [m_gm]
                    Q.after(m_xdt, m_dec, xw.free)
                    m_xw = Q.done(po.tensor_tensor(xw.t[:], xdt.t[:], decs.t[:, 1, :].unsqueeze(2).to_broadcast([P, NH, HD]), ALU.mult))
                    Q.after(m_cd, m_old, new.free)
                    m_sd = Q.done(po.tensor_tensor(new.t[:], old.t[:], decs.t[:, 2, :].unsqueeze(2).to_broadcast([P, NH, HD]), ALU.mult))
                    decs.free = [m_sd]
                    V.after(m_e, m_gm)
                    m_m = V.done(ve.tensor_tensor(de.t[:], de.t[:], gmask.t[:].unsqueeze(1).to_broadcast([P, NH, P]), ALU.mult))
                    gmask.free = [m_m]
                    pz = bank("pair")
                    for j in range(2):
                        n = 0
                        for k in range(KD):
                            for ha, w in ((0, whi), (0, wlo), (1, whi)):
                                ins = pe.matmul(pz.t[:, j * 512:(j + 1) * 512], xt.t[:, ha, k, cs], w[:, k, j * 512:(j + 1) * 512],
                                                start=n == 0, stop=n == 3 * KD - 1)
                                n += 1
                    m_z = PE.done(ins)
                    V.after(m_z, zs.free)
                    m_zs = V.done(ve.scalar_tensor_tensor(zs.t[:], pz.t[:], 1.0 / WS, z_bias[:], ALU.mult, ALU.add))
                    A.after(m_zs)
                    m_zt = A.done(ac.activation(pz.t[:], zs.t[:], ACT.Tanh, scale=0.5))
                    V.after(m_zt)
                    m_sz = V.done(ve.scalar_tensor_tensor(zs.t[:], pz.t[:], 1.0, zs.t[:], ALU.add, ALU.mult))
                    pz.free = [m_sz]
                    yield
                    PE.after(m_old)
                    pi = bank("pair")
                    sf = old.t[:].rearrange("p h d -> p (h d)")
                    for j in range(2):
                        ins = pe.matmul(pi.t[:, j * 512:(j + 1) * 512], xs.t[:, KI + 1, cs], sf[:, j * 512:(j + 1) * 512], start=True, stop=True)
                    m_i = PE.done(ins)
                    V.after(m_i, m_ec, yb.free)
                    m_y = V.done(ve.tensor_tensor(yb.t[:], pi.t[:].rearrange("p (h d) -> p h d", h=NH),
                                                  ec[:, c, :].unsqueeze(2).to_broadcast([P, NH, HD]), ALU.mult))
                    pi.free = [m_y]
                    PE.after(m_bt, m_xw)
                    pn = bank("pair")
                    xf = xw.t[:].rearrange("p h d -> p (h d)")
                    for j in range(2):
                        ins = pe.matmul(pn.t[:, j * 512:(j + 1) * 512], btok.t[:], xf[:, j * 512:(j + 1) * 512], start=True, stop=True)
                    m_n = PE.done(ins)
                    btok.free = [m_n]
                    xw.free = [m_n]
                    V.after(m_n, m_sd)
                    m_new = V.done(ve.tensor_tensor(new.t[:], new.t[:], pn.t[:].rearrange("p (h d) -> p h d", h=NH), ALU.add))
                    pn.free = [m_new]
                    new.ready = m_new
                    old.free = [m_i, m_sd]
                    PE.after(m_m, m_xdt)
                    pw = bank("pair")
                    for h in range(NH):
                        ins = pe.matmul(pw.t[:, h * HD:(h + 1) * HD], de.t[:, h, :], xdt.t[:, h, :], start=True, stop=True)
                    m_w = PE.done(ins)
                    de.free = [m_w]
                    xdt.free = [m_w, m_xw]
                    V.after(m_w, m_y)
                    m_y = V.done(ve.tensor_tensor(yb.t[:], yb.t[:], pw.t[:].rearrange("p (h d) -> p h d", h=NH), ALU.add))
                    pw.free = [m_y]
                    V.after(m_y, m_dxs)
                    m_y = V.done(ve.tensor_tensor(yb.t[:], yb.t[:], dxs.t[:], ALU.add))
                    dxs.free = [m_y]
                    yf = yb.t[:].rearrange("p h d -> p (h d)")
                    V.after(m_y, m_sz)
                    m_y = V.done(ve.scalar_tensor_tensor(yf, yf, 0.5, zs.t[:], ALU.mult, ALU.mult))
                    zs.free = [m_y]
                    yield
                    A.after(m_y, yhl.free)
                    m = A.done(ac.activation(yhl.t[:, 0, :], yf, ACT.Square, accum_out=yn[:, 0:1]))
                    V.after(m)
                    m = V.done(ve.tensor_scalar(yn[:, 1:2], yn[:, 0:1], 1.0 / DI, EPS, ALU.mult, ALU.add))
                    Q.after(m)
                    m_r = Q.done(po.tensor_tensor(yn[:, 2:3], yn[:, 1:2], neghalf[:, 0:1], ALU.pow))
                    A.after(m_r)
                    m_h = A.done(ac.activation(yhl.t[:, 0, :], yf, ACT.Copy, scale=yn[:, 2:3]))
                    V.after(m_h)
                    m_l = V.done(ve.scalar_tensor_tensor(yhl.t[:, 1, :], yf, yn[:, 2:3], yhl.t[:, 0, :], ALU.mult, ALU.subtract))
                    yb.free = [m_h, m_l]
                    yield
                    PE.after(m_l)
                    pt = bank("pair")
                    pt16 = pt.t[:].bitcast(F16)
                    for j in range(2 * KI):
                        ins = pe.transpose(pt16[:, j * P:(j + 1) * P], yhl.t[:, j // KI, (j % KI) * P:(j % KI + 1) * P], id16[:])
                    m_t = PE.done(ins)
                    yhl.free = [m_t]
                    A.after(m_t, yT.free)
                    m_yT = A.done(ac.copy(yT.t[:].bitcast(F32).rearrange("p j t -> p (j t)"), pt.t[:]))
                    pt.free = [m_yT]
                    yield
                    PE.after(m_yT)
                    bk = bank("single")
                    n = 0
                    for k in range(KI):
                        for ha, w in ((0, ohi), (0, olo), (1, ohi)):
                            ins = pe.matmul(bk.t[:], yT.t[:, ha * KI + k, :], w[:, k, :], start=n == 0, stop=n == 3 * KI - 1)
                            n += 1
                    m_o = PE.done(ins)
                    yT.free = [m_o]
                    V.after(m_o, m_sk)
                    m_s = V.done(ve.scalar_tensor_tensor(sk.t[:], bk.t[:], 1.0 / WS, sk.t[:], ALU.mult, ALU.add))
                    bk.free = [m_s]
                    SP.after(m_s)
                    m_a = accw[ch % 2].landed(sp.dma_start(acc_d[ch * P:(ch + 1) * P, :], sk.t[:]))
                    sk.free = [m_a]
                    acc_marks.append(m_a)
                    yield
                xs.free = [m_g, m_i]
                xt.free = [m_z]
                dt_t[u].free = [m_xdt]
                cum_t[u].free = [m_d1, m_e, m_ec]
                ecum[u].free = [m_y]

            for _ in front(0):
                pass
            for i in range(NBLK):
                if i + 1 < NBLK:
                    weave((back(i), 16), (front(i + 1), 10))
                else:
                    for _ in back(i):
                        pass
            mamba_end = [m for m in (acc_marks[-1], acc_marks[-2], row_marks[-1], skip_marks[NBLK - 1])]
            mamba_end += [(id(e), e.sem, e.n) for e in (PE, V, A, Q)]

        for e in (PE, V, A, Q, SP):
            e.after(mamba_end)

        idx_tok = sb(ctx, "idx_tok", [P, TPS, NR], I32)
        cnt = sb(ctx, "cnt", [P, TPS, NB], F32)
        none = sb(ctx, "none", [P, TPS, NB], F32)
        s_rank = Slot(None, sem("s_rank"))
        top = ExitStack()
        with top:
            lg = sb(top, "lg", [NR, L], F32)
            junk = sb(top, "junk", [NR, L], F32)
            gt = sb(top, "gt", [NR, L], F32)
            eq = sb(top, "eq", [NR, L], F32)
            rk = sb(top, "rk", [NR, L], F32)
            zero = sb(top, "zero", [NR, L], F32)
            rk16 = sb(top, "rk16", [NR, L], F16)
            key = sb(top, "key", [NR, 4], I32)
            num = sb(top, "num", [NR, 4], F32)
            selt = sb(top, "selt", [P, TPS, NR], F32)
            PE.after([(id(V), V.sem, V.n)])
            for c in range(TPS):
                bk = bank("single")
                m = PE.done(pe.transpose(bk.t[0:NR, 0:P], logit[:, c, :, :].rearrange("p b j -> p (b j)"), id32))
                V.after(m)
                m = V.done(ve.tensor_copy(lg[:, c * P:(c + 1) * P], bk.t[0:NR, 0:P]))
                bk.free = [m]
            V.done(ve.memset(zero[:], 0.0))
            m = V.done(ve.memset(key[:], 0))
            found, cand, inv, ok = (key[:, j:j + 1] for j in range(4))
            val = num[:, 0:1]
            ks = cst[0:NR, C_K:C_K + 1]
            MIN = -2 ** 31

            def decode(src):
                m = V.done(ve.tensor_scalar(inv, src, 31, -1, ALU.arith_shift_right, ALU.bitwise_xor))
                V.after(m)
                m = V.done(ve.tensor_scalar(inv, inv, MIN, None, ALU.bitwise_or))
                V.after(m)
                m = V.done(ve.tensor_tensor(val.bitcast(I32), inv, src, ALU.bitwise_xor))
                V.after(m)

            for bit in range(31, -1, -1):
                V.after(m)
                m = V.done(ve.tensor_scalar(cand, found, MIN if bit == 31 else 1 << bit, None, ALU.bitwise_or))
                V.after(m)
                decode(cand)
                m = V.done(ve.tensor_scalar(junk[:], lg[:], val, 0.0, ALU.is_ge, ALU.add, accum_out=num[:, 1:2]))
                V.after(m)
                m = V.done(ve.tensor_tensor(ok, num[:, 1:2], ks, ALU.is_ge))
                V.after(m)
                m = V.done(ve.copy_predicated(found, ok, cand))
            V.after(m)
            decode(found)
            m = V.done(ve.tensor_scalar(gt[:], lg[:], val, 0.0, ALU.is_gt, ALU.add, accum_out=num[:, 1:2]))
            m2 = V.done(ve.tensor_scalar(eq[:], lg[:], val, None, ALU.is_equal))
            V.after(m2)
            m = V.done(ve.tensor_tensor(num[:, 2:3], ks, num[:, 1:2], ALU.subtract))
            m = V.done(ve.tensor_tensor_scan(rk[:], eq[:], zero[:], 0.0, ALU.add, ALU.add))
            V.after(m)
            m = V.done(ve.scalar_tensor_tensor(eq[:], rk[:], num[:, 2:3], eq[:], ALU.is_le, ALU.mult))
            V.after(m)
            m = V.done(ve.tensor_tensor(gt[:], gt[:], eq[:], ALU.add))
            V.after(m)
            m = V.done(ve.tensor_tensor_scan(rk[:], gt[:], zero[:], 0.0, ALU.add, ALU.add))
            V.after(m)
            m_rk = V.done(ve.tensor_copy(rk16[:], rk[:]))
            SP.after(m_rk)
            m_rank = s_rank.landed(sp.dma_start(rank_d, rk16[:]))
            m = V.done(ve.scalar_tensor_tensor(eq[:], rk[:], cst[0:NR, C_BASE:C_BASE + 1], gt[:], ALU.add, ALU.mult))
            V.after(m)
            m = V.done(ve.tensor_scalar(eq[:], eq[:], float(NULLROW), None, ALU.add))
            PE.after(m)
            for c in range(TPS):
                bk = bank("single")
                pe.transpose(bk.t[:, 0:NR], eq[:, c * P:(c + 1) * P], cst[0:NR, C_ID:C_ID + NR])
                m = PE.done(pe.transpose(bk.t[:, NR:2 * NR], gt[:, c * P:(c + 1) * P], cst[0:NR, C_ID:C_ID + NR]))
                V.after(m)
                m_ix = V.done(ve.tensor_copy(idx_tok[:, c, :], bk.t[:, 0:NR]))
                m = V.done(ve.tensor_copy(selt[:, c, :], bk.t[:, NR:2 * NR]))
                bk.free = [m]
            V.after(m)
            m = V.done(ve.tensor_reduce(cnt[:], selt[:].rearrange("p c (b j) -> p c b j", b=NB)[:, :, :, 0:G], AX.X, ALU.add))
            V.after(m)
            m = V.done(ve.tensor_scalar(none[:], cnt[:], 0.0, None, ALU.is_equal))
            m = V.done(ve.tensor_scalar(cnt[:], cnt[:], EPS, None, ALU.max))
            V.after(m)
            m_cnt = V.done(ve.reciprocal(cnt[:], cnt[:]))
            top_end = [m_cnt, m_rank]
        for e in (PE, V, A, Q, SP):
            e.after(top_end)

        NW = 4 * D
        wts = [[Slot(sb(ctx, f"w{h}{i}", [P, KD, NW], F16)) for h in ("hi", "lo")] for i in range(2)]
        SC = 256
        wst = [Slot(sb(ctx, f"wst{i}", [P, KD, SC], F32), sem(f"s_wst{i}")) for i in range(2)]
        rbc = [Slot(sb(ctx, f"rbc{i}", [P, L], F16), sem(f"s_rbc{i}")) for i in range(2)]
        rjunk = sb(ctx, "rjunk", [P, L], F16)
        slot_f = sb(ctx, "slot_f", [P, QT + KT], F32)
        slot_i = [Slot(sb(ctx, f"slot_i{i}", [P, QT + KT], I32)) for i in range(2)]
        gat = [Slot(sb(ctx, f"gat{i}", [P, ROW], F32), sem(f"s_gat{i}")) for i in range(QT + KT)]
        qscore = [Slot(sb(ctx, f"qscore{i}", [P, QT], F32)) for i in range(2)]
        xq = Slot(sb(ctx, "xq", [P, 2 * KD, NQ], F16))
        xk = Slot(sb(ctx, "xk", [P, 2 * KD, NK], F16))
        qa = [Slot(sb(ctx, f"qa{i}", [P, H, NQ], F16)) for i in range(2)]
        qb = [Slot(sb(ctx, f"qb{i}", [P, H, NQ], F16)) for i in range(1)]
        KW = NK + 2
        ka = [Slot(sb(ctx, f"ka{i}", [P, H, KW], F16)) for i in range(2)]
        kb = [Slot(sb(ctx, f"kb{i}", [P, H, NK], F16)) for i in range(2)]
        vhi = [Slot(sb(ctx, f"vhi{i}", [P, KT, H, DH + 1], F16)) for i in range(2)]
        vlo = [Slot(sb(ctx, f"vlo{i}", [P, KT, H, DH], F16)) for i in range(2)]
        nkf = [Slot(sb(ctx, f"nkf{i}", [DH, H], F32), sem(f"s_nkf{i}")) for i in range(2)]
        nkl = [Slot(sb(ctx, f"nkl{i}", [DH, 2, H], F16)) for i in range(2)]
        nvf = [Slot(sb(ctx, f"nvf{i}", [H, DH + 1], F32), sem(f"s_nvf{i}")) for i in range(2)]
        nvd = sb(ctx, "nvd", [H, H, DH + 1], F32)
        nvb = [Slot(sb(ctx, f"nvb{i}", [96, H, DH + 1], F16)) for i in range(2)]
        smx = sb(ctx, "smx", [P, QT, H], F32)
        snl = sb(ctx, "snl", [P, QT, H], F32)
        pnl = sb(ctx, "pnl", [P, QT, H], F32)
        pnm = sb(ctx, "pnm", [P, QT, 104], F16)
        pnT = sb(ctx, "pnT", [96, NQ], F16)
        pf = [Slot(sb(ctx, f"pf{i}", [P, KT, NQ], F32)) for i in range(2)]
        ph = [Slot(sb(ctx, f"ph{i}", [P, 2, KT, NQ], F16)) for i in range(2)]
        rden = sb(ctx, "rden", [P, H, QT], F32)
        on = Slot(sb(ctx, "on", [P, QT, D], F32))
        ohl = Slot(sb(ctx, "ohl", [P, 2, D], F16))
        oT = Slot(sb(ctx, "oT", [P, 2 * KD, P], F16))
        res = [Slot(sb(ctx, f"res{i}", [P, D], F32), sem(f"s_res{i}")) for i in range(2)]
        gres = [Slot(sb(ctx, f"gres{i}", [P, D], F32), sem(f"s_gres{i}")) for i in range(G)]
        accb = Slot(sb(ctx, "accb", [P, D], F32), sem("s_accb"))
        s_out = Slot(None, sem("s_out"))
        SCALE = DH ** -0.5
        null_bc = sb(ctx, "null_bc", [P, D], F32)
        m = load_null.landed(sp.dma_start(null_bc[:], null_tok.partition_broadcast(P)))
        V.after(m)

        m = V.done(ve.memset(pnm[:], 0.0))
        for i in range(2):
            m = V.done(ve.memset(nvb[i].t[:], 0.0))
            m = V.done(ve.memset(vhi[i].t[:], 1.0))
            m = V.done(ve.tensor_scalar(kb[i].t[DH:DH + H, :, :],
                                        cst[0:H, C_ID:C_ID + H].unsqueeze(2).to_broadcast([H, H, NK]), MS, None, ALU.mult))
            m = V.done(ve.memset(nvf[i].t[:], 1.0))
        m_z = V.done(ve.memset(res[0].t[:], 0.0))
        zero_rows = Slot(None, sem("s_zero_rows"))
        SP.after(m_z)
        for b in range(NB):
            m_zero = zero_rows.landed(sp.dma_start(res_d[b][NULLROW:, :], res[0].t[:]))
        res[0].free = [m_zero]
        for e in (PE, V, A, Q):
            e.after(m_z)
        res_marks = [m_zero]

        def split_weights(g):
            wh, wl = wts[g % 2]
            for n in range(NW // SC):
                s = wst[n % 2]
                c0_ = n * SC
                src = (wq[g][:, c0_:c0_ + SC] if c0_ < D else wkv[g][:, c0_ - D:c0_ - D + SC] if c0_ < 3 * D
                       else wo[g][:, c0_ - 3 * D:c0_ - 3 * D + SC])
                SP.after(s.free)
                got = s.landed(sp.dma_start(s.t[:], src.rearrange("(k p) n -> p k n", p=P)))
                cs = slice(n * SC, (n + 1) * SC)
                A.after(got, wh.free if n == 0 else None)
                m = A.done(ac.mul(wh.t[:, :, cs], s.t[:], WS))
                V.after(m, wl.free if n == 0 else None)
                for k in range(KD):
                    m = V.done(ve.scalar_tensor_tensor(wl.t[:, k, cs], s.t[:, k, :], WS, wh.t[:, k, cs], ALU.mult, ALU.subtract))
                s.free = [m]
                yield
            wl.ready = m
            nk, nv, nl, nb = nkf[g % 2], nvf[g % 2], nkl[g % 2], nvb[g % 2]
            SP.after(nk.free, nv.free)
            m_k = nk.landed(sp.dma_start(nk.t[:], null_k[g], allow_slow_non_contiguous=True))
            m_v = nv.landed(sp.dma_start(nv.t[:, 0:DH], null_v[g]))
            V.after(m_k, m_v, nl.free, nb.free)
            m = V.done(ve.tensor_copy(nl.t[:, 0, :], nk.t[:]))
            V.after(m)
            m = V.done(ve.tensor_tensor(nl.t[:, 1, :], nk.t[:], nl.t[:, 0, :], ALU.subtract))
            nk.free = [m]
            m = V.done(ve.tensor_tensor(nvd[:], nv.t[:].unsqueeze(1).to_broadcast([H, H, DH + 1]),
                                        cst[0:H, C_ID:C_ID + H].unsqueeze(2).to_broadcast([H, H, DH + 1]), ALU.mult))
            nv.free = [m]
            V.after(m)
            m = V.done(ve.tensor_copy(nb.t[0:H], nvd[:]))
            V.after(m)
            V.done(ve.tensor_copy(nb.t[32:32 + H], nvd[:]))
            m = V.done(ve.tensor_tensor(nb.t[64:64 + H], nvd[:], nb.t[0:H], ALU.subtract))
            nb.ready = m
            yield

        made = {}

        def prepare(n):
            g, b = divmod(n, NB)
            u = n % 2
            wh, wl = wts[g % 2]
            si = slot_i[u]
            for kind, r, nt, off in (("q", b * 2 * G + g, QT, 0), ("k", b * 2 * G + G + g, KT, QT)):
                s = rbc[0 if kind == "q" else 1]
                SP.after(s.free)
                got = s.landed(sp.dma_start(s.t[:], rank_d[r].partition_broadcast(P)))
                V.after(got)
                for j in range(nt):
                    m = V.done(ve.tensor_scalar(rjunk[:], s.t[:], cst[:, C_J + j:C_J + j + 1], 0.0, ALU.is_le, ALU.add,
                                                accum_out=slot_f[:, off + j:off + j + 1]))
                    V.after(m)
                s.free = [m]
            V.after(si.free)
            m_si = V.done(ve.tensor_scalar(si.t[:], slot_f[:], float(b * L), None, ALU.add))
            got = []
            for j in range(QT + KT):
                t = gat[j]
                Q.after(m_si, t.free)
                got.append(t.landed(po.indirect_dma_start(
                    t.t[:], None, rows_d, bass.IndirectOffsetOnAxis(ap=si.t[:, j:j + 1], axis=0))))
            si.free = got
            yield
            for j in range(QT + KT):
                t = gat[j]
                g16 = t.t[:].bitcast(F16)
                PE.after(got[j])
                bk = bank("single")
                b16 = bk.t[:].bitcast(F16)
                for c in range(2 * KD):
                    ins = pe.transpose(b16[:, c * P:(c + 1) * P], g16[:, c * P:(c + 1) * P], id16[:])
                m_t = PE.done(ins)
                dst, s0 = (xq, j) if j < QT else (xk, j - QT)
                A.after(m_t, dst.free if s0 == 0 else None)
                m_x = A.done(ac.copy(dst.t[:].bitcast(F32)[:, :, s0 * P // 2:(s0 + 1) * P // 2],
                                     bk.t[:].rearrange("p (c t) -> p c t", c=2 * KD)))
                bk.free = [m_x]
                if j < QT:
                    V.after(got[j], qscore[u].free if j == 0 else None)
                    m_qs = V.done(ve.tensor_copy(qscore[u].t[:, j:j + 1], t.t[:, D + g:D + g + 1]))
                    t.free = [m_t, m_qs]
                else:
                    t.free = [m_t]
                if j % 2:
                    yield
            PE.after(m_x, wl.ready)
            qa_, ka_, kb_, vh, vl = qa[u], ka[u], kb[u], vhi[u], vlo[u]
            nl = nkl[g % 2]
            for e in range(KD):
                bk = bank("single")
                n_ = 0
                for k in range(KD):
                    ws = slice(e * P, (e + 1) * P)
                    for w, ha in ((wh, 0), (wh, 1), (wl, 0)):
                        ins = pe.matmul(bk.t[:], w.t[:, k, ws], xq.t[:, ha * KD + k, :], start=n_ == 0, stop=n_ == 3 * KD - 1)
                        n_ += 1
                m = PE.done(ins)
                A.after(m, qa_.free if e == 0 else None)
                for a in range(2):
                    m = A.done(ac.mul(qa_.t[0:DH, 2 * e + a, :], bk.t[a * DH:(a + 1) * DH, :], 1.0 / WS))
                V.after(m)
                for a in range(2):
                    m_q = V.done(ve.scalar_tensor_tensor(qa_.t[DH:P, 2 * e + a, :], bk.t[a * DH:(a + 1) * DH, :], 1.0 / WS,
                                                         qa_.t[0:DH, 2 * e + a, :], ALU.mult, ALU.subtract))
                bk.free = [m_q]
                if e % 2:
                    yield
            xq.free = [m_q]
            for e2 in range(KD // 2):
                bk = bank("single")
                for e in (2 * e2, 2 * e2 + 1):
                    n_ = 0
                    o = bk.t[:, (e % 2) * NK:(e % 2 + 1) * NK]
                    for k in range(KD):
                        ws = slice(D + e * P, D + (e + 1) * P)
                        for w, ha in ((wh, 0), (wh, 1), (wl, 0)):
                            ins = pe.matmul(o, w.t[:, k, ws], xk.t[:, ha * KD + k, :], start=n_ == 0, stop=n_ == 3 * KD - 1)
                            n_ += 1
                m = PE.done(ins)
                A.after(m, ka_.free if e2 == 0 else None)
                srcs = [bk.t[a * DH:(a + 1) * DH, :].rearrange("p (e t) -> p e t", e=2) for a in range(2)]
                heads = [slice(4 * e2 + a, 4 * e2 + a + 3, 2) for a in range(2)]
                for src, hs in zip(srcs, heads):
                    A.done(ac.mul(ka_.t[0:DH, hs, 0:NK], src, 1.0 / WS))
                    m_k2 = A.done(ac.mul(ka_.t[DH:P, hs, 0:NK], src, 1.0 / WS))
                V.after(m_k2, kb_.free if e2 == 0 else None)
                for src, hs in zip(srcs, heads):
                    m_kb = V.done(ve.scalar_tensor_tensor(kb_.t[0:DH, hs, :], src, 1.0 / WS, ka_.t[0:DH, hs, 0:NK],
                                                          ALU.mult, ALU.subtract))
                bk.free = [m_kb, m_k2]
            V.after(ka_.free)
            V.done(ve.tensor_copy(ka_.t[0:DH, :, NK], nl.t[:, 0, :]))
            m_nk = V.done(ve.tensor_copy(ka_.t[DH:P, :, NK], nl.t[:, 0, :]))
            yield
            for j in range(KT):
                bk = bank("single")
                n_ = 0
                for k in range(KD):
                    for ha, w in ((0, wh), (0, wl), (1, wh)):
                        ins = pe.matmul(bk.t[:], xk.t[:, ha * KD + k, j * P:(j + 1) * P], w.t[:, k, 2 * D:3 * D],
                                        start=n_ == 0, stop=n_ == 3 * KD - 1)
                        n_ += 1
                m_mm = PE.done(ins)
                t = gat[QT + j]
                src = bk.t[:].rearrange("p (h d) -> p h d", h=H)
                V.after(m_mm, vh.free if j == 0 else None, vl.free if j == 0 else None)
                vsc = t.t[:, D + G + g:D + G + g + 1]
                m = V.done(ve.tensor_scalar(vh.t[:, j, :, 0:DH], src, vsc, 1.0 / WS, ALU.mult, ALU.mult))
                m_f = V.done(ve.tensor_scalar(bk.t[:], bk.t[:], vsc, 1.0 / WS, ALU.mult, ALU.mult))
                V.after(m_f)
                m_v = V.done(ve.tensor_tensor(vl.t[:, j, :, :], src, vh.t[:, j, :, 0:DH], ALU.subtract))
                bk.free = [m_v]
                t.free = t.free + [m_f]
            xk.free = [m_mm]
            made[n] = (m_q, m_kb, m_k2, m_nk, m_v, m_qs)
            yield

        def attend(n):
            g, b = divmod(n, NB)
            u = n % 2
            wh, wl = wts[g % 2]
            qa_, ka_, kb_, vh, vl = qa[u], ka[u], kb[u], vhi[u], vlo[u]
            nl, nb, qb_ = nkl[g % 2], nvb[g % 2], qb[0]
            PE.after(*made[n])
            for qt in range(QT):
                qs = slice(qt * P, (qt + 1) * P)
                for h2 in range(H // 2):
                    bk = bank("pair")
                    for a in range(2):
                        h = 2 * h2 + a
                        pe.matmul(bk.t[:, a * 512:a * 512 + NK + 1], qa_.t[:, h, qs], ka_.t[:, h, 0:NK + 1], start=True, stop=False,
                                  skip_group_check=True)
                        ins = pe.matmul(bk.t[:, a * 512 + NK:a * 512 + NK + 1], qa_.t[0:DH, h, qs], nl.t[:, 1, h:h + 1],
                                        start=False, stop=True, skip_group_check=True)
                    m = PE.done(ins)
                    sc = bk.t[:].rearrange("p (a t) -> p a t", a=2)
                    V.after(m)
                    m_mx = V.done(ve.tensor_reduce(smx[:, qt, 2 * h2:2 * h2 + 2], sc[:, :, 0:NK + 1], AX.X, ALU.max))
                    m_sn = V.done(ve.tensor_copy(snl[:, qt, 2 * h2:2 * h2 + 2], sc[:, :, NK]))
                    bk.free = [m_sn]
                yield
            V.after(qb_.free, m_sn)
            V.done(ve.tensor_copy(qb_.t[0:DH], qa_.t[0:DH]))
            shift = pnm[:, :, 96:96 + H]
            m = V.done(ve.tensor_scalar(shift, smx[:], -1.0 / MS, None, ALU.mult))
            V.after(m)
            m = V.done(ve.scalar_tensor_tensor(pnl[:], shift, MS, snl[:], ALU.mult, ALU.add))
            A.after(m)
            m = A.done(ac.activation(pnl[:], pnl[:], ACT.Exp, scale=SCALE))
            V.after(m)
            m = V.done(ve.tensor_copy(pnm[:, :, 0:H], pnl[:]))
            V.after(m)
            V.done(ve.tensor_copy(pnm[:, :, 64:64 + H], pnl[:]))
            m = V.done(ve.tensor_tensor(pnm[:, :, 32:32 + H], pnl[:], pnm[:, :, 0:H], ALU.subtract))
            yield
            PE.after(m)
            bk = bank("single")
            b16 = bk.t[:].bitcast(F16)
            for qt in range(QT):
                ins = pe.transpose(b16[0:104, qt * P:(qt + 1) * P], pnm[:, qt, :], id16[:])
            m = PE.done(ins)
            V.after(m)
            m_qb = V.done(ve.tensor_copy(qb_.t[DH:DH + H], b16[96:96 + H, 0:NQ].unsqueeze(1).to_broadcast([H, H, NQ])))
            m_pT = V.done(ve.tensor_copy(pnT[:], b16[0:96, 0:NQ]))
            bk.free = [m_pT]
            yield

            def scores(h):
                PE.after(m_qb)
                bk = bank("pair")
                for j in range(KT):
                    o = bk.t[:, j * NQ:(j + 1) * NQ]
                    pe.matmul(o, ka_.t[:, h, j * P:(j + 1) * P], qa_.t[:, h, :], start=True, stop=False)
                    ins = pe.matmul(o, kb_.t[0:DH + H, h, j * P:(j + 1) * P], qb_.t[0:DH + H, h, :], start=False, stop=True)
                m_s = PE.done(ins)
                f, p_ = pf[h % 2], ph[h % 2]
                A.after(m_s, f.free)
                m = A.done(ac.activation(f.t[:].rearrange("p k q -> p (k q)"), bk.t[:], ACT.Exp, scale=SCALE))
                bk.free = [m]
                A.after(m, p_.free)
                m_h = A.done(ac.copy(p_.t[:, 0], f.t[:]))
                E, e = (Q, po) if h % 2 else (V, ve)
                E.after(m_h)
                m_l = E.done(e.tensor_tensor(p_.t[:, 1], f.t[:], p_.t[:, 0], ALU.subtract))
                f.free = [m_h, m_l]
                return m_s, m_l

            def values(h, m_l):
                p_ = ph[h % 2]
                PE.after(m_l, m_pT, nb.ready)
                bk = bank("single")
                for qt in range(QT):
                    qs = slice(qt * P, (qt + 1) * P)
                    o = bk.t[:, qt * (DH + 1):(qt + 1) * (DH + 1)]
                    pe.matmul(o, pnT[:, qs], nb.t[:, h, :], start=True, stop=False, skip_group_check=True)
                    for j in range(KT):
                        pe.matmul(o, p_.t[:, 0, j, qs], vh.t[:, j, h, :], start=False, stop=False, skip_group_check=True)
                        pe.matmul(o[:, 0:DH], p_.t[:, 0, j, qs], vl.t[:, j, h, :], start=False, stop=False, skip_group_check=True)
                        ins = pe.matmul(o, p_.t[:, 1, j, qs], vh.t[:, j, h, :], start=False, stop=j == KT - 1, skip_group_check=True)
                m = PE.done(ins)
                p_.free = [m]
                o3 = bk.t[:, 0:QT * (DH + 1)].rearrange("p (q d) -> p q d", q=QT)
                V.after(m, on.free if h == 0 else None)
                m1 = V.done(ve.reciprocal(rden[:, h, :], o3[:, :, DH]))
                V.after(m1)
                m1 = V.done(ve.tensor_tensor(rden[:, h, :], rden[:, h, :], qscore[u].t[:], ALU.mult))
                V.after(m1)
                m1 = V.done(ve.tensor_tensor(on.t[:, :, h * DH:(h + 1) * DH], o3[:, :, 0:DH],
                                             rden[:, h, :].unsqueeze(2).to_broadcast([P, QT, DH]), ALU.mult))
                bk.free = [m1]
                return m, m1

            wait = []
            for h in range(H + 1):
                if h < H:
                    wait.append(scores(h))
                if h >= 1:
                    m_pv, m_on = values(h - 1, wait[h - 1][1])
                yield
            m_s = wait[-1][0]
            qa_.free = [m_s]
            qb_.free = [m_s]
            ka_.free = [m_s]
            kb_.free = [m_s]
            vh.free = [m_pv]
            vl.free = [m_pv]
            qscore[u].free = [m_on]
            for qt in range(QT):
                A.after(m_on, ohl.free)
                m = A.done(ac.copy(ohl.t[:, 0, :], on.t[:, qt, :]))
                Q.after(m)
                m = Q.done(po.tensor_tensor(ohl.t[:, 1, :], on.t[:, qt, :], ohl.t[:, 0, :], ALU.subtract))
                PE.after(m)
                bk = bank("single")
                b16 = bk.t[:].bitcast(F16)
                for j in range(2 * KD):
                    ins = pe.transpose(b16[:, j * P:(j + 1) * P], ohl.t[:, j // KD, (j % KD) * P:(j % KD + 1) * P], id16[:])
                m_t = PE.done(ins)
                ohl.free = [m_t]
                if qt == QT - 1:
                    on.free = [m]
                A.after(m_t, oT.free)
                m = A.done(ac.copy(oT.t[:].bitcast(F32).rearrange("p j t -> p (j t)"), bk.t[:]))
                bk.free = [m]
                yield
                PE.after(m)
                bk = bank("single")
                n_ = 0
                for k in range(KD):
                    for ha, w in ((0, wh), (0, wl), (1, wh)):
                        ins = pe.matmul(bk.t[:], oT.t[:, ha * KD + k, :], w.t[:, k, 3 * D:4 * D], start=n_ == 0, stop=n_ == 3 * KD - 1)
                        n_ += 1
                m = PE.done(ins)
                oT.free = [m]
                r_ = res[qt % 2]
                A.after(m, r_.free)
                m1 = A.done(ac.mul(r_.t[:], bk.t[:], 1.0 / WS))
                bk.free = [m1]
                SP.after(m1)
                r0 = g * NQ + qt * P
                m2 = r_.landed(sp.dma_start(res_d[b][r0:r0 + P, :], r_.t[:]))
                r_.free = [m2]
                last[qt % 2] = m2
            if b == NB - 1:
                wh.free = [m]
                wl.free = [m]
                nkl[g % 2].free = [m_pv]
                nvb[g % 2].free = [m_pv]
            yield

        last = [m_zero, m_zero]

        def combine(b):
            done = list(last) + [m_zero]
            for c in range(TPS):
                t = b * TPS + c
                for g in range(G):
                    s = gres[g]
                    Q.after(s.free, done)
                    s.got = s.landed(po.indirect_dma_start(
                        s.t[:], None, res_d[b],
                        bass.IndirectOffsetOnAxis(ap=idx_tok[:, c, b * 2 * G + g:b * 2 * G + g + 1], axis=0)))
                SP.after(accb.free)
                m_a = accb.landed(sp.dma_start(accb.t[:], acc_d[t * P:(t + 1) * P, :]))
                V.after(*[s.got for s in gres], m_a)
                a0, a1, a2, a3 = (s.t[:] for s in gres)
                Q.after(gres[3].got, gres[2].got)
                m_p = Q.done(po.tensor_tensor(a2, a2, a3, ALU.add))
                m = V.done(ve.tensor_tensor(a0, a0, a1, ALU.add))
                V.after(m, m_p)
                m = V.done(ve.tensor_tensor(a0, a0, a2, ALU.add))
                V.after(m)
                m = V.done(ve.scalar_tensor_tensor(accb.t[:], a0, cnt[:, c, b:b + 1], accb.t[:], ALU.mult, ALU.add))
                V.after(m)
                m = V.done(ve.scalar_tensor_tensor(accb.t[:], null_bc[:], none[:, c, b:b + 1], accb.t[:], ALU.mult, ALU.add))
                for s in gres:
                    s.free = [m]
                SP.after(m)
                m_o = s_out.landed(sp.dma_start(out[t * P:(t + 1) * P, :], accb.t[:]))
                accb.free = [m_o]
                yield
            fin.append(m_o)

        fin = []
        items = G * NB
        for _ in split_weights(0):
            pass
        for _ in prepare(0):
            pass
        for n in range(items):
            work = [(attend(n), 25)]
            if n % NB == NB - 1 and n + 1 < items:
                pass
            if n % NB == 2 and n // NB + 1 < G:
                work.append((split_weights(n // NB + 1), 5))
            if n + 1 < items:
                work.append((prepare(n + 1), 8))
            if n // NB == G - 1 and n % NB >= 1:
                work.append((combine(n % NB - 1), TPS))
            weave(*work)
        for _ in combine(NB - 1):
            pass
        SP.after(fin[-1])
        SP.after(list(last))


def kernel(L0_attn_x, L0_attn_ln_w, L0_attn_ln_b, L0_attn_in_proj_w, L0_attn_conv_w, L0_attn_conv_b,
           L0_attn_A_log, L0_attn_D, L0_attn_dt_bias, L0_attn_gamma, L0_attn_out_proj_w, L0_ffn_w_qr,
           L0_ffn_w_kvr, L0_ffn_w_q, L0_ffn_w_kv, L0_ffn_w_out, L0_ffn_null_kv, L0_ffn_null_token):
    import numpy as np
    import concourse.bacc as bacc
    from concourse.bass_utils import run_bass_kernel_spmd

    c = np.zeros((P, C_N), np.float32)
    c[:, C_ID:C_ID + P] = np.eye(P)
    c[:, C_U:C_U + P] = np.triu(np.ones((P, P)))
    for j in range(QT):
        c[:, C_J + j] = j * P + np.arange(P)
    for r in range(NR):
        b, j = divmod(r, 2 * G)
        c[r, C_K] = NQ if j < G else NK
        c[r, C_BASE] = j * NQ - 1 - NULLROW if j < G else 0.0
    a = np.asarray
    arrays = {
        "x": a(L0_attn_x).reshape(T, D),
        "w_in": a(L0_attn_in_proj_w).T,
        "ln_w": a(L0_attn_ln_w),
        "ln_b": a(L0_attn_ln_b),
        "conv_w": a(L0_attn_conv_w),
        "conv_b": a(L0_attn_conv_b),
        "a_log": a(L0_attn_A_log),
        "d_skip": a(L0_attn_D),
        "dt_bias": a(L0_attn_dt_bias),
        "gamma": a(L0_attn_gamma),
        "w_out": a(L0_attn_out_proj_w).T,
        "w_route": np.concatenate([a(L0_ffn_w_qr), a(L0_ffn_w_kvr)], 0).T,
        "wq": a(L0_ffn_w_q).transpose(0, 2, 1),
        "wkv": a(L0_ffn_w_kv).transpose(0, 2, 1),
        "wo": a(L0_ffn_w_out).transpose(0, 2, 1),
        "null_k": a(L0_ffn_null_kv)[0, :, :, 0, :].transpose(0, 2, 1),
        "null_v": a(L0_ffn_null_kv)[1, :, :, 0, :],
        "null_tok": a(L0_ffn_null_token).reshape(D),
        "consts": c,
    }
    nc = bacc.Bacc("TRN2", target_bir_lowering=False, num_devices=1)
    feeds, args = {}, []
    for name, v in arrays.items():
        v = np.ascontiguousarray(v)
        feeds[name] = v
        args.append(nc.dram_tensor(name, v.shape, mybir.dt.from_np(v.dtype), kind="ExternalInput").ap())
    out = nc.dram_tensor("y", (T, D), F32, kind="ExternalOutput").ap()
    program(nc, *args, out)
    r = run_bass_kernel_spmd(nc, [feeds], core_ids=[0])
    return r.results[0]["y"].reshape(NB, L, D)
```

```python
from contextlib import ExitStack

import concourse.bass as bass
from concourse import mybir
from concourse.alu_op_type import AluOpType as ALU

ACT = mybir.ActivationFunctionType
AX = mybir.AxisListType
F32 = mybir.dt.float32
F16 = mybir.dt.float16
I32 = mybir.dt.int32

P = 128
NB, L, D = 8, 1024, 512
T = NB * L
KD = D // P
DI, NS, NH, HD = 1024, 128, 16, 64
CH = DI + 2 * NS
NCT = CH // P
KI = DI // P
TAPS = 4
BLK = 512
CK = BLK // P
NBLK = T // BLK
WC = DI + CH
G, NQ, NK, H, DH = 4, 512, 256, 8, 64
QT, KT = NQ // P, NK // P
NR = NB * 2 * G
NT = T // P
TPS = L // P
ROW = D + 2 * G
EPS = 1e-5
WS = 64.0
MS = 16.0
RES0 = P

C_ID, C_U, C_J, C_K, C_BASE, C_BATCH = 0, P, 2 * P, 2 * P + QT, 2 * P + QT + 1, 2 * P + QT + 2
C_N = C_BATCH + NB


class Engine:

    def __init__(self, eng, sem):
        self.eng, self.sem, self.n, self.seen = eng, sem, 0, {}

    def after(self, *marks):
        for m in marks:
            if m is None:
                continue
            if type(m) is list:
                self.after(*m)
                continue
            name, sem, value = m
            if self.seen.get(name, 0) < value:
                self.eng.wait_ge(sem, value)
                self.seen[name] = value

    def done(self, ins):
        self.n += 1
        ins.then_inc(self.sem, 1)
        return (id(self), self.sem, self.n)


class Slot:

    count = 0

    def __init__(self, t, sem=None):
        self.t, self.free, self.sem, self.n = t, [], sem, 0

    @property
    def free(self):
        return self._free

    @free.setter
    def free(self, marks):
        self._free = marks
        Slot.count += 1
        self.since = Slot.count

    def landed(self, dma):
        self.n += 16
        dma.then_inc(self.sem, 16)
        return (id(self), self.sem, self.n)


class Feed:

    def __init__(self, gen, total):
        self.gen, self.total, self.spent, self.live = gen, total, 0.0, True

    def to(self, share):
        while self.live and (share >= 1 or self.spent < share * self.total):
            try:
                self.spent += next(self.gen)
            except StopIteration:
                self.live = False


class Part:

    def __init__(self, feed, share):
        self.feed, self.share = feed, share

    def to(self, share):
        self.feed.to(min(share, 1) * self.share)


def weave(main, *feeds):
    while main.live:
        main.to(main.spent / main.total + 1e-6)
        for f in feeds:
            f.to(min(main.spent / main.total, 0.999))
    for f in feeds:
        f.to(1)


def program(nc, x, w_in, ln_w, ln_b, conv_w, conv_b, a_log, d_skip, dt_bias, gamma, w_out,
            w_route, wq, wkv, wo, null_k, null_v, null_tok, consts, out):
    ctx = ExitStack()
    with ctx:
        def sem(name):
            return ctx.enter_context(nc.semaphore(name))

        PE = Engine(nc.tensor, sem("pe_done"))
        V = Engine(nc.vector, sem("dve_done"))
        A = Engine(nc.scalar, sem("act_done"))
        Q = Engine(nc.gpsimd, sem("pool_done"))
        SP = Engine(nc.sync, sem("sp_done"))
        pe, ve, ac, po, sp = nc.tensor, nc.vector, nc.scalar, nc.gpsimd, nc.sync

        def scratch(name, shape, dt):
            return nc.dram_tensor(name, shape, dt, kind="Internal").ap()

        rows_d = scratch("rows", (T, ROW), F32)
        skip_d = scratch("skip", (T, D), F32)
        acc_d = scratch("acc", (T, D), F32)
        cum_d = scratch("cum", (NBLK, NH, BLK), F32)
        rank_d = scratch("rank", (NR, L), F16)
        res_d = [scratch(f"results{b}", (RES0 + G * NQ, D), F32) for b in range(NB)]

        singles = [Slot(ctx.enter_context(nc.psum_tensor(f"bank{i}", [P, 512], F32))) for i in range(2)]
        pairs = [Slot(ctx.enter_context(nc.psum_tensor(f"pair{i}", [P, 1024], F32))) for i in range(3)]

        def bank(kind):
            s = min((s for s in (singles if kind == "single" else pairs) if s.free is not None), key=lambda s: s.since)
            PE.after(s.free)
            s.free = None
            return s

        def sb(stack, name, shape, dt):
            return stack.enter_context(nc.sbuf_tensor(name, shape, dt))

        cst = sb(ctx, "cst", [P, C_N], F32)
        id16 = sb(ctx, "id16", [P, P], F16)
        neghalf = sb(ctx, "neghalf", [P, CK], F32)
        logit = sb(ctx, "logit", [P, TPS, NB, 2 * G], F32)
        load_const, load_small, load_wout, load_null = (Slot(None, sem(f"s_load{i}")) for i in range(4))
        id32 = cst[:, C_ID:C_ID + P]
        upper = cst[:, C_U:C_U + P]

        c1 = load_const.landed(sp.dma_start(cst[:], consts))
        A.after(c1)
        m_id16 = A.done(ac.copy(id16[:], id32))
        m_half = V.done(ve.memset(neghalf[:], -0.5))
        V.after(c1)
        PE.after(c1, m_id16)
        Q.after(c1, m_half)

        mam = ExitStack()
        with mam:
            whi = sb(mam, "whi", [P, KD, WC], F16)
            wlo = sb(mam, "wlo", [P, KD, WC], F16)
            shi = sb(mam, "shi", [P, KD, 2 * G + NH], F16)
            slo = sb(mam, "slo", [P, KD, 2 * G + NH], F16)
            ohi = sb(mam, "ohi", [P, KI, D], F16)
            olo = sb(mam, "olo", [P, KI, D], F16)
            z_bias = sb(mam, "z_bias", [P, DI], F32)
            dt_b = sb(mam, "dt_b", [P, NH], F32)
            a_neg = sb(mam, "a_neg", [P, NH], F32)
            d_bc = sb(mam, "d_bc", [P, NH], F32)
            raw_bias = sb(mam, "raw_bias", [P, NCT], F32)
            taps = sb(mam, "taps", [P, NCT, TAPS], F32)
            conv_bias = sb(mam, "conv_bias", [P, NCT], F32)

            prep = ExitStack()
            with prep:
                lw = sb(prep, "lw", [P, KD], F32)
                lb = sb(prep, "lb", [P, KD], F32)
                gm = sb(prep, "gm", [P, KI], F32)
                lb_bc = sb(prep, "lb_bc", [P, KD, P], F32)
                bias_bc = sb(prep, "bias_bc", [P, WC + NH], F32)
                al = sb(prep, "al", [P, NH], F32)
                route = sb(prep, "route", [P, KD, 2 * G], F32)
                wout_f = sb(prep, "wout_f", [P, KI, D], F32)
                NC5 = 5
                CW = (WC + NH) // NC5
                stage = [Slot(sb(prep, f"stage{i}", [P, KD, CW], F32), sem(f"s_stage{i}")) for i in range(2)]
                lw64 = sb(prep, "lw64", [P, KD], F32)
                gm64 = sb(prep, "gm64", [P, KI], F32)
                for dst, src in ((lw[:], ln_w.rearrange("(k p) -> p k", p=P)),
                                 (lb[:], ln_b.rearrange("(k p) -> p k", p=P)),
                                 (gm[:], gamma.rearrange("(k p) -> p k", p=P)),
                                 (al[:], a_log.partition_broadcast(P)),
                                 (d_bc[:], d_skip.partition_broadcast(P)),
                                 (dt_b[:], dt_bias.partition_broadcast(P)),
                                 (taps[:], conv_w.rearrange("(c p) t -> p c t", p=P)),
                                 (conv_bias[:], conv_b.rearrange("(c p) -> p c", p=P)),
                                 (route[:], w_route.rearrange("(k p) r -> p k r", p=P))):
                    small = load_small.landed(sp.dma_start(dst, src, allow_slow_non_contiguous=True))
                m_wof = load_wout.landed(sp.dma_start(wout_f[:], w_out.rearrange("(k p) n -> p k n", p=P)))
                V.after(small, m_wof)
                A.after(small, m_wof)
                m = A.done(ac.activation(a_neg[:], al[:], ACT.Exp))
                V.after(m)
                V.done(ve.tensor_scalar(a_neg[:], a_neg[:], -1.0, None, ALU.mult))
                V.done(ve.tensor_scalar(taps[:], taps[:], 0.5, None, ALU.mult))
                V.done(ve.tensor_scalar(conv_bias[:], conv_bias[:], 0.5, None, ALU.mult))
                V.done(ve.tensor_scalar(lw64[:], lw[:], WS, None, ALU.mult))
                m = V.done(ve.tensor_scalar(gm64[:], gm[:], WS, None, ALU.mult))
                m_lb = V.done(ve.tensor_copy(lb_bc[:], lb[:].unsqueeze(2).to_broadcast([P, KD, P])))
                A.after(m)
                V.after(m_lb)
                m = A.done(ac.mul(shi[:, :, 0:2 * G], route[:], WS))
                V.after(m)
                V.done(ve.scalar_tensor_tensor(slo[:, :, 0:2 * G], route[:], WS, shi[:, :, 0:2 * G],
                                               ALU.mult, ALU.subtract))
                for k in range(KI):
                    m = A.done(ac.activation(ohi[:, k, :], wout_f[:, k, :], ACT.Copy, scale=gm64[:, k:k + 1]))
                    V.after(m)
                    V.done(ve.scalar_tensor_tensor(olo[:, k, :], wout_f[:, k, :], gm64[:, k:k + 1],
                                                   ohi[:, k, :], ALU.mult, ALU.subtract))
                PE.after(m_lb)
                wr = w_in.rearrange("(k p) n -> p k n", p=P)
                for n in range(NC5):
                    s = stage[n % 2]
                    SP.after(s.free)
                    got = s.landed(sp.dma_start(s.t[:], wr[:, :, n * CW:(n + 1) * CW]))
                    A.after(got)
                    V.after(got)
                    PE.after(got)
                    bk = bank("single")
                    for k in range(KD):
                        ins = pe.matmul(bk.t[:, 0:CW], lb_bc[:, k, :], s.t[:, k, :], start=k == 0, stop=k == KD - 1)
                    m_pe = PE.done(ins)
                    A.after(m_pe)
                    m_b = A.done(ac.copy(bias_bc[:, n * CW:(n + 1) * CW], bk.t[:, 0:CW]))
                    bk.free = [m_b]
                    last = n == NC5 - 1
                    for k in range(KD):
                        w = min(CW, WC - n * CW)
                        m = A.done(ac.activation(whi[:, k, n * CW:n * CW + w], s.t[:, k, 0:w], ACT.Copy,
                                                 scale=lw64[:, k:k + 1]))
                        if last:
                            m = A.done(ac.activation(shi[:, k, 2 * G:], s.t[:, k, w:CW], ACT.Copy,
                                                     scale=lw64[:, k:k + 1]))
                        V.after(m)
                        m_v = V.done(ve.scalar_tensor_tensor(wlo[:, k, n * CW:n * CW + w], s.t[:, k, 0:w],
                                                             lw64[:, k:k + 1], whi[:, k, n * CW:n * CW + w],
                                                             ALU.mult, ALU.subtract))
                        if last:
                            m_v = V.done(ve.scalar_tensor_tensor(slo[:, k, 2 * G:], s.t[:, k, w:CW],
                                                                 lw64[:, k:k + 1], shi[:, k, 2 * G:],
                                                                 ALU.mult, ALU.subtract))
                    s.free = [m_pe, m_v]
                V.after(m_b)
                V.done(ve.tensor_copy(z_bias[:], bias_bc[:, 0:DI]))
                V.done(ve.tensor_tensor(dt_b[:], dt_b[:], bias_bc[:, WC:], ALU.add))
                PE.after(m_b)
                for c in range(NCT):
                    bk = bank("single")
                    m = PE.done(pe.transpose(bk.t[:, 0:P], bias_bc[:, DI + c * P:DI + (c + 1) * P], id32))
                    V.after(m)
                    m_v = V.done(ve.tensor_copy(raw_bias[:, c:c + 1], bk.t[:, 0:1]))
                    bk.free = [m_v]
                w_ready = [m_v, m]

            for e in (PE, V, A, Q, SP):
                e.after(w_ready)

            s_x = [sem(f"s_x{i}") for i in range(1)]
            xin = [Slot(sb(mam, "xin", [P, CK, D], F32), s_x[0])]
            xn = [Slot(sb(mam, f"xn{i}", [P, D], F32)) for i in range(1)]
            rowt = Slot(sb(mam, "rowt", [P, CK, ROW], F32), sem("s_row"))
            row16 = rowt.t[:].bitcast(F16)
            xh = [Slot(sb(mam, f"xh{i}", [P, 2, D], F16)) for i in range(1)]
            xhT = [Slot(sb(mam, f"xhT{i}", [P, 2, KD, BLK], F16)) for i in range(2)]
            s_skip = sem("s_skip")
            stats = sb(mam, "stats", [P, CK, 6], F32)
            mv = sb(mam, "mv", [P, CK, 2], F32)
            nrm = sb(mam, "nrm", [P, 6, CK], F32)
            dts = sb(mam, "dts", [P, 5, CK * NH], F32)
            dt_t = [Slot(sb(mam, f"dt{i}", [P, CK, NH], F32)) for i in range(2)]
            cum_t = [Slot(sb(mam, f"cum{i}", [P, CK, NH], F32)) for i in range(2)]
            ecum = [Slot(sb(mam, f"ecum{i}", [P, CK, NH], F32)) for i in range(2)]
            cumT = Slot(sb(mam, "cumT", [NH, BLK], F32), sem("s_cumT"))
            raw = [Slot(sb(mam, f"raw{i}", [P, BLK + TAPS - 1], F32)) for i in range(2)]
            halo = sb(mam, "halo", [P, NCT, TAPS - 1], F32)
            cv = [Slot(sb(mam, f"cv{i}", [P, BLK], F32)) for i in range(2)]
            xsT = [Slot(sb(mam, f"xsT{i}", [P, NCT, BLK], F32)) for i in range(2)]

            bc = Slot(sb(mam, "bc", [P, NH, P], F32), sem("s_bc"))
            de = Slot(sb(mam, "de", [P, NH, P], F32))
            skipb = [Slot(sb(mam, f"skipb{i}", [P, D], F32), sem(f"s_skipb{i}")) for i in range(2)]
            s_acc = [sem(f"s_acc{i}") for i in range(2)]
            accw = [Slot(None, s) for s in s_acc]
            xdt = Slot(sb(mam, "xdt", [P, NH, HD], F32))
            dxs = Slot(sb(mam, "dxs", [P, NH, HD], F32))
            xw = Slot(sb(mam, "xw", [P, NH, HD], F32))
            state = [Slot(sb(mam, f"state{i}", [P, NH, HD], F32)) for i in range(2)]
            btok = Slot(sb(mam, "btok", [P, P], F32))
            gmask = Slot(sb(mam, "gmask", [P, P], F32))
            decs = Slot(sb(mam, "decs", [P, 3, NH], F32))
            zs = Slot(sb(mam, "zs", [P, DI], F32))
            yb = Slot(sb(mam, "yb", [P, NH, HD], F32))
            yn = sb(mam, "yn", [P, 3], F32)
            yhl = Slot(sb(mam, "yhl", [P, 2, DI], F16))
            yT = Slot(sb(mam, "yT", [P, 2 * KI, P], F16))
            skip_w = Slot(None, s_skip)
            skip_marks = {}
            cum_marks = {}
            row_marks = []
            front_out = {}
            acc_marks = []

            def front(i):
                b, half = divmod(i, L // BLK)
                u = i % 2
                xi = xin[0]
                SP.after(xi.free)
                got = xi.landed(sp.dma_start(xi.t[:], x[i * BLK:(i + 1) * BLK, :].rearrange("(c p) d -> p c d", p=P)))
                V.after(got)
                for c in range(CK):
                    m = V.done(ve.bn_stats(stats[:, c, :], xi.t[:, c, :]))
                    V.after(m)
                    m = V.done(ve.bn_aggr(mv[:, c, :], stats[:, c, :]))
                V.after(m)
                var, mean = mv[:, :, 1], mv[:, :, 0]
                r1, r2, q2, t0, v2 = (nrm[:, j, :] for j in range(5))
                m = V.done(ve.tensor_scalar(t0, var, EPS, None, ALU.add))
                Q.after(m)
                m = Q.done(po.tensor_tensor(r1, t0, neghalf[:], ALU.pow))
                V.after(m)
                m = V.done(ve.tensor_tensor(v2, var, r1, ALU.mult))
                V.after(m)
                m = V.done(ve.tensor_tensor(v2, v2, r1, ALU.mult))
                V.after(m)
                m = V.done(ve.tensor_scalar(v2, v2, EPS, None, ALU.add))
                Q.after(m)
                m = Q.done(po.tensor_tensor(r2, v2, neghalf[:], ALU.pow))
                V.after(m)
                m_q2 = V.done(ve.tensor_tensor(q2, v2, r2, ALU.mult))
                A.after(m_q2)
                xt = xhT[u]
                yield 0.1
                for c in range(CK):
                    n_, h_ = xn[0], xh[0]
                    V.after(n_.free)
                    m_xn = V.done(ve.tensor_scalar(n_.t[:], xi.t[:, c, :], mean[:, c:c + 1], r1[:, c:c + 1],
                                                   ALU.subtract, ALU.mult))
                    A.after(m_xn, rowt.free if c == 0 else None, h_.free)
                    hi, lo = row16[:, c, 0:D], row16[:, c, D:2 * D]
                    m_hi = A.done(ac.copy(hi, n_.t[:]))
                    m_xh = A.done(ac.activation(h_.t[:, 0, :], n_.t[:], ACT.Copy, scale=r2[:, c:c + 1]))
                    Q.after(m_hi)
                    m_lo = Q.done(po.tensor_tensor(lo, n_.t[:], hi, ALU.subtract))
                    m_sk = Q.done(po.tensor_tensor(xi.t[:, c, :], xi.t[:, c, :], n_.t[:], ALU.add))
                    V.after(m_xh)
                    m_xl = V.done(ve.scalar_tensor_tensor(h_.t[:, 1, :], n_.t[:], r2[:, c:c + 1], h_.t[:, 0, :],
                                                          ALU.mult, ALU.subtract))
                    n_.free = [m_xh, m_xl, m_sk]
                    yield 0.0
                    PE.after(m_xl)
                    bk = bank("single")
                    b16 = bk.t[:].bitcast(F16)
                    for j in range(2 * KD):
                        ins = pe.transpose(b16[:, j * P:(j + 1) * P], h_.t[:, j // KD, (j % KD) * P:(j % KD + 1) * P], id16[:])
                    m_t = PE.done(ins)
                    h_.free = [m_t]
                    A.after(m_t, xt.free if c == 0 else None)
                    m_e = A.done(ac.copy(xt.t[:].bitcast(F32)[:, :, :, c * P // 2:(c + 1) * P // 2].rearrange("p h k t -> p (h k) t"),
                                         bk.t[:].rearrange("p (j t) -> p j t", j=2 * KD)))
                    bk.free = [m_e]
                    yield 0.9
                m_xhT = m_e
                SP.after(m_sk)
                skip_marks[i] = skip_w.landed(sp.dma_start(
                    skip_d[i * BLK:(i + 1) * BLK, :].rearrange("(c p) d -> p c d", p=P), xi.t[:]))
                xi.free = [skip_marks[i]]
                PE.after(m_xhT)
                bk = bank("single")
                NW = 2 * G + NH
                for c in range(CK):
                    cs = slice(c * P, (c + 1) * P)
                    n = 0
                    for k in range(KD):
                        for ha, w in ((0, shi), (0, slo), (1, shi)):
                            ins = pe.matmul(bk.t[:, c * NW:(c + 1) * NW], xt.t[:, ha, k, cs], w[:, k, :],
                                            start=n == 0, stop=n == 3 * KD - 1)
                            n += 1
                m = PE.done(ins)
                V.after(m)
                sm = bk.t[:, 0:CK * NW].rearrange("p (c n) -> p c n", c=CK)
                for c in range(CK):
                    m_lg = V.done(ve.tensor_scalar(logit[:, half * CK + c, b, :], sm[:, c, 0:2 * G], q2[:, c:c + 1],
                                                   1.0 / WS, ALU.mult, ALU.mult))
                xr, ex, sq, s2, pl = (dts[:, j, :].rearrange("p (c h) -> p c h", c=CK) for j in range(5))
                m = V.done(ve.scalar_tensor_tensor(xr, sm[:, :, 2 * G:], 1.0 / WS,
                                                   dt_b[:].unsqueeze(1).to_broadcast([P, CK, NH]), ALU.mult, ALU.add))
                bk.free = [m_lg, m]
                V.after(m)
                yield 1.3
                A.after(m_lg)
                sc = rowt.t[:, :, D:ROW]
                m_s = A.done(ac.activation(sc, logit[:, half * CK:(half + 1) * CK, b, :], ACT.Tanh, scale=0.5))
                V.after(m_s)
                m_s = V.done(ve.tensor_scalar(sc, sc, 0.5, 0.5, ALU.mult, ALU.add))
                SP.after(m_s, m_lo)
                m_row = rowt.landed(sp.dma_start(rows_d[i * BLK:(i + 1) * BLK, :].rearrange("(c p) d -> p c d", p=P), rowt.t[:]))
                rowt.free = [m_row]
                row_marks.append(m_row)
                m = V.done(ve.scalar_tensor_tensor(ex, xr, -1.0, xr, ALU.mult, ALU.max))
                A.after(m)
                m = A.done(ac.activation(ex, ex, ACT.Exp, scale=-1.0))
                V.after(m)
                m = V.done(ve.tensor_scalar(sq, ex, 2.0, None, ALU.add))
                V.after(m)
                m = V.done(ve.reciprocal(sq, sq))
                V.after(m)
                m = V.done(ve.tensor_tensor(sq, sq, ex, ALU.mult))
                V.after(m)
                m = V.done(ve.tensor_tensor(s2, sq, sq, ALU.mult))
                V.after(m)
                m = V.done(ve.tensor_scalar(pl, s2, 2.0 / 17, None, ALU.mult))
                for j in range(15, 1, -2):
                    V.after(m)
                    m = V.done(ve.scalar_tensor_tensor(pl, pl, 2.0 / j, s2, ALU.add, ALU.mult))
                V.after(m)
                m = V.done(ve.scalar_tensor_tensor(pl, pl, 2.0, sq, ALU.add, ALU.mult))
                V.after(m, dt_t[u].free)
                dt = dt_t[u].t
                m_dt = V.done(ve.scalar_tensor_tensor(dt[:], xr, 0.0, pl, ALU.max, ALU.add))
                V.after(m_dt)
                m_a = V.done(ve.tensor_tensor(xr, dt[:], a_neg[:].unsqueeze(1).to_broadcast([P, CK, NH]), ALU.mult))
                if half == 0:
                    if i > 0:
                        V.after(front_out[i - 1][4])
                    m_halo = V.done(ve.memset(halo[:], 0.0))
                xs = xsT[u]
                for pr in range(NCT // 2):
                    bk = bank("pair")
                    for j in range(2):
                        ct = 2 * pr + j
                        n = 0
                        for k in range(KD):
                            ws = slice(DI + ct * P, DI + (ct + 1) * P)
                            for ha, w in ((0, whi), (1, whi), (0, wlo)):
                                ins = pe.matmul(bk.t[:, j * BLK:(j + 1) * BLK], w[:, k, ws], xt.t[:, ha, k, :],
                                                start=n == 0, stop=n == 3 * KD - 1)
                                n += 1
                        m_mm = PE.done(ins)
                        r_, c_ = raw[j], cv[j]
                        A.after(m_mm, r_.free)
                        m_r = A.done(ac.activation(r_.t[:, TAPS - 1:], bk.t[:, j * BLK:(j + 1) * BLK], ACT.Identity,
                                                   bias=raw_bias[:, ct:ct + 1], scale=1.0 / WS))
                        if half == 0 and ct == 0:
                            A.after(m_halo)
                        m = A.done(ac.copy(r_.t[:, 0:TAPS - 1], halo[:, ct, :]))
                        A.after(m, m_r)
                        m_h = A.done(ac.copy(halo[:, ct, :], r_.t[:, BLK:]))
                        A.after(c_.free)
                        m = A.done(ac.activation(c_.t[:], r_.t[:, 0:BLK], ACT.Identity, bias=conv_bias[:, ct:ct + 1],
                                                 scale=taps[:, ct, 0:1]))
                        for t in range(1, TAPS):
                            V.after(m, m_h)
                            m = V.done(ve.scalar_tensor_tensor(c_.t[:], r_.t[:, t:t + BLK], taps[:, ct, t:t + 1], c_.t[:],
                                                               ALU.mult, ALU.add))
                        r_.free = [m, m_h]
                        A.after(m)
                        th = bk.t[:, j * BLK:(j + 1) * BLK]
                        m_th = A.done(ac.activation(th, c_.t[:], ACT.Tanh))
                        V.after(m_th, xs.free if ct == 0 else None)
                        m_xs = V.done(ve.scalar_tensor_tensor(xs.t[:, ct, :], th, 1.0, c_.t[:], ALU.add, ALU.mult))
                        c_.free = [m_xs]
                        yield 2.6
                    bk.free = [m_xs]
                    if pr == 0:
                        PE.after(m_a)
                        bk = bank("single")
                        for c in range(CK):
                            ins = pe.matmul(bk.t[:, c * NH:(c + 1) * NH], upper, xr[:, c, :], start=True, stop=True)
                        m = PE.done(ins)
                        V.after(m, cum_t[u].free)
                        A.after(m, ecum[u].free)
                        m_cum = V.done(ve.tensor_copy(cum_t[u].t[:], bk.t[:, 0:CK * NH].rearrange("p (c h) -> p c h", c=CK)))
                        A.after(m_cum)
                        m_ec = A.done(ac.activation(ecum[u].t[:], cum_t[u].t[:], ACT.Exp))
                        bk.free = [m_cum]
                        bk = bank("single")
                        for c in range(CK):
                            ins = pe.matmul(bk.t[0:NH, c * P:(c + 1) * P], xr[:, c, :], upper, start=True, stop=True)
                        m = PE.done(ins)
                        A.after(m, cumT.free)
                        m = A.done(ac.copy(cumT.t[:], bk.t[0:NH, :]))
                        bk.free = [m]
                        SP.after(m)
                        cum_marks[i] = cumT.landed(sp.dma_start(cum_d[i], cumT.t[:]))
                        cumT.free = [cum_marks[i]]
                front_out[i] = (m_xs, m_dt, m_cum, m_ec, m_h)

            norm_of, yT_of = {}, {}
            bc.chunk = None

            def load_chunk(ch):
                i, c = divmod(ch, CK)
                SP.after(bc.free, cum_marks[i])
                bc.chunk = ch
                bc.got = bc.landed(sp.dma_start(bc.t[:], cum_d[i][:, c * P:(c + 1) * P].partition_broadcast(P)))
                sk = skipb[ch % 2]
                SP.after(sk.free, skip_marks[i])
                sk.got = sk.landed(sp.dma_start(sk.t[:], skip_d[ch * P:(ch + 1) * P, :]))

            def normalise(ch):
                yf, m_y = norm_of[ch]
                A.after(m_y, yhl.free)
                m = A.done(ac.activation(yhl.t[:, 0, :], yf, ACT.Square, accum_out=yn[:, 0:1]))
                V.after(m)
                m = V.done(ve.tensor_scalar(yn[:, 1:2], yn[:, 0:1], 1.0 / DI, EPS, ALU.mult, ALU.add))
                Q.after(m)
                m_r = Q.done(po.tensor_tensor(yn[:, 2:3], yn[:, 1:2], neghalf[:, 0:1], ALU.pow))
                A.after(m_r)
                m_h = A.done(ac.activation(yhl.t[:, 0, :], yf, ACT.Copy, scale=yn[:, 2:3]))
                V.after(m_h)
                m_l = V.done(ve.scalar_tensor_tensor(yhl.t[:, 1, :], yf, yn[:, 2:3], yhl.t[:, 0, :], ALU.mult, ALU.subtract))
                yb.free = [m_h, m_l]
                norm_of[ch] = m_l

            def turn_y(ch):
                PE.after(norm_of[ch])
                pt = bank("pair")
                pt16 = pt.t[:].bitcast(F16)
                for j in range(2 * KI):
                    ins = pe.transpose(pt16[:, j * P:(j + 1) * P], yhl.t[:, j // KI, (j % KI) * P:(j % KI + 1) * P], id16[:])
                m_t = PE.done(ins)
                yhl.free = [m_t]
                A.after(m_t, yT.free)
                m_yT = A.done(ac.copy(yT.t[:].bitcast(F32).rearrange("p j t -> p (j t)"), pt.t[:]))
                pt.free = [m_yT]
                yT_of[ch] = m_yT

            def project(ch):
                PE.after(yT_of[ch])
                bk = bank("single")
                n = 0
                for k in range(KI):
                    for ha, w in ((0, ohi), (0, olo), (1, ohi)):
                        ins = pe.matmul(bk.t[:], yT.t[:, ha * KI + k, :], w[:, k, :], start=n == 0, stop=n == 3 * KI - 1)
                        n += 1
                m_o = PE.done(ins)
                yT.free = [m_o]
                sk = skipb[ch % 2]
                V.after(m_o, sk.got)
                m_s = V.done(ve.scalar_tensor_tensor(sk.t[:], bk.t[:], 1.0 / WS, sk.t[:], ALU.mult, ALU.add))
                bk.free = [m_s]
                SP.after(m_s)
                m_a = accw[ch % 2].landed(sp.dma_start(acc_d[ch * P:(ch + 1) * P, :], sk.t[:]))
                sk.free = [m_a]
                acc_marks.append(m_a)

            def back(i):
                b, half = divmod(i, L // BLK)
                u = i % 2
                m_xs, m_dt, m_cum, m_ec, _ = front_out[i]
                xs, xt = xsT[u], xhT[u]
                dt, cum, ec = dt_t[u].t, cum_t[u].t, ecum[u].t
                for c in range(CK):
                    ch = i * CK + c
                    cs = slice(c * P, (c + 1) * P)
                    old, new = state[ch % 2], state[(ch + 1) % 2]
                    if bc.chunk != ch:
                        load_chunk(ch)
                    m_bc = bc.got
                    if half == 0 and c == 0:
                        V.after(old.free)
                        old.ready = V.done(ve.memset(old.t[:], 0.0))
                    m_old = old.ready
                    PE.after(m_xs)
                    px = bank("pair")
                    for k in range(KI):
                        ins = pe.transpose(px.t[:, k * P:(k + 1) * P], xs.t[:, k, cs], id32)
                    m_px = PE.done(ins)
                    bk = bank("single")
                    pe.transpose(bk.t[:, 0:P], xs.t[:, KI, cs], id32)
                    m_g = PE.done(pe.matmul(bk.t[:, P:2 * P], xs.t[:, KI, cs], xs.t[:, KI + 1, cs], start=True, stop=True))
                    Q.after(m_bc, m_cum, de.free)
                    m = Q.done(po.tensor_tensor(de.t[:], cum[:, c, :].unsqueeze(2).to_broadcast([P, NH, P]), bc.t[:], ALU.subtract))
                    V.after(m_bc, m_cum, decs.free)
                    m_d1 = V.done(ve.tensor_tensor(decs.t[:, 0, :], bc.t[:, :, P - 1], cum[:, c, :], ALU.subtract))
                    A.after(m_d1, m_bc)
                    m_dec = A.done(ac.activation(decs.t[:, 1, :], decs.t[:, 0, :], ACT.Exp))
                    m_cd = A.done(ac.activation(decs.t[:, 2, :], bc.t[:, :, P - 1], ACT.Exp))
                    A.after(m_g, btok.free)
                    m_bt = A.done(ac.copy(btok.t[:], bk.t[:, 0:P]))
                    bc.free = [m, m_d1, m_cd]
                    A.after(m)
                    m_e = A.done(ac.activation(de.t[:], de.t[:], ACT.Relu))
                    A.after(m_e)
                    m_e = A.done(ac.activation(de.t[:], de.t[:], ACT.Exp, scale=-1.0))
                    V.after(m_px, m_dt, xdt.free)
                    p3 = px.t[:].rearrange("p (h d) -> p h d", h=NH)
                    m_xdt = V.done(ve.tensor_tensor(xdt.t[:], p3, dt[:, c, :].unsqueeze(2).to_broadcast([P, NH, HD]), ALU.mult))
                    V.after(dxs.free)
                    m_dxs = V.done(ve.tensor_tensor(dxs.t[:], p3, d_bc[:].unsqueeze(2).to_broadcast([P, NH, HD]), ALU.mult))
                    px.free = [m_dxs]
                    V.after(m_g, m_bt, gmask.free)
                    m_gm = V.done(ve.tensor_tensor(gmask.t[:], bk.t[:, P:2 * P], upper, ALU.mult))
                    bk.free = [m_gm]
                    Q.after(m_xdt, m_dec, xw.free)
                    m_xw = Q.done(po.tensor_tensor(xw.t[:], xdt.t[:], decs.t[:, 1, :].unsqueeze(2).to_broadcast([P, NH, HD]), ALU.mult))
                    Q.after(m_cd, m_old, new.free)
                    m_sd = Q.done(po.tensor_tensor(new.t[:], old.t[:], decs.t[:, 2, :].unsqueeze(2).to_broadcast([P, NH, HD]), ALU.mult))
                    decs.free = [m_sd]
                    yield 1.2
                    pz = bank("pair")
                    for j in range(2):
                        n = 0
                        for k in range(KD):
                            for ha, w in ((0, whi), (0, wlo), (1, whi)):
                                ins = pe.matmul(pz.t[:, j * 512:(j + 1) * 512], xt.t[:, ha, k, cs], w[:, k, j * 512:(j + 1) * 512],
                                                start=n == 0, stop=n == 3 * KD - 1)
                                n += 1
                    m_z = PE.done(ins)
                    V.after(m_z, zs.free)
                    m_zs = V.done(ve.scalar_tensor_tensor(zs.t[:], pz.t[:], 1.0 / WS, z_bias[:], ALU.mult, ALU.add))
                    A.after(m_zs)
                    m_zt = A.done(ac.activation(pz.t[:], zs.t[:], ACT.Tanh, scale=0.5))
                    if ch > 0:
                        turn_y(ch - 1)
                    V.after(m_e, m_gm)
                    m_m = V.done(ve.tensor_tensor(de.t[:], de.t[:], gmask.t[:].unsqueeze(1).to_broadcast([P, NH, P]), ALU.mult))
                    gmask.free = [m_m]
                    V.after(m_zt)
                    m_sz = V.done(ve.scalar_tensor_tensor(zs.t[:], pz.t[:], 1.0, zs.t[:], ALU.add, ALU.mult))
                    pz.free = [m_sz]
                    yield 6.0
                    PE.after(m_old)
                    pi = bank("pair")
                    sf = old.t[:].rearrange("p h d -> p (h d)")
                    for j in range(2):
                        ins = pe.matmul(pi.t[:, j * 512:(j + 1) * 512], xs.t[:, KI + 1, cs], sf[:, j * 512:(j + 1) * 512], start=True, stop=True)
                    m_i = PE.done(ins)
                    V.after(m_i, m_ec, yb.free)
                    m_y = V.done(ve.tensor_tensor(yb.t[:], pi.t[:].rearrange("p (h d) -> p h d", h=NH),
                                                  ec[:, c, :].unsqueeze(2).to_broadcast([P, NH, HD]), ALU.mult))
                    pi.free = [m_y]
                    Q.after(m_y, m_dxs)
                    m_y = Q.done(po.tensor_tensor(yb.t[:], yb.t[:], dxs.t[:], ALU.add))
                    dxs.free = [m_y]
                    PE.after(m_bt, m_xw)
                    pn = bank("pair")
                    xf = xw.t[:].rearrange("p h d -> p (h d)")
                    for j in range(2):
                        ins = pe.matmul(pn.t[:, j * 512:(j + 1) * 512], btok.t[:], xf[:, j * 512:(j + 1) * 512], start=True, stop=True)
                    m_n = PE.done(ins)
                    btok.free = [m_n]
                    xw.free = [m_n]
                    V.after(m_n, m_sd)
                    m_new = V.done(ve.tensor_tensor(new.t[:], new.t[:], pn.t[:].rearrange("p (h d) -> p h d", h=NH), ALU.add))
                    pn.free = [m_new]
                    new.ready = m_new
                    old.free = [m_i, m_sd]
                    if ch > 0:
                        project(ch - 1)
                    if ch + 1 < NBLK * CK and (c < CK - 1 or i + 1 in cum_marks):
                        load_chunk(ch + 1)
                    yield 8.5
                    PE.after(m_m, m_xdt)
                    pw = bank("pair")
                    for h in range(NH):
                        ins = pe.matmul(pw.t[:, h * HD:(h + 1) * HD], de.t[:, h, :], xdt.t[:, h, :], start=True, stop=True)
                    m_w = PE.done(ins)
                    de.free = [m_w]
                    xdt.free = [m_w, m_xw]
                    V.after(m_w, m_y)
                    m_y = V.done(ve.tensor_tensor(yb.t[:], yb.t[:], pw.t[:].rearrange("p (h d) -> p h d", h=NH), ALU.add))
                    pw.free = [m_y]
                    yf = yb.t[:].rearrange("p h d -> p (h d)")
                    V.after(m_y, m_sz)
                    m_y = V.done(ve.scalar_tensor_tensor(yf, yf, 0.5, zs.t[:], ALU.mult, ALU.mult))
                    zs.free = [m_y]
                    norm_of[ch] = (yf, m_y)
                    yield 3.4
                    normalise(ch)
                    yield 0.1
                xs.free = [m_g, m_i]
                xt.free = [m_z]
                dt_t[u].free = [m_xdt]
                cum_t[u].free = [m_d1, m_e, m_ec]
                ecum[u].free = [m_y]

            Feed(front(0), 1).to(1)
            for i in range(NBLK):
                weave(Feed(back(i), CK * 19.2), *([Feed(front(i + 1), 31.0)] if i + 1 < NBLK else []))
            turn_y(NBLK * CK - 1)
            project(NBLK * CK - 1)
            mamba_end = [m for m in (acc_marks[-1], acc_marks[-2], row_marks[-1], skip_marks[NBLK - 1])]
            mamba_end += [(id(e), e.sem, e.n) for e in (PE, V, A, Q)]

        for e in (PE, V, A, Q, SP):
            e.after(mamba_end)

        idx_tok = sb(ctx, "idx_tok", [P, TPS, NR], I32)
        cnt = sb(ctx, "cnt", [P, TPS, NB], F32)
        s_rank = Slot(None, sem("s_rank"))
        top = ExitStack()
        with top:
            lg = sb(top, "lg", [NR, L], F32)
            junk = sb(top, "junk", [NR, L], F32)
            gt = sb(top, "gt", [NR, L], F32)
            eq = sb(top, "eq", [NR, L], F32)
            rk = sb(top, "rk", [NR, L], F32)
            zero = sb(top, "zero", [NR, L], F32)
            rk16 = sb(top, "rk16", [NR, L], F16)
            key = sb(top, "key", [NR, 4], I32)
            num = sb(top, "num", [NR, 4], F32)
            idx_f = sb(top, "idx_f", [P, TPS, NR], F32)
            none = sb(top, "none", [P, TPS, NB], F32)
            selt = sb(top, "selt", [P, TPS, NR], F32)
            PE.after([(id(V), V.sem, V.n)])
            for c in range(TPS):
                bk = bank("single")
                m = PE.done(pe.transpose(bk.t[0:NR, 0:P], logit[:, c, :, :].rearrange("p b j -> p (b j)"), id32))
                V.after(m)
                m = V.done(ve.tensor_copy(lg[:, c * P:(c + 1) * P], bk.t[0:NR, 0:P]))
                bk.free = [m]
            V.done(ve.memset(zero[:], 0.0))
            m = V.done(ve.memset(key[:], 0))
            found, cand, inv, ok = (key[:, j:j + 1] for j in range(4))
            val = num[:, 0:1]
            ks = cst[0:NR, C_K:C_K + 1]
            MIN = -2 ** 31

            def decode(src):
                m = V.done(ve.tensor_scalar(inv, src, 31, -1, ALU.arith_shift_right, ALU.bitwise_xor))
                V.after(m)
                m = V.done(ve.tensor_scalar(inv, inv, MIN, None, ALU.bitwise_or))
                V.after(m)
                m = V.done(ve.tensor_tensor(val.bitcast(I32), inv, src, ALU.bitwise_xor))
                V.after(m)

            for bit in range(31, -1, -1):
                V.after(m)
                m = V.done(ve.tensor_scalar(cand, found, MIN if bit == 31 else 1 << bit, None, ALU.bitwise_or))
                V.after(m)
                decode(cand)
                m = V.done(ve.tensor_scalar(junk[:], lg[:], val, 0.0, ALU.is_ge, ALU.add, accum_out=num[:, 1:2]))
                V.after(m)
                m = V.done(ve.tensor_tensor(ok, num[:, 1:2], ks, ALU.is_ge))
                V.after(m)
                m = V.done(ve.copy_predicated(found, ok, cand))
            V.after(m)
            decode(found)
            m = V.done(ve.tensor_scalar(gt[:], lg[:], val, 0.0, ALU.is_gt, ALU.add, accum_out=num[:, 1:2]))
            m2 = V.done(ve.tensor_scalar(eq[:], lg[:], val, None, ALU.is_equal))
            V.after(m2)
            m = V.done(ve.tensor_tensor(num[:, 2:3], ks, num[:, 1:2], ALU.subtract))
            m = V.done(ve.tensor_tensor_scan(rk[:], eq[:], zero[:], 0.0, ALU.add, ALU.add))
            V.after(m)
            m = V.done(ve.scalar_tensor_tensor(eq[:], rk[:], num[:, 2:3], eq[:], ALU.is_le, ALU.mult))
            V.after(m)
            m = V.done(ve.tensor_tensor(gt[:], gt[:], eq[:], ALU.add))
            V.after(m)
            m = V.done(ve.tensor_tensor_scan(rk[:], gt[:], zero[:], 0.0, ALU.add, ALU.add))
            V.after(m)
            m_rk = V.done(ve.tensor_copy(rk16[:], rk[:]))
            SP.after(m_rk)
            m_rank = s_rank.landed(sp.dma_start(rank_d, rk16[:]))
            m = V.done(ve.scalar_tensor_tensor(eq[:], rk[:], cst[0:NR, C_BASE:C_BASE + 1], gt[:], ALU.add, ALU.mult))
            V.after(m)
            PE.after(m)
            for c in range(TPS):
                bk = bank("single")
                pe.transpose(bk.t[:, 0:NR], eq[:, c * P:(c + 1) * P], cst[0:NR, C_ID:C_ID + NR])
                m = PE.done(pe.transpose(bk.t[:, NR:2 * NR], gt[:, c * P:(c + 1) * P], cst[0:NR, C_ID:C_ID + NR]))
                V.after(m)
                m_ix = V.done(ve.tensor_copy(idx_f[:, c, :], bk.t[:, 0:NR]))
                m = V.done(ve.tensor_copy(selt[:, c, :], bk.t[:, NR:2 * NR]))
                bk.free = [m]
            V.after(m)
            m = V.done(ve.tensor_reduce(cnt[:], selt[:].rearrange("p c (b j) -> p c b j", b=NB)[:, :, :, 0:G], AX.X, ALU.add))
            V.after(m)
            m = V.done(ve.tensor_scalar(none[:], cnt[:], 0.0, None, ALU.is_equal))
            V.after(m)
            idx0 = idx_f[:].rearrange("p c (b j) -> p c b j", b=NB)[:, :, :, 0]
            m = V.done(ve.tensor_tensor(idx0, idx0, none[:], ALU.add))
            V.after(m)
            V.done(ve.tensor_copy(idx_tok[:], idx_f[:]))
            m = V.done(ve.tensor_scalar(cnt[:], cnt[:], 1.0, None, ALU.max))
            V.after(m)
            m_cnt = V.done(ve.reciprocal(cnt[:], cnt[:]))
            top_end = [m_cnt, m_rank]
        for e in (PE, V, A, Q, SP):
            e.after(top_end)

        NW = 4 * D
        wts = [[Slot(sb(ctx, f"w{h}{i}", [P, KD, NW], F16)) for h in ("hi", "lo")] for i in range(2)]
        SC = 256
        wst = [Slot(sb(ctx, f"wst{i}", [P, KD, SC], F32), sem(f"s_wst{i}")) for i in range(2)]
        rbc = [Slot(sb(ctx, f"rbc{i}", [P, L], F16), sem(f"s_rbc{i}")) for i in range(2)]
        rjunk = sb(ctx, "rjunk", [P, L], F16)
        slot_f = sb(ctx, "slot_f", [P, QT + KT], F32)
        slot_i = [Slot(sb(ctx, f"slot_i{i}", [P, QT + KT], I32)) for i in range(2)]
        gat = [Slot(sb(ctx, f"gat{i}", [P, ROW], F32), sem(f"s_gat{i}")) for i in range(QT + KT)]
        kscore = Slot(sb(ctx, "kscore", [P, KT], F32))
        qscore = [Slot(sb(ctx, f"qscore{i}", [P, QT], F32)) for i in range(2)]
        xq = Slot(sb(ctx, "xq", [P, 2 * KD, NQ], F16))
        xk = Slot(sb(ctx, "xk", [P, 2 * KD, NK], F16))
        qa = [Slot(sb(ctx, f"qa{i}", [P, H, NQ], F16)) for i in range(2)]
        qb = [Slot(sb(ctx, f"qb{i}", [P, H, NQ], F16)) for i in range(1)]
        KW = NK + 2
        ka = [Slot(sb(ctx, f"ka{i}", [P, H, KW], F16)) for i in range(2)]
        kb = [Slot(sb(ctx, f"kb{i}", [P, H, NK], F16)) for i in range(2)]
        vhi = [Slot(sb(ctx, f"vhi{i}", [P, KT, H, DH + 1], F16)) for i in range(2)]
        vlo = [Slot(sb(ctx, f"vlo{i}", [P, KT, H, DH], F16)) for i in range(2)]
        nkf = [Slot(sb(ctx, f"nkf{i}", [DH, H], F32), sem(f"s_nkf{i}")) for i in range(2)]
        nkl = [Slot(sb(ctx, f"nkl{i}", [DH, 2, H], F16)) for i in range(2)]
        nvf = [Slot(sb(ctx, f"nvf{i}", [H, DH + 1], F32), sem(f"s_nvf{i}")) for i in range(2)]
        nvd = sb(ctx, "nvd", [H, H, DH + 1], F32)
        nvb = [Slot(sb(ctx, f"nvb{i}", [96, H, DH + 1], F16)) for i in range(2)]
        smx = sb(ctx, "smx", [P, QT, H], F32)
        snl = sb(ctx, "snl", [P, QT, H], F32)
        pnl = sb(ctx, "pnl", [P, QT, H], F32)
        pnm = sb(ctx, "pnm", [P, QT, 104], F16)
        pnT = sb(ctx, "pnT", [104, NQ], F16)
        pf = [Slot(sb(ctx, f"pf{i}", [P, KT, NQ], F32)) for i in range(2)]
        ph = [Slot(sb(ctx, f"ph{i}", [P, 2, KT, NQ], F16)) for i in range(2)]
        rden = sb(ctx, "rden", [P, H, QT], F32)
        of = [Slot(sb(ctx, f"of{i}", [P, QT, DH], F32)) for i in range(2)]
        ohl = Slot(sb(ctx, "ohl", [P, 2, QT, D], F16))
        oT = [Slot(sb(ctx, f"oT{i}", [P, 2 * KD, P], F16)) for i in range(2)]
        res = [Slot(sb(ctx, f"res{i}", [P, D], F32), sem(f"s_res{i}")) for i in range(2)]
        accb = [Slot(sb(ctx, f"accb{i}", [P, D], F32), sem(f"s_accb{i}")) for i in range(2)]
        stored = [Slot(None, sem(f"s_out{i}")) for i in range(2)]
        spare = [h.t[:].rearrange("p k n -> p (k n)").bitcast(F32) for h in wts[G % 2]]
        gres = [[Slot(spare[0][:, (i * G + g) * D:(i * G + g + 1) * D], sem(f"s_gres{i}{g}")) for g in range(G)]
                for i in range(2)]
        held = [spare[1][:, c * D:(c + 1) * D] for c in range(TPS)]
        SCALE = DH ** -0.5
        m = V.done(ve.memset(pnm[:], 0.0))
        for i in range(2):
            m = V.done(ve.memset(nvb[i].t[:], 0.0))
            m = V.done(ve.memset(vhi[i].t[:], 1.0))
            m = V.done(ve.tensor_scalar(kb[i].t[DH:DH + H, :, :],
                                        cst[0:H, C_ID:C_ID + H].unsqueeze(2).to_broadcast([H, H, NK]), MS, None, ALU.mult))
            m = V.done(ve.memset(nvf[i].t[:], 1.0))
        m_z = V.done(ve.memset(res[0].t[:], 0.0))
        zero_rows = Slot(None, sem("s_zero_rows"))
        SP.after(m_z)
        SP.after(load_null.landed(sp.dma_start(res[0].t[1:2, :], null_tok)))
        for b in range(NB):
            m_zero = zero_rows.landed(sp.dma_start(res_d[b][0:RES0, :], res[0].t[:]))
        res[0].free = [m_zero]
        for e in (PE, V, A, Q):
            e.after(m_z)
        res_marks = [m_zero]

        def split_weights(g):
            wh, wl = wts[g % 2]
            for n in range(NW // SC):
                s = wst[n % 2]
                c0_ = n * SC
                src = (wq[g][:, c0_:c0_ + SC] if c0_ < D else wkv[g][:, c0_ - D:c0_ - D + SC] if c0_ < 3 * D
                       else wo[g][:, c0_ - 3 * D:c0_ - 3 * D + SC])
                SP.after(s.free)
                got = s.landed(sp.dma_start(s.t[:], src.rearrange("(k p) n -> p k n", p=P)))
                cs = slice(n * SC, (n + 1) * SC)
                A.after(got, wh.free if n == 0 else None)
                m = A.done(ac.mul(wh.t[:, :, cs], s.t[:], WS))
                V.after(m, wl.free if n == 0 else None)
                for k in range(KD):
                    m = V.done(ve.scalar_tensor_tensor(wl.t[:, k, cs], s.t[:, k, :], WS, wh.t[:, k, cs], ALU.mult, ALU.subtract))
                s.free = [m]
                yield 1
            wl.ready = m
            nk, nv, nl, nb = nkf[g % 2], nvf[g % 2], nkl[g % 2], nvb[g % 2]
            SP.after(nk.free, nv.free)
            m_k = nk.landed(sp.dma_start(nk.t[:], null_k[g], allow_slow_non_contiguous=True))
            m_v = nv.landed(sp.dma_start(nv.t[:, 0:DH], null_v[g]))
            V.after(m_k, m_v, nl.free, nb.free)
            m = V.done(ve.tensor_copy(nl.t[:, 0, :], nk.t[:]))
            V.after(m)
            m = V.done(ve.tensor_tensor(nl.t[:, 1, :], nk.t[:], nl.t[:, 0, :], ALU.subtract))
            nk.free = [m]
            m = V.done(ve.tensor_tensor(nvd[:], nv.t[:].unsqueeze(1).to_broadcast([H, H, DH + 1]),
                                        cst[0:H, C_ID:C_ID + H].unsqueeze(2).to_broadcast([H, H, DH + 1]), ALU.mult))
            nv.free = [m]
            V.after(m)
            m = V.done(ve.tensor_copy(nb.t[0:H], nvd[:]))
            V.after(m)
            V.done(ve.tensor_copy(nb.t[32:32 + H], nvd[:]))
            m = V.done(ve.tensor_tensor(nb.t[64:64 + H], nvd[:], nb.t[0:H], ALU.subtract))
            nb.ready = m
            yield 1

        made = {}

        def route(n):
            g, b = divmod(n, NB)
            si = slot_i[n % 2]
            for kind, r, nt, off in (("q", b * 2 * G + g, QT, 0), ("k", b * 2 * G + G + g, KT, QT)):
                s = rbc[0 if kind == "q" else 1]
                SP.after(s.free)
                got = s.landed(sp.dma_start(s.t[:], rank_d[r].partition_broadcast(P)))
                yield 0.1
                V.after(got)
                for j in range(nt):
                    m = V.done(ve.tensor_scalar(rjunk[:], s.t[:], cst[:, C_J + j:C_J + j + 1], 0.0, ALU.is_le, ALU.add,
                                                accum_out=slot_f[:, off + j:off + j + 1]))
                    V.after(m)
                s.free = [m]
            V.after(si.free)
            m_si = V.done(ve.tensor_scalar(si.t[:], slot_f[:], float(b * L), None, ALU.add))
            yield 0.1
            got = []
            for j in range(QT + KT):
                t = gat[j]
                Q.after(m_si, t.free)
                t.got = t.landed(po.indirect_dma_start(
                    t.t[:], None, rows_d, bass.IndirectOffsetOnAxis(ap=si.t[:, j:j + 1], axis=0)))
                got.append(t.got)
                if j % 2:
                    yield 0.1
            si.free = got

        made = {}

        rows_of = {}

        def turn_rows(n):
            g, u = n // NB, n % 2
            for j in range(QT + KT):
                t = gat[j]
                g16 = t.t[:].bitcast(F16)
                PE.after(t.got)
                if j % 2 == 0:
                    bk = bank("pair")
                b16 = bk.t[:, (j % 2) * 512:(j % 2 + 1) * 512].bitcast(F16)
                for c in range(2 * KD):
                    ins = pe.transpose(b16[:, c * P:(c + 1) * P], g16[:, c * P:(c + 1) * P], id16[:])
                m_t = PE.done(ins)
                V.after(t.got, qscore[u].free if j == 0 else None, kscore.free if j == QT else None)
                if j < QT:
                    m_qs = V.done(ve.tensor_copy(qscore[u].t[:, j:j + 1], t.t[:, D + g:D + g + 1]))
                else:
                    m_qs = V.done(ve.tensor_scalar(kscore.t[:, j - QT:j - QT + 1], t.t[:, D + G + g:D + G + g + 1],
                                                   1.0 / WS, None, ALU.mult))
                t.free = [m_t, m_qs]
                if j % 2 == 0:
                    continue
                dst, s0 = (xq, j - 1) if j < QT else (xk, j - 1 - QT)
                A.after(m_t, dst.free if s0 == 0 else None)
                m_x = A.done(ac.copy(dst.t[:].bitcast(F32)[:, :, s0 * P // 2:(s0 + 2) * P // 2].rearrange("p c (j t) -> p c j t", j=2),
                                     bk.t[:].rearrange("p (j c t) -> p c j t", j=2, c=2 * KD)))
                bk.free = [m_x]
                yield 0.86
            rows_of[n] = (m_x, m_qs)

        def prepare(n):
            g, b = divmod(n, NB)
            u = n % 2
            wh, wl = wts[g % 2]
            m_x, m_qs = rows_of[n]
            PE.after(m_x, wl.ready)
            qa_, ka_, kb_, vh, vl = qa[u], ka[u], kb[u], vhi[u], vlo[u]
            nl = nkl[g % 2]
            ahead = Feed(route(n + 1), 0.5) if n + 1 < G * NB else None
            for e2 in range(KD // 2):
                bk = bank("pair")
                for e in (2 * e2, 2 * e2 + 1):
                    n_ = 0
                    for k in range(KD):
                        ws = slice(e * P, (e + 1) * P)
                        for w, ha in ((wh, 0), (wh, 1), (wl, 0)):
                            ins = pe.matmul(bk.t[:, (e % 2) * NQ:(e % 2 + 1) * NQ], w.t[:, k, ws], xq.t[:, ha * KD + k, :],
                                            start=n_ == 0, stop=n_ == 3 * KD - 1)
                            n_ += 1
                    m = PE.done(ins)
                    if e % 2 == 0:
                        if ahead:
                            ahead.to((e2 + 1) / 4)
                        yield 2.6
                A.after(m, qa_.free if e2 == 0 else None)
                srcs = [bk.t[a * DH:(a + 1) * DH, :].rearrange("p (e t) -> p e t", e=2) for a in range(2)]
                heads = [slice(4 * e2 + a, 4 * e2 + a + 3, 2) for a in range(2)]
                m_a = [A.done(ac.mul(qa_.t[0:DH, hs, :], src, 1.0 / WS)) for src, hs in zip(srcs, heads)]
                V.after(m_a)
                for src, hs in zip(srcs, heads):
                    m_q = V.done(ve.scalar_tensor_tensor(qa_.t[DH:P, hs, :], src, 1.0 / WS, qa_.t[0:DH, hs, :],
                                                         ALU.mult, ALU.subtract))
                bk.free = [m_q]
                yield 2.6
            xq.free = [m]
            bk = bank("pair")
            for e in range(KD):
                n_ = 0
                for k in range(KD):
                    ws = slice(D + e * P, D + (e + 1) * P)
                    for w, ha in ((wh, 0), (wh, 1), (wl, 0)):
                        ins = pe.matmul(bk.t[:, e * NK:(e + 1) * NK], w.t[:, k, ws], xk.t[:, ha * KD + k, :],
                                        start=n_ == 0, stop=n_ == 3 * KD - 1)
                        n_ += 1
                m = PE.done(ins)
                if e % 2:
                    if ahead:
                        ahead.to((e // 2 + 3) / 4)
                    if e < KD - 1:
                        yield 2.6
            A.after(m, ka_.free)
            srcs = [bk.t[a * DH:(a + 1) * DH, :].rearrange("p (e t) -> p e t", e=KD) for a in range(2)]
            for a in range(2):
                m = A.done(ac.mul(ka_.t[0:DH, a::2, 0:NK], srcs[a], 1.0 / WS))
            V.after(m, kb_.free)
            for a in range(2):
                m_kb = V.done(ve.scalar_tensor_tensor(kb_.t[0:DH, a::2, :], srcs[a], 1.0 / WS, ka_.t[0:DH, a::2, 0:NK],
                                                      ALU.mult, ALU.subtract))
            m_k2 = V.done(ve.tensor_copy(ka_.t[DH:P, :, 0:NK], ka_.t[0:DH, :, 0:NK]))
            bk.free = [m_kb]
            yield 2.6
            V.after(ka_.free)
            V.done(ve.tensor_copy(ka_.t[0:DH, :, NK], nl.t[:, 0, :]))
            m_nk = V.done(ve.tensor_copy(ka_.t[DH:P, :, NK], nl.t[:, 0, :]))
            for j in range(KT):
                bk = bank("single")
                n_ = 0
                for k in range(KD):
                    for ha, w in ((0, wh), (0, wl), (1, wh)):
                        ins = pe.matmul(bk.t[:], xk.t[:, ha * KD + k, j * P:(j + 1) * P], w.t[:, k, 2 * D:3 * D],
                                        start=n_ == 0, stop=n_ == 3 * KD - 1)
                        n_ += 1
                m_mm = PE.done(ins)
                src = bk.t[:].rearrange("p (h d) -> p h d", h=H)
                vsc = kscore.t[:, j:j + 1]
                A.after(m_mm, m_qs, vh.free if j == 0 else None)
                m = A.done(ac.activation(vh.t[:, j, :, 0:DH], src, ACT.Copy, scale=vsc))
                V.after(m, vl.free if j == 0 else None)
                m_v = V.done(ve.scalar_tensor_tensor(vl.t[:, j, :, :], src, vsc, vh.t[:, j, :, 0:DH], ALU.mult, ALU.subtract))
                bk.free = [m_v]
                yield 2.6
            kscore.free = [m, m_v]
            xk.free = [m_mm]
            made[n] = (m_q, m_kb, m_k2, m_nk, m_v, m_qs)

        def maxima(n):
            u = n % 2
            qa_, ka_ = qa[u], ka[u]
            nl, qb_ = nkl[n // NB % 2], qb[0]
            PE.after(*made[n])
            V.after(qb_.free, made[n][0])
            V.done(ve.tensor_copy(qb_.t[0:DH], qa_.t[0:DH]))
            for qt in range(QT):
                qs = slice(qt * P, (qt + 1) * P)
                for h2 in range(H // 2):
                    bk = bank("pair")
                    for a in range(2):
                        h = 2 * h2 + a
                        pe.matmul(bk.t[:, a * 512:a * 512 + NK + 1], qa_.t[:, h, qs], ka_.t[:, h, 0:NK + 1], start=True, stop=False,
                                  skip_group_check=True)
                        ins = pe.matmul(bk.t[:, a * 512 + NK:a * 512 + NK + 1], qa_.t[0:DH, h, qs], nl.t[:, 1, h:h + 1],
                                        start=False, stop=True, skip_group_check=True)
                    m = PE.done(ins)
                    sc = bk.t[:].rearrange("p (a t) -> p a t", a=2)
                    V.after(m)
                    m_mx = V.done(ve.tensor_reduce(smx[:, qt, 2 * h2:2 * h2 + 2], sc[:, :, 0:NK + 1], AX.X, ALU.max))
                    m_sn = V.done(ve.tensor_copy(snl[:, qt, 2 * h2:2 * h2 + 2], sc[:, :, NK]))
                    bk.free = [m_sn]
                    yield 0.25
            shift = pnm[:, :, 96:96 + H]
            V.after(m_sn)
            m = V.done(ve.tensor_scalar(shift, smx[:], -1.0 / MS, None, ALU.mult))
            V.after(m)
            m = V.done(ve.scalar_tensor_tensor(pnl[:], shift, MS, snl[:], ALU.mult, ALU.add))
            A.after(m)
            m = A.done(ac.activation(pnl[:], pnl[:], ACT.Exp, scale=SCALE))
            V.after(m)
            m = V.done(ve.tensor_copy(pnm[:, :, 0:H], pnl[:]))
            V.after(m)
            V.done(ve.tensor_copy(pnm[:, :, 64:64 + H], pnl[:]))
            m = V.done(ve.tensor_tensor(pnm[:, :, 32:32 + H], pnl[:], pnm[:, :, 0:H], ALU.subtract))
            yield 1.5
            PE.after(m)
            bk = bank("single")
            b16 = bk.t[:].bitcast(F16)
            for qt in range(QT):
                ins = pe.transpose(b16[0:104, qt * P:(qt + 1) * P], pnm[:, qt, :], id16[:])
            m = PE.done(ins)
            V.after(m)
            m_pT = V.done(ve.tensor_copy(pnT[:], b16[0:104, 0:NQ]))
            bk.free = [m_pT]
            V.after(m_pT)
            m_qb = [V.done(ve.tensor_copy(qb_.t[DH:DH + H, h], pnT[96:96 + H, :])) for h in range(H)]
            turned[n] = (m_qb, m_pT)
            yield 0.2

        turned = {}

        def heads_of(n):
            g, b = divmod(n, NB)
            u = n % 2
            qa_, ka_, kb_, vh, vl = qa[u], ka[u], kb[u], vhi[u], vlo[u]
            nb, qb_ = nvb[g % 2], qb[0]
            m_qb, m_pT = turned[n]

            def scores(h):
                PE.after(m_qb[h])
                bk = bank("pair")
                for j in range(KT):
                    o = bk.t[:, j * NQ:(j + 1) * NQ]
                    pe.matmul(o, ka_.t[:, h, j * P:(j + 1) * P], qa_.t[:, h, :], start=True, stop=False)
                    ins = pe.matmul(o, kb_.t[0:DH + H, h, j * P:(j + 1) * P], qb_.t[0:DH + H, h, :], start=False, stop=True)
                m_s = PE.done(ins)
                f, p_ = pf[h % 2], ph[h % 2]
                A.after(m_s, f.free)
                m = A.done(ac.activation(f.t[:].rearrange("p k q -> p (k q)"), bk.t[:], ACT.Exp, scale=SCALE))
                bk.free = [m]
                A.after(m, p_.free)
                m_h = A.done(ac.copy(p_.t[:, 0], f.t[:]))
                m_l = []
                for j, E, e in ((0, V, ve), (1, Q, po)):
                    E.after(m_h)
                    m_l.append(E.done(e.tensor_tensor(p_.t[:, 1, j], f.t[:, j], p_.t[:, 0, j], ALU.subtract)))
                f.free = m_l
                return m_s, m_l

            def values(h, m_l):
                p_ = ph[h % 2]
                PE.after(m_l, m_pT, nb.ready)
                bk = bank("single")
                for qt in range(QT):
                    qs = slice(qt * P, (qt + 1) * P)
                    o = bk.t[:, qt * (DH + 1):(qt + 1) * (DH + 1)]
                    pe.matmul(o, pnT[0:96, qs], nb.t[:, h, :], start=True, stop=False, skip_group_check=True)
                    for j in range(KT):
                        pe.matmul(o, p_.t[:, 0, j, qs], vh.t[:, j, h, :], start=False, stop=False, skip_group_check=True)
                        pe.matmul(o[:, 0:DH], p_.t[:, 0, j, qs], vl.t[:, j, h, :], start=False, stop=False, skip_group_check=True)
                        ins = pe.matmul(o, p_.t[:, 1, j, qs], vh.t[:, j, h, :], start=False, stop=j == KT - 1, skip_group_check=True)
                m = PE.done(ins)
                p_.free = [m]
                o3 = bk.t[:, 0:QT * (DH + 1)].rearrange("p (q d) -> p q d", q=QT)
                V.after(m)
                m1 = V.done(ve.reciprocal(rden[:, h, :], o3[:, :, DH]))
                V.after(m1)
                m1 = V.done(ve.tensor_tensor(rden[:, h, :], rden[:, h, :], qscore[u].t[:], ALU.mult))
                f = of[h % 2]
                V.after(m1, f.free)
                m1 = V.done(ve.tensor_tensor(f.t[:], o3[:, :, 0:DH], rden[:, h, :].unsqueeze(2).to_broadcast([P, QT, DH]), ALU.mult))
                bk.free = [m1]
                A.after(m1, ohl.free if h == 0 else None)
                m2 = A.done(ac.copy(ohl.t[:, 0, :, h * DH:(h + 1) * DH], f.t[:]))
                Q.after(m2)
                m2 = Q.done(po.tensor_tensor(ohl.t[:, 1, :, h * DH:(h + 1) * DH], f.t[:],
                                             ohl.t[:, 0, :, h * DH:(h + 1) * DH], ALU.subtract))
                f.free = [m2]
                return m, m1, m2

            wait = []
            for h in range(H + 1):
                if h < H:
                    wait.append(scores(h))
                    yield 0.85
                if h >= 1:
                    m_pv, m_on, m_ohl = values(h - 1, wait[h - 1][1])
                    yield 0.76
            m_s = wait[-1][0]
            qa_.free = [m_s]
            qb_.free = [m_s]
            ka_.free = [m_s]
            kb_.free = [m_s]
            vh.free = [m_pv]
            vl.free = [m_pv]
            qscore[u].free = [m_on]
            if b == NB - 1:
                nkl[g % 2].free = [m_pv]
                nvb[g % 2].free = [m_pv]
            ohl.ready = m_ohl

        def finish(n):
            g, b = divmod(n, NB)
            wh, wl = wts[g % 2]
            PE.after(ohl.ready)
            for qt in range(QT + 1):
                if qt < QT:
                    bk = bank("single")
                    b16 = bk.t[:].bitcast(F16)
                    for j in range(2 * KD):
                        ins = pe.transpose(b16[:, j * P:(j + 1) * P], ohl.t[:, j // KD, qt, (j % KD) * P:(j % KD + 1) * P], id16[:])
                    m = PE.done(ins)
                    if qt == QT - 1:
                        ohl.free = [m]
                    o_ = oT[qt % 2]
                    A.after(m, o_.free)
                    o_.ready = A.done(ac.copy(o_.t[:].bitcast(F32).rearrange("p j t -> p (j t)"), bk.t[:]))
                    bk.free = [o_.ready]
                    yield 0.43
                if qt == 0:
                    continue
                qt -= 1
                o_ = oT[qt % 2]
                PE.after(o_.ready)
                bk = bank("single")
                n_ = 0
                for k in range(KD):
                    for ha, w in ((0, wh), (0, wl), (1, wh)):
                        ins = pe.matmul(bk.t[:], o_.t[:, ha * KD + k, :], w.t[:, k, 3 * D:4 * D], start=n_ == 0, stop=n_ == 3 * KD - 1)
                        n_ += 1
                    if k == KD // 2 - 1:
                        yield 1.3
                m = PE.done(ins)
                o_.free = [m]
                r_ = res[qt % 2]
                A.after(m, r_.free)
                m1 = A.done(ac.mul(r_.t[:], bk.t[:], 1.0 / WS))
                bk.free = [m1]
                SP.after(m1)
                r0 = RES0 + g * NQ + qt * P
                m2 = r_.landed(sp.dma_start(res_d[b][r0:r0 + P, :], r_.t[:]))
                r_.free = [m2]
                last[qt % 2] = m2
                yield 1.3
            if b == NB - 1:
                wh.free = [m]
                wl.free = [m]

        last = [m_zero, m_zero]

        def fetch(b, s, c, g, ready=G):
            Q.after(s.free, *last, [w.free for w in wts[G % 2]])
            s.got = s.landed(po.indirect_dma_start(
                s.t, None, res_d[b][0:RES0 + ready * NQ, :], bass.IndirectOffsetOnAxis(ap=idx_tok[:, c, b * 2 * G + g:b * 2 * G + g + 1], axis=0)))

        def load_acc(b, c):
            a_ = accb[c % 2]
            SP.after(a_.free)
            r0 = (b * TPS + c) * P
            a_.got = a_.landed(sp.dma_start(a_.t[:], acc_d[r0:r0 + P, :]))

        def store_out(b, c, total, m):
            a_, o_ = accb[c % 2], stored[c % 2]
            V.after(a_.got, m)
            m = V.done(ve.scalar_tensor_tensor(a_.t[:], total, cnt[:, c, b:b + 1], a_.t[:], ALU.mult, ALU.add))
            SP.after(m)
            r0 = (b * TPS + c) * P
            o_.got = o_.landed(sp.dma_start(out[r0:r0 + P, :], a_.t[:]))
            a_.free = [o_.got]
            return m

        def combine(b):
            for c in range(TPS + 1):
                if c < TPS:
                    for g in range(G):
                        fetch(b, gres[c % 2][g], c, g)
                        if g == 1:
                            yield 1
                    load_acc(b, c)
                if c > 0:
                    s = gres[(c - 1) % 2]
                    a0, a1, a2, a3 = (r.t for r in s)
                    Q.after(s[2].got, s[3].got)
                    m_p = Q.done(po.tensor_tensor(a2, a2, a3, ALU.add))
                    V.after(s[0].got, s[1].got)
                    m = V.done(ve.tensor_tensor(a0, a0, a1, ALU.add))
                    V.after(m, m_p)
                    m = V.done(ve.tensor_tensor(a0, a0, a2, ALU.add))
                    m = store_out(b, c - 1, a0, m)
                    for r in s:
                        r.free = [m]
                yield 1

        def hold(b):
            for c in range(TPS + 1):
                if c < TPS:
                    for g in range(G - 1):
                        fetch(b, gres[c % 2][g], c, g, G - 1)
                        yield 1
                if c > 0:
                    s = gres[(c - 1) % 2]
                    V.after([r.got for r in s[:G - 1]])
                    m = V.done(ve.tensor_tensor(held[c - 1], s[0].t, s[1].t, ALU.add))
                    V.after(m)
                    m = V.done(ve.tensor_tensor(held[c - 1], held[c - 1], s[2].t, ALU.add))
                    for r in s[:G - 1]:
                        r.free = [m]

        def combine_held(b):
            rows = [gres[c // G][c % G] for c in range(TPS)]
            for c in range(TPS):
                fetch(b, rows[c], c, G - 1)
            for c in range(TPS):
                load_acc(b, c)
                V.after(rows[c].got)
                m = V.done(ve.tensor_tensor(held[c], held[c], rows[c].t, ALU.add))
                rows[c].free = [store_out(b, c, held[c], m)]

        items = G * NB
        for gen in (split_weights(0), route(0), turn_rows(0), prepare(0), turn_rows(1), maxima(0)):
            Feed(gen, 1).to(1)
        for n in range(items):
            work = []
            if n % NB == 2 and n // NB + 1 < G:
                work.append(Feed(split_weights(n // NB + 1), NW // SC + 1))
            if n + 1 < items:
                work.append(Feed(prepare(n + 1), 20.8))
            merge = []
            if n // NB == G - 1:
                merge.append(Feed(combine(n % NB - 1) if n % NB else hold(NB - 1), 2 * TPS + 1 if n % NB else (G - 1) * TPS))
            weave(Feed(heads_of(n), 12.9), *work, *[Part(f, 0.6) for f in merge])
            beside = list(merge)
            if n + 2 < items:
                beside.append(Feed(turn_rows(n + 2), 3 * 0.86))
            if n + 1 < items:
                beside.append(Feed(maxima(n + 1), 5.7 * 1.3))
            for f in beside[len(merge):]:
                f.to(0.1)
            weave(Feed(finish(n), 12.1), *beside)
        combine_held(NB - 1)
        SP.after(*[o.got for o in stored], *last)


def kernel(L0_attn_x, L0_attn_ln_w, L0_attn_ln_b, L0_attn_in_proj_w, L0_attn_conv_w, L0_attn_conv_b,
           L0_attn_A_log, L0_attn_D, L0_attn_dt_bias, L0_attn_gamma, L0_attn_out_proj_w, L0_ffn_w_qr,
           L0_ffn_w_kvr, L0_ffn_w_q, L0_ffn_w_kv, L0_ffn_w_out, L0_ffn_null_kv, L0_ffn_null_token):
    import numpy as np
    import concourse.bacc as bacc
    from concourse.bass_utils import run_bass_kernel_spmd

    c = np.zeros((P, C_N), np.float32)
    c[:, C_ID:C_ID + P] = np.eye(P)
    c[:, C_U:C_U + P] = np.triu(np.ones((P, P)))
    for j in range(QT):
        c[:, C_J + j] = j * P + np.arange(P)
    for r in range(NR):
        b, j = divmod(r, 2 * G)
        c[r, C_K] = NQ if j < G else NK
        c[r, C_BASE] = RES0 + j * NQ - 1 if j < G else 0.0
    a = np.asarray
    arrays = {
        "x": a(L0_attn_x).reshape(T, D),
        "w_in": a(L0_attn_in_proj_w).T,
        "ln_w": a(L0_attn_ln_w),
        "ln_b": a(L0_attn_ln_b),
        "conv_w": a(L0_attn_conv_w),
        "conv_b": a(L0_attn_conv_b),
        "a_log": a(L0_attn_A_log),
        "d_skip": a(L0_attn_D),
        "dt_bias": a(L0_attn_dt_bias),
        "gamma": a(L0_attn_gamma),
        "w_out": a(L0_attn_out_proj_w).T,
        "w_route": np.concatenate([a(L0_ffn_w_qr), a(L0_ffn_w_kvr)], 0).T,
        "wq": a(L0_ffn_w_q).transpose(0, 2, 1),
        "wkv": a(L0_ffn_w_kv).transpose(0, 2, 1),
        "wo": a(L0_ffn_w_out).transpose(0, 2, 1),
        "null_k": a(L0_ffn_null_kv)[0, :, :, 0, :].transpose(0, 2, 1),
        "null_v": a(L0_ffn_null_kv)[1, :, :, 0, :],
        "null_tok": a(L0_ffn_null_token).reshape(D),
        "consts": c,
    }
    nc = bacc.Bacc("TRN2", target_bir_lowering=False, num_devices=1)
    feeds, args = {}, []
    for name, v in arrays.items():
        v = np.ascontiguousarray(v)
        feeds[name] = v
        args.append(nc.dram_tensor(name, v.shape, mybir.dt.from_np(v.dtype), kind="ExternalInput").ap())
    out = nc.dram_tensor("y", (T, D), F32, kind="ExternalOutput").ap()
    program(nc, *args, out)
    r = run_bass_kernel_spmd(nc, [feeds], core_ids=[0])
    return r.results[0]["y"].reshape(NB, L, D)
```

```python
from contextlib import ExitStack
from itertools import count

import concourse.bass as bass
from concourse import mybir
from concourse.alu_op_type import AluOpType as ALU

ACT = mybir.ActivationFunctionType
AX = mybir.AxisListType
F32 = mybir.dt.float32
F16 = mybir.dt.float16
I32 = mybir.dt.int32

P = 128
NB, L, D = 8, 1024, 512
T = NB * L
KD = D // P
DI, NS, NH, HD = 1024, 128, 16, 64
CH = DI + 2 * NS
NCT = CH // P
KI = DI // P
TAPS = 4
BLK = 512
CK = BLK // P
NBLK = T // BLK
WC = DI + CH
G, NQ, NK, H, DH = 4, 512, 256, 8, 64
QT, KT = NQ // P, NK // P
NR = NB * 2 * G
NT = T // P
TPS = L // P
ROW = D + 2 * G
EPS = 1e-5
WS = 64.0
MS = 16.0
RES0 = P
LAG = 2

C_ID, C_U, C_J, C_K, C_BASE = 0, P, 2 * P, 2 * P + QT, 2 * P + QT + 1
C_N = C_BASE + 1


keys = count()


class Engine:

    def __init__(self, eng, sem):
        self.eng, self.sem, self.n, self.seen, self.key = eng, sem, 0, {}, next(keys)

    def after(self, *marks):
        for m in marks:
            if m is None:
                continue
            if type(m) is list:
                self.after(*m)
                continue
            name, sem, value = m
            if self.seen.get(name, 0) < value:
                self.eng.wait_ge(sem, value)
                self.seen[name] = value

    def done(self, ins):
        self.n += 1
        ins.then_inc(self.sem, 1)
        return (self.key, self.sem, self.n)


class Slot:

    given_back = 0

    def __init__(self, t, sem=None):
        self.t, self.free, self.sem, self.n, self.key = t, [], sem, 0, next(keys)

    @property
    def free(self):
        return self._free

    @free.setter
    def free(self, marks):
        self._free = marks
        Slot.given_back += 1
        self.since = Slot.given_back

    def landed(self, dma):
        self.n += 16
        dma.then_inc(self.sem, 16)
        return (self.key, self.sem, self.n)


class Feed:

    def __init__(self, gen, total):
        self.gen, self.total, self.spent, self.live = gen, total, 0.0, True

    def to(self, share):
        while self.live and (share >= 1 or self.spent < share * self.total):
            try:
                self.spent += next(self.gen)
            except StopIteration:
                self.live = False


class Part:

    def __init__(self, feed, start, end):
        self.feed, self.start, self.end = feed, start, end

    def to(self, share):
        self.feed.to(self.start + min(share, 1) * (self.end - self.start))


def chain(*gens):
    for g in gens:
        yield from g


def weave(main, *feeds):
    while main.live:
        main.to(main.spent / main.total + 1e-6)
        for f in feeds:
            f.to(min(main.spent / main.total, 0.999))
    for f in feeds:
        f.to(1)


def program(nc, x, w_in, ln_w, ln_b, conv_w, conv_b, a_log, d_skip, dt_bias, gamma, w_out,
            w_route, wq, wkv, wo, null_k, null_v, null_tok, consts, out):
    ctx = ExitStack()
    with ctx:
        def sem(name):
            return ctx.enter_context(nc.semaphore(name))

        PE = Engine(nc.tensor, sem("pe_done"))
        V = Engine(nc.vector, sem("dve_done"))
        A = Engine(nc.scalar, sem("act_done"))
        Q = Engine(nc.gpsimd, sem("pool_done"))
        SP = Engine(nc.sync, sem("sp_done"))
        pe, ve, ac, po, sp = nc.tensor, nc.vector, nc.scalar, nc.gpsimd, nc.sync

        def scratch(name, shape, dt):
            return nc.dram_tensor(name, shape, dt, kind="Internal").ap()

        rows_d = scratch("rows", (T, ROW), F32)
        skip_d = scratch("skip", (T, D), F32)
        acc_d = scratch("acc", (T, D), F32)
        cum_d = scratch("cum", (NBLK, NH, BLK), F32)
        rank_d = scratch("rank", (NR, L), F16)
        res_d = [scratch(f"results{b}", (RES0 + G * NQ, D), F32) for b in range(NB)]

        pairs = [Slot(ctx.enter_context(nc.psum_tensor(f"pair{i}", [P, 1024], F32))) for i in range(2)]
        singles = [Slot(ctx.enter_context(nc.psum_tensor(f"bank{i}", [P, 512], F32))) for i in range(4)]
        pools = {"pair": pairs, "single": singles}

        def bank(kind):
            s = min((s for s in pools[kind] if s.free is not None), key=lambda s: s.since)
            PE.after(s.free)
            s.free = None
            return s

        def sb(stack, name, shape, dt):
            return stack.enter_context(nc.sbuf_tensor(name, shape, dt))

        cst = sb(ctx, "cst", [P, C_N], F32)
        id16 = sb(ctx, "id16", [P, P], F16)
        neghalf = sb(ctx, "neghalf", [P, CK], F32)
        logit = sb(ctx, "logit", [P, TPS, NB, 2 * G], F32)
        load_const, load_small, load_wout, load_null = (Slot(None, sem(f"s_load{i}")) for i in range(4))
        id32 = cst[:, C_ID:C_ID + P]
        upper = cst[:, C_U:C_U + P]

        c1 = load_const.landed(sp.dma_start(cst[:], consts))
        A.after(c1)
        m_id16 = A.done(ac.copy(id16[:], id32))
        m_half = V.done(ve.memset(neghalf[:], -0.5))
        V.after(c1)
        PE.after(c1, m_id16)
        Q.after(c1, m_half)

        mam = ExitStack()
        with mam:
            whi = sb(mam, "whi", [P, KD, WC], F16)
            wlo = sb(mam, "wlo", [P, KD, WC], F16)
            shi = sb(mam, "shi", [P, KD, 2 * G + NH], F16)
            slo = sb(mam, "slo", [P, KD, 2 * G + NH], F16)
            ohi = sb(mam, "ohi", [P, KI, D], F16)
            olo = sb(mam, "olo", [P, KI, D], F16)
            z_bias = sb(mam, "z_bias", [33, DI], F16)
            ones = sb(mam, "ones", [33, P], F16)
            dt_b = sb(mam, "dt_b", [P, NH], F32)
            a_neg = sb(mam, "a_neg", [P, NH], F32)
            d_bc = sb(mam, "d_bc", [P, NH], F32)
            raw_bias = sb(mam, "raw_bias", [P, NCT], F32)
            taps = sb(mam, "taps", [P, NCT, TAPS], F32)
            conv_bias = sb(mam, "conv_bias", [P, NCT], F32)

            s_x = [sem(f"s_x{i}") for i in range(1)]
            xin = [Slot(sb(mam, "xin", [P, CK, D], F32), s_x[0])]
            xn = [Slot(sb(mam, f"xn{i}", [P, D], F32)) for i in range(1)]
            rowt = Slot(sb(mam, "rowt", [P, CK, ROW], F32), sem("s_row"))
            row16 = rowt.t[:].bitcast(F16)
            xh = [Slot(sb(mam, f"xh{i}", [P, 2, D], F16)) for i in range(1)]
            xhT = [Slot(sb(mam, f"xhT{i}", [P, 2, KD, BLK], F16)) for i in range(2)]
            s_skip = sem("s_skip")
            stats = sb(mam, "stats", [P, CK, 6], F32)
            mv = sb(mam, "mv", [P, CK, 2], F32)
            nrm = sb(mam, "nrm", [P, 6, CK], F32)
            skip_w = Slot(None, s_skip)
            skip_marks = {}
            cum_marks = {}
            nrm_of = {}
            row_marks = []
            front_out = {}
            acc_marks = []

            def statistics(i):
                xi = xin[0]
                SP.after(xi.free)
                got = xi.landed(sp.dma_start(xi.t[:], x[i * BLK:(i + 1) * BLK, :].rearrange("(c p) d -> p c d", p=P)))
                V.after(got)
                for c in range(CK):
                    m = V.done(ve.bn_stats(stats[:, c, :], xi.t[:, c, :]))
                V.after(m)
                for c in range(CK):
                    m = V.done(ve.bn_aggr(mv[:, c, :], stats[:, c, :]))
                V.after(m)
                var, mean = mv[:, :, 1], mv[:, :, 0]
                r1, r2, q2, t0, v2 = (nrm[:, j, :] for j in range(5))
                m = V.done(ve.tensor_scalar(t0, var, EPS, None, ALU.add))
                Q.after(m)
                m = Q.done(po.tensor_tensor(r1, t0, neghalf[:], ALU.pow))
                yield 2.0
                V.after(m)
                m = V.done(ve.tensor_tensor(v2, var, r1, ALU.mult))
                V.after(m)
                m = V.done(ve.tensor_tensor(v2, v2, r1, ALU.mult))
                V.after(m)
                m = V.done(ve.tensor_scalar(v2, v2, EPS, None, ALU.add))
                Q.after(m)
                m = Q.done(po.tensor_tensor(r2, v2, neghalf[:], ALU.pow))
                yield 2.0
                V.after(m)
                m_q2 = V.done(ve.tensor_tensor(q2, v2, r2, ALU.mult))
                nrm_of[i] = m_q2

            def front(i):
                b, half = divmod(i, L // BLK)
                u = i % 2
                xi = xin[0]
                mean = mv[:, :, 0]
                r1, r2, q2 = (nrm[:, j, :] for j in range(3))
                A.after(nrm_of[i])
                xt = xhT[u]
                for c in range(CK):
                    n_, h_ = xn[0], xh[0]
                    V.after(n_.free)
                    m_xn = V.done(ve.tensor_scalar(n_.t[:], xi.t[:, c, :], mean[:, c:c + 1], r1[:, c:c + 1],
                                                   ALU.subtract, ALU.mult))
                    A.after(m_xn, rowt.free if c == 0 else None, h_.free)
                    hi, lo = row16[:, c, 0:D], row16[:, c, D:2 * D]
                    m_hi = A.done(ac.copy(hi, n_.t[:]))
                    m_xh = A.done(ac.activation(h_.t[:, 0, :], n_.t[:], ACT.Copy, scale=r2[:, c:c + 1]))
                    Q.after(m_hi)
                    m_lo = Q.done(po.tensor_tensor(lo, n_.t[:], hi, ALU.subtract))
                    m_sk = Q.done(po.tensor_tensor(xi.t[:, c, :], xi.t[:, c, :], n_.t[:], ALU.add))
                    yield 1.2
                    V.after(m_xh)
                    m_xl = V.done(ve.scalar_tensor_tensor(h_.t[:, 1, :], n_.t[:], r2[:, c:c + 1], h_.t[:, 0, :],
                                                          ALU.mult, ALU.subtract))
                    n_.free = [m_xh, m_xl, m_sk]
                    yield 1.2
                    PE.after(m_xl)
                    bk = bank("single")
                    b16 = bk.t[:].bitcast(F16)
                    for j in range(2 * KD):
                        ins = pe.transpose(b16[:, j * P:(j + 1) * P], h_.t[:, j // KD, (j % KD) * P:(j % KD + 1) * P], id16[:])
                    m_t = PE.done(ins)
                    h_.free = [m_t]
                    A.after(m_t, xt.free if c == 0 else None)
                    m_e = A.done(ac.copy(xt.t[:].bitcast(F32)[:, :, :, c * P // 2:(c + 1) * P // 2].rearrange("p h k t -> p (h k) t"),
                                         bk.t[:].rearrange("p (j t) -> p j t", j=2 * KD)))
                    bk.free = [m_e]
                    yield 0.9 if c < CK - 1 else 2.5
                m_xhT = m_e
                SP.after(m_sk)
                skip_marks[i] = skip_w.landed(sp.dma_start(
                    skip_d[i * BLK:(i + 1) * BLK, :].rearrange("(c p) d -> p c d", p=P), xi.t[:]))
                xi.free = [skip_marks[i]]
                PE.after(m_xhT)
                bk = bank("single")
                NW = 2 * G + NH
                for c in range(CK):
                    cs = slice(c * P, (c + 1) * P)
                    n = 0
                    for k in range(KD):
                        for ha, w in ((0, shi), (0, slo), (1, shi)):
                            ins = pe.matmul(bk.t[:, c * NW:(c + 1) * NW], xt.t[:, ha, k, cs], w[:, k, :],
                                            start=n == 0, stop=n == 3 * KD - 1)
                            n += 1
                m = PE.done(ins)
                V.after(m)
                sm = bk.t[:, 0:CK * NW].rearrange("p (c n) -> p c n", c=CK)
                for c in range(CK):
                    m_lg = V.done(ve.tensor_scalar(logit[:, half * CK + c, b, :], sm[:, c, 0:2 * G], q2[:, c:c + 1],
                                                   1.0 / WS, ALU.mult, ALU.mult))
                xr, ex, sq, s2, pl = (dts[:, j, :].rearrange("p (c h) -> p c h", c=CK) for j in range(5))
                m = V.done(ve.scalar_tensor_tensor(xr, sm[:, :, 2 * G:], 1.0 / WS,
                                                   dt_b[:].unsqueeze(1).to_broadcast([P, CK, NH]), ALU.mult, ALU.add))
                bk.free = [m_lg, m]
                V.after(m)
                yield 1.3
                A.after(m_lg)
                sc = rowt.t[:, :, D:ROW]
                m_s = A.done(ac.activation(sc, logit[:, half * CK:(half + 1) * CK, b, :], ACT.Tanh, scale=0.5))
                V.after(m_s)
                m_s = V.done(ve.tensor_scalar(sc, sc, 0.5, 0.5, ALU.mult, ALU.add))
                SP.after(m_s, m_lo)
                m_row = rowt.landed(sp.dma_start(rows_d[i * BLK:(i + 1) * BLK, :].rearrange("(c p) d -> p c d", p=P), rowt.t[:]))
                rowt.free = [m_row]
                row_marks.append(m_row)
                m = V.done(ve.scalar_tensor_tensor(ex, xr, -1.0, xr, ALU.mult, ALU.max))
                A.after(m)
                m = A.done(ac.activation(ex, ex, ACT.Exp, scale=-1.0))
                V.after(m)
                m = V.done(ve.tensor_scalar(sq, ex, 2.0, None, ALU.add))
                V.after(m)
                m = V.done(ve.reciprocal(sq, sq))
                V.after(m)
                m = V.done(ve.tensor_tensor(sq, sq, ex, ALU.mult))
                V.after(m)
                m = V.done(ve.tensor_tensor(s2, sq, sq, ALU.mult))
                V.after(m)
                m = V.done(ve.tensor_scalar(pl, s2, 2.0 / 17, None, ALU.mult))
                for j in range(15, 1, -2):
                    V.after(m)
                    m = V.done(ve.scalar_tensor_tensor(pl, pl, 2.0 / j, s2, ALU.add, ALU.mult))
                V.after(m)
                m = V.done(ve.scalar_tensor_tensor(pl, pl, 2.0, sq, ALU.add, ALU.mult))
                V.after(m, dt_t[u].free)
                dt = dt_t[u].t
                m_dt = V.done(ve.scalar_tensor_tensor(dt[:], xr, 0.0, pl, ALU.max, ALU.add))
                V.after(m_dt)
                m_a = V.done(ve.tensor_tensor(xr, dt[:], a_neg[:].unsqueeze(1).to_broadcast([P, CK, NH]), ALU.mult))
                if half == 0:
                    if i > 0:
                        V.after(front_out[i - 1][4])
                    m_halo = V.done(ve.memset(halo[:], 0.0))
                xs = xsT[u]

                def silu(ct, c_):
                    A.after(c_.ready, xs.free if ct == 0 else None)
                    m_th = A.done(ac.activation(xs.t[:, ct, :], c_.t[:], ACT.Tanh))
                    V.after(m_th)
                    m_xs = V.done(ve.scalar_tensor_tensor(xs.t[:, ct, :], xs.t[:, ct, :], 1.0, c_.t[:], ALU.add, ALU.mult))
                    c_.free = [m_xs]
                    return m_xs

                for pr in range(NCT // 2):
                    for j in range(2):
                        bk = bank("single")
                        ct = 2 * pr + j
                        n = 0
                        for k in range(KD):
                            ws = slice(DI + ct * P, DI + (ct + 1) * P)
                            for ha, w in ((0, whi), (1, whi), (0, wlo)):
                                ins = pe.matmul(bk.t[:], w[:, k, ws], xt.t[:, ha, k, :],
                                                start=n == 0, stop=n == 3 * KD - 1)
                                n += 1
                        m_mm = PE.done(ins)
                        r_, c_ = raw[j], cv[j]
                        A.after(m_mm, r_.free)
                        m_r = A.done(ac.activation(r_.t[:, TAPS - 1:], bk.t[:], ACT.Identity,
                                                   bias=raw_bias[:, ct:ct + 1], scale=1.0 / WS))
                        bk.free = [m_r]
                        if half == 0 and ct == 0:
                            A.after(m_halo)
                        m = A.done(ac.copy(r_.t[:, 0:TAPS - 1], halo[:, ct, :]))
                        A.after(m, m_r)
                        m_h = A.done(ac.copy(halo[:, ct, :], r_.t[:, BLK:]))
                        A.after(c_.free)
                        m = A.done(ac.activation(c_.t[:], r_.t[:, 0:BLK], ACT.Identity, bias=conv_bias[:, ct:ct + 1],
                                                 scale=taps[:, ct, 0:1]))
                        for t in range(1, TAPS):
                            V.after(m, m_h)
                            m = V.done(ve.scalar_tensor_tensor(c_.t[:], r_.t[:, t:t + BLK], taps[:, ct, t:t + 1], c_.t[:],
                                                               ALU.mult, ALU.add))
                        r_.free = [m, m_h]
                        c_.ready = m
                        if ct > 0:
                            m_xs = silu(*tile)
                        tile = (ct, c_)
                        yield 2.6
                    if pr == 0:
                        PE.after(m_a)
                        bk = bank("single")
                        for c in range(CK):
                            ins = pe.matmul(bk.t[:, c * NH:(c + 1) * NH], upper, xr[:, c, :], start=True, stop=True)
                        m = PE.done(ins)
                        V.after(m, cum_t[u].free)
                        A.after(m, ecum[u].free)
                        m_cum = V.done(ve.tensor_copy(cum_t[u].t[:], bk.t[:, 0:CK * NH].rearrange("p (c h) -> p c h", c=CK)))
                        A.after(m_cum)
                        m_ec = A.done(ac.activation(ecum[u].t[:], cum_t[u].t[:], ACT.Exp))
                        bk.free = [m_cum]
                        bk = bank("single")
                        for c in range(CK):
                            ins = pe.matmul(bk.t[0:NH, c * P:(c + 1) * P], xr[:, c, :], upper, start=True, stop=True)
                        m = PE.done(ins)
                        A.after(m, cumT.free)
                        m = A.done(ac.copy(cumT.t[:], bk.t[0:NH, :]))
                        bk.free = [m]
                        SP.after(m)
                        cum_marks[i] = cumT.landed(sp.dma_start(cum_d[i], cumT.t[:]))
                        cumT.free = [cum_marks[i]]
                m_xs = silu(*tile)
                front_out[i] = (m_xs, m_dt, m_cum, m_ec, m_h)
                if i + 1 < NBLK:
                    yield from statistics(i + 1)

            norm_of, yT_of, yn_m = {}, {}, [None]

            def load_decay(ch):
                i, c = divmod(ch, CK)
                SP.after(bc.free, cum_marks[i])
                bc.chunk = ch
                bc.got = bc.landed(sp.dma_start(bc.t[:], cum_d[i][:, c * P:(c + 1) * P].partition_broadcast(P)))

            def load_skip(ch):
                sk = skipb[ch % 2]
                SP.after(sk.free, skip_marks[ch // CK])
                sk.got = sk.landed(sp.dma_start(sk.t[:], skip_d[ch * P:(ch + 1) * P, :]))

            def differences(ch):
                i, c = divmod(ch, CK)
                Q.after(bc.got, front_out[i][2] if i in front_out else None, de.free)
                de.chunk = ch
                de.got = Q.done(po.tensor_tensor(de.t[:], cum_t[i % 2].t[:, c, :].unsqueeze(2).to_broadcast([P, NH, P]),
                                                 bc.t[:], ALU.subtract))

            def square(ch):
                yf, m_y = norm_of[ch]
                A.after(m_y, yhl.free)
                yn_m[0] = A.done(ac.activation(yhl.t[:, 0, :], yf, ACT.Square, accum_out=yn[:, 0:1]))

            def root(ch):
                V.after(yn_m[0])
                m = V.done(ve.tensor_scalar(yn[:, 1:2], yn[:, 0:1], 1.0 / DI, EPS, ALU.mult, ALU.add))
                Q.after(m)
                yn_m[0] = Q.done(po.tensor_tensor(yn[:, 2:3], yn[:, 1:2], neghalf[:, 0:1], ALU.pow))

            def split_high(ch):
                A.after(yn_m[0])
                yn_m[0] = A.done(ac.activation(yhl.t[:, 0, :], norm_of[ch][0], ACT.Copy, scale=yn[:, 2:3]))

            def split_low(ch):
                V.after(yn_m[0])
                m_l = V.done(ve.scalar_tensor_tensor(yhl.t[:, 1, :], norm_of[ch][0], yn[:, 2:3], yhl.t[:, 0, :],
                                                     ALU.mult, ALU.subtract))
                yb.free = [yn_m[0], m_l]
                norm_of[ch] = m_l

            def turn_y(ch):
                PE.after(norm_of[ch])
                pt = bank("pair")
                pt16 = pt.t[:].bitcast(F16)
                for j in range(2 * KI):
                    ins = pe.transpose(pt16[:, j * P:(j + 1) * P], yhl.t[:, j // KI, (j % KI) * P:(j % KI + 1) * P], id16[:])
                m_t = PE.done(ins)
                yhl.free = [m_t]
                A.after(m_t, yT.free)
                m_yT = A.done(ac.copy(yT.t[:].bitcast(F32).rearrange("p j t -> p (j t)"), pt.t[:]))
                pt.free = [m_yT]
                yT_of[ch] = m_yT

            def project(ch):
                PE.after(yT_of[ch])
                bk = bank("single")
                n = 0
                for k in range(KI):
                    for ha, w in ((0, ohi), (0, olo), (1, ohi)):
                        ins = pe.matmul(bk.t[:], yT.t[:, ha * KI + k, :], w[:, k, :], start=n == 0, stop=n == 3 * KI - 1)
                        n += 1
                    if k == KI // 2 - 1:
                        yield 2.6
                m_o = PE.done(ins)
                yT.free = [m_o]
                sk = skipb[ch % 2]
                V.after(m_o, sk.got)
                m_s = V.done(ve.scalar_tensor_tensor(sk.t[:], bk.t[:], 1.0 / WS, sk.t[:], ALU.mult, ALU.add))
                bk.free = [m_s]
                SP.after(m_s)
                m_a = accw[ch % 2].landed(sp.dma_start(acc_d[ch * P:(ch + 1) * P, :], sk.t[:]))
                sk.free = [m_a]
                acc_marks.append(m_a)

            def back(i):
                b, half = divmod(i, L // BLK)
                u = i % 2
                m_xs, m_dt, m_cum, m_ec, _ = front_out[i]
                xs, xt = xsT[u], xhT[u]
                dt, cum, ec = dt_t[u].t, cum_t[u].t, ecum[u].t
                for c in range(CK):
                    ch = i * CK + c
                    cs = slice(c * P, (c + 1) * P)
                    old, new = state[ch % 2], state[(ch + 1) % 2]
                    if bc.chunk != ch:
                        load_decay(ch)
                    if ch == 0:
                        load_skip(ch)
                    m_bc = bc.got
                    if half == 0 and c == 0:
                        V.after(old.free)
                        old.ready = V.done(ve.memset(old.t[:], 0.0))
                    m_old = old.ready
                    PE.after(m_xs)
                    px = bank("pair")
                    for k in range(KI):
                        ins = pe.transpose(px.t[:, k * P:(k + 1) * P], xs.t[:, k, cs], id32)
                    m_px = PE.done(ins)
                    bk = bank("single")
                    pe.transpose(bk.t[:, 0:P], xs.t[:, KI, cs], id32)
                    m_g = PE.done(pe.matmul(bk.t[:, P:2 * P], xs.t[:, KI, cs], xs.t[:, KI + 1, cs], start=True, stop=True))
                    if de.chunk != ch:
                        differences(ch)
                    m = de.got
                    V.after(m_bc, m_cum, decs.free)
                    m_d1 = V.done(ve.tensor_tensor(decs.t[:, 0, :], bc.t[:, :, P - 1], cum[:, c, :], ALU.subtract))
                    A.after(m_d1, m_bc)
                    m_dec = A.done(ac.activation(decs.t[:, 1, :], decs.t[:, 0, :], ACT.Exp))
                    m_cd = A.done(ac.activation(decs.t[:, 2, :], bc.t[:, :, P - 1], ACT.Exp))
                    A.after(m_g, btok.free)
                    m_bt = A.done(ac.copy(btok.t[:], bk.t[:, 0:P]))
                    bc.free = [m, m_d1, m_cd]
                    V.after(m_px, m_dt, xdt.free)
                    p3 = px.t[:].rearrange("p (h d) -> p h d", h=NH)
                    m_xdt = V.done(ve.tensor_tensor(xdt.t[:], p3, dt[:, c, :].unsqueeze(2).to_broadcast([P, NH, HD]), ALU.mult))
                    V.after(dxs.free)
                    m_dxs = V.done(ve.tensor_tensor(dxs.t[:], p3, d_bc[:].unsqueeze(2).to_broadcast([P, NH, HD]), ALU.mult))
                    px.free = [m_dxs]
                    V.after(m_g, m_bt, gmask.free)
                    m_gm = V.done(ve.tensor_tensor(gmask.t[:], bk.t[:, P:2 * P], upper, ALU.mult))
                    bk.free = [m_gm]
                    if ch + 1 < NBLK * CK and (c < CK - 1 or i + 1 in cum_marks):
                        load_decay(ch + 1)
                    Q.after(m_xdt, m_dec, xw.free)
                    m_xw = Q.done(po.tensor_tensor(xw.t[:], xdt.t[:], decs.t[:, 1, :].unsqueeze(2).to_broadcast([P, NH, HD]), ALU.mult))
                    Q.after(m_cd, m_old, new.free)
                    m_sd = Q.done(po.tensor_tensor(new.t[:], old.t[:], decs.t[:, 2, :].unsqueeze(2).to_broadcast([P, NH, HD]), ALU.mult))
                    decs.free = [m_sd]
                    yield 1.2
                    if ch > 0:
                        split_high(ch - 1)
                    for j in range(2):
                        pz = bank("single")
                        n = 0
                        for k in range(KD):
                            for ha, w in ((0, whi), (0, wlo), (1, whi)):
                                pe.matmul(pz.t[:], xt.t[:, ha, k, cs], w[:, k, j * 512:(j + 1) * 512],
                                          start=n == 0, stop=False)
                                n += 1
                        m_z = PE.done(pe.matmul(pz.t[:], ones[:], z_bias[:, j * 512:(j + 1) * 512], start=False, stop=True))
                        if j == 0 and ch > 0:
                            split_low(ch - 1)
                        zj = zs.t[:, j * 512:(j + 1) * 512]
                        A.after(m_z, zs.free if j == 0 else None)
                        m_zt = A.done(ac.activation(zj, pz.t[:], ACT.Tanh, scale=0.5 / WS))
                        if j == 0:
                            A.after(de.got)
                            m_e = A.done(ac.activation(de.t[:], de.t[:], ACT.Relu))
                        yield 2.8
                        V.after(m_zt)
                        m_sz = V.done(ve.scalar_tensor_tensor(zj, zj, 1.0, pz.t[:], ALU.add, ALU.mult))
                        pz.free = [m_sz]
                    if ch > 0:
                        turn_y(ch - 1)
                    A.after(m_e)
                    m_e = A.done(ac.activation(de.t[:], de.t[:], ACT.Exp, scale=-1.0))
                    yield 0.9
                    PE.after(m_old)
                    pi = bank("pair")
                    sf = old.t[:].rearrange("p h d -> p (h d)")
                    for j in range(2):
                        ins = pe.matmul(pi.t[:, j * 512:(j + 1) * 512], xs.t[:, KI + 1, cs], sf[:, j * 512:(j + 1) * 512], start=True, stop=True)
                    m_i = PE.done(ins)
                    V.after(m_i, m_ec, yb.free)
                    m_y = V.done(ve.tensor_tensor(yb.t[:], pi.t[:].rearrange("p (h d) -> p h d", h=NH),
                                                  ec[:, c, :].unsqueeze(2).to_broadcast([P, NH, HD]), ALU.mult))
                    pi.free = [m_y]
                    Q.after(m_y, m_dxs)
                    m_y = Q.done(po.tensor_tensor(yb.t[:], yb.t[:], dxs.t[:], ALU.add))
                    dxs.free = [m_y]
                    yield 1.7
                    PE.after(m_bt, m_xw)
                    pn = bank("pair")
                    xf = xw.t[:].rearrange("p h d -> p (h d)")
                    for j in range(2):
                        ins = pe.matmul(pn.t[:, j * 512:(j + 1) * 512], btok.t[:], xf[:, j * 512:(j + 1) * 512], start=True, stop=True)
                    m_n = PE.done(ins)
                    btok.free = [m_n]
                    xw.free = [m_n]
                    V.after(m_n, m_sd)
                    m_new = V.done(ve.tensor_tensor(new.t[:], new.t[:], pn.t[:].rearrange("p (h d) -> p h d", h=NH), ALU.add))
                    pn.free = [m_new]
                    new.ready = m_new
                    old.free = [m_i, m_sd]
                    V.after(m_e, m_gm)
                    m_m = V.done(ve.tensor_tensor(de.t[:], de.t[:], gmask.t[:].unsqueeze(1).to_broadcast([P, NH, P]), ALU.mult))
                    gmask.free = [m_m]
                    yield 1.7
                    if ch > 0:
                        yield from project(ch - 1)
                    if ch + 1 < NBLK * CK:
                        load_skip(ch + 1)
                    yield 2.6
                    PE.after(m_m, m_xdt)
                    pw = bank("pair")
                    for h in range(NH):
                        ins = pe.matmul(pw.t[:, h * HD:(h + 1) * HD], de.t[:, h, :], xdt.t[:, h, :], start=True, stop=True)
                    m_w = PE.done(ins)
                    de.free = [m_w]
                    xdt.free = [m_w, m_xw]
                    V.after(m_w, m_y)
                    m_y = V.done(ve.tensor_tensor(yb.t[:], yb.t[:], pw.t[:].rearrange("p (h d) -> p h d", h=NH), ALU.add))
                    pw.free = [m_y]
                    yf = yb.t[:].rearrange("p h d -> p (h d)")
                    V.after(m_y, m_sz)
                    m_y = V.done(ve.scalar_tensor_tensor(yf, yf, 0.5 / WS, zs.t[:], ALU.mult, ALU.mult))
                    zs.free = [m_y]
                    norm_of[ch] = (yf, m_y)
                    if bc.chunk == ch + 1:
                        differences(ch + 1)
                    square(ch)
                    yield 3.4
                    root(ch)
                xs.free = [m_g, m_i]
                xt.free = [m_z]
                dt_t[u].free = [m_xdt]
                cum_t[u].free = [m_d1, m_e, m_ec]
                ecum[u].free = [m_y]

            prep = ExitStack()
            with prep:
                lw = sb(prep, "lw", [P, KD], F32)
                lb = sb(prep, "lb", [P, KD], F32)
                gm = sb(prep, "gm", [P, KI], F32)
                lb_bc = sb(prep, "lb_bc", [P, KD, P], F32)
                bias_bc = sb(prep, "bias_bc", [P, WC + NH], F32)
                al = sb(prep, "al", [P, NH], F32)
                w_routes = sb(prep, "w_routes", [P, KD, 2 * G], F32)
                wout_f = sb(prep, "wout_f", [P, KI, D], F32)
                NC5 = 5
                CW = (WC + NH) // NC5
                stage = [Slot(sb(prep, f"stage{i}", [P, KD, CW], F32), sem(f"s_stage{i}")) for i in range(2)]
                lw64 = sb(prep, "lw64", [P, KD], F32)
                gm64 = sb(prep, "gm64", [P, KI], F32)
                for dst, src in ((lw[:], ln_w.rearrange("(k p) -> p k", p=P)),
                                 (lb[:], ln_b.rearrange("(k p) -> p k", p=P)),
                                 (gm[:], gamma.rearrange("(k p) -> p k", p=P)),
                                 (al[:], a_log.partition_broadcast(P)),
                                 (d_bc[:], d_skip.partition_broadcast(P)),
                                 (dt_b[:], dt_bias.partition_broadcast(P)),
                                 (taps[:], conv_w.rearrange("(c p) t -> p c t", p=P)),
                                 (conv_bias[:], conv_b.rearrange("(c p) -> p c", p=P)),
                                 (w_routes[:], w_route.rearrange("(k p) r -> p k r", p=P))):
                    small = load_small.landed(sp.dma_start(dst, src, allow_slow_non_contiguous=True))
                m_wof = load_wout.landed(sp.dma_start(wout_f[:], w_out.rearrange("(k p) n -> p k n", p=P)))
                V.after(small, m_wof)
                A.after(small, m_wof)
                m = A.done(ac.activation(a_neg[:], al[:], ACT.Exp))
                V.after(m)
                V.done(ve.tensor_scalar(a_neg[:], a_neg[:], -1.0, None, ALU.mult))
                V.done(ve.tensor_scalar(taps[:], taps[:], 0.5, None, ALU.mult))
                V.done(ve.tensor_scalar(conv_bias[:], conv_bias[:], 0.5, None, ALU.mult))
                V.done(ve.tensor_scalar(lw64[:], lw[:], WS, None, ALU.mult))
                m = V.done(ve.tensor_scalar(gm64[:], gm[:], WS, None, ALU.mult))
                m_lb = V.done(ve.tensor_copy(lb_bc[:], lb[:].unsqueeze(2).to_broadcast([P, KD, P])))
                A.after(m)
                V.after(m_lb)
                m = A.done(ac.mul(shi[:, :, 0:2 * G], w_routes[:], WS))
                V.after(m)
                V.done(ve.scalar_tensor_tensor(slo[:, :, 0:2 * G], w_routes[:], WS, shi[:, :, 0:2 * G],
                                               ALU.mult, ALU.subtract))
                for k in range(KI):
                    m = A.done(ac.activation(ohi[:, k, :], wout_f[:, k, :], ACT.Copy, scale=gm64[:, k:k + 1]))
                    V.after(m)
                    V.done(ve.scalar_tensor_tensor(olo[:, k, :], wout_f[:, k, :], gm64[:, k:k + 1],
                                                   ohi[:, k, :], ALU.mult, ALU.subtract))
                PE.after(m_lb)
                wr = w_in.rearrange("(k p) n -> p k n", p=P)
                first = Feed(chain(statistics(0), front(0)), 49)
                normalised = 2 * 2.0 + CK * (1.2 + 1.2 + 0.9) + 1.6 - 0.01
                for n in range(NC5):
                    first.to((n + 1) / NC5 * normalised / first.total)
                    s = stage[n % 2]
                    SP.after(s.free)
                    got = s.landed(sp.dma_start(s.t[:], wr[:, :, n * CW:(n + 1) * CW]))
                    A.after(got)
                    V.after(got)
                    PE.after(got)
                    bk = bank("single")
                    for k in range(KD):
                        ins = pe.matmul(bk.t[:, 0:CW], lb_bc[:, k, :], s.t[:, k, :], start=k == 0, stop=k == KD - 1)
                    m_pe = PE.done(ins)
                    A.after(m_pe)
                    m_b = A.done(ac.copy(bias_bc[:, n * CW:(n + 1) * CW], bk.t[:, 0:CW]))
                    bk.free = [m_b]
                    last = n == NC5 - 1
                    for k in range(KD):
                        w = min(CW, WC - n * CW)
                        m = A.done(ac.activation(whi[:, k, n * CW:n * CW + w], s.t[:, k, 0:w], ACT.Copy,
                                                 scale=lw64[:, k:k + 1]))
                        if last:
                            m = A.done(ac.activation(shi[:, k, 2 * G:], s.t[:, k, w:CW], ACT.Copy,
                                                     scale=lw64[:, k:k + 1]))
                        V.after(m)
                        m_v = V.done(ve.scalar_tensor_tensor(wlo[:, k, n * CW:n * CW + w], s.t[:, k, 0:w],
                                                             lw64[:, k:k + 1], whi[:, k, n * CW:n * CW + w],
                                                             ALU.mult, ALU.subtract))
                        if last:
                            m_v = V.done(ve.scalar_tensor_tensor(slo[:, k, 2 * G:], s.t[:, k, w:CW],
                                                                 lw64[:, k:k + 1], shi[:, k, 2 * G:],
                                                                 ALU.mult, ALU.subtract))
                    s.free = [m_pe, m_v]
                V.after(m_b)
                V.done(ve.memset(z_bias[:], 0.0))
                m = V.done(ve.memset(ones[:], 1.0))
                A.after(m)
                m = A.done(ac.mul(z_bias[32:33, :], bias_bc[32:33, 0:DI], WS))
                V.after(m)
                V.done(ve.scalar_tensor_tensor(z_bias[0:1, :], bias_bc[32:33, 0:DI], WS, z_bias[32:33, :],
                                               ALU.mult, ALU.subtract))
                V.done(ve.tensor_tensor(dt_b[:], dt_b[:], bias_bc[:, WC:], ALU.add))
                PE.after(m_b)
                for c in range(NCT):
                    bk = bank("single")
                    m = PE.done(pe.transpose(bk.t[:, 0:P], bias_bc[:, DI + c * P:DI + (c + 1) * P], id32))
                    V.after(m)
                    m_v = V.done(ve.tensor_copy(raw_bias[:, c:c + 1], bk.t[:, 0:1]))
                    bk.free = [m_v]
                w_ready = [m_v, m]

            for e in (PE, V, A, Q, SP):
                e.after(w_ready)

            dts = sb(mam, "dts", [P, 5, CK * NH], F32)
            dt_t = [Slot(sb(mam, f"dt{i}", [P, CK, NH], F32)) for i in range(2)]
            cum_t = [Slot(sb(mam, f"cum{i}", [P, CK, NH], F32)) for i in range(2)]
            ecum = [Slot(sb(mam, f"ecum{i}", [P, CK, NH], F32)) for i in range(2)]
            cumT = Slot(sb(mam, "cumT", [NH, BLK], F32), sem("s_cumT"))
            raw = [Slot(sb(mam, f"raw{i}", [P, BLK + TAPS - 1], F32)) for i in range(2)]
            halo = sb(mam, "halo", [P, NCT, TAPS - 1], F32)
            cv = [Slot(sb(mam, f"cv{i}", [P, BLK], F32)) for i in range(2)]
            xsT = [Slot(sb(mam, f"xsT{i}", [P, NCT, BLK], F32)) for i in range(2)]

            bc = Slot(sb(mam, "bc", [P, NH, P], F32), sem("s_bc"))
            de = Slot(sb(mam, "de", [P, NH, P], F32))
            skipb = [Slot(sb(mam, f"skipb{i}", [P, D], F32), sem(f"s_skipb{i}")) for i in range(2)]
            s_acc = [sem(f"s_acc{i}") for i in range(2)]
            accw = [Slot(None, s) for s in s_acc]
            xdt = Slot(sb(mam, "xdt", [P, NH, HD], F32))
            dxs = Slot(sb(mam, "dxs", [P, NH, HD], F32))
            xw = Slot(sb(mam, "xw", [P, NH, HD], F32))
            state = [Slot(sb(mam, f"state{i}", [P, NH, HD], F32)) for i in range(2)]
            btok = Slot(sb(mam, "btok", [P, P], F32))
            gmask = Slot(sb(mam, "gmask", [P, P], F32))
            decs = Slot(sb(mam, "decs", [P, 3, NH], F32))
            zs = Slot(sb(mam, "zs", [P, DI], F32))
            yb = Slot(sb(mam, "yb", [P, NH, HD], F32))
            yn = sb(mam, "yn", [P, 3], F32)
            yhl = Slot(sb(mam, "yhl", [P, 2, DI], F16))
            yT = Slot(sb(mam, "yT", [P, 2 * KI, P], F16))
            bc.chunk = de.chunk = None
            first.to(1)
            for i in range(NBLK):
                weave(Feed(back(i), CK * 19.2), *([Feed(front(i + 1), 44.5)] if i + 1 < NBLK else []))
            for step in (split_high, split_low, turn_y):
                step(NBLK * CK - 1)
            Feed(project(NBLK * CK - 1), 1).to(1)
            mamba_end = [m for m in (acc_marks[-1], acc_marks[-2], row_marks[-1], skip_marks[NBLK - 1])]
            mamba_end += [(e.key, e.sem, e.n) for e in (PE, V, A, Q)]

        for e in (PE, V, A, Q, SP):
            e.after(mamba_end)

        NW = 4 * D
        wts = [[Slot(sb(ctx, f"w{h}{i}", [P, KD, NW], F16)) for h in ("hi", "lo")] for i in range(2)]
        SC = 256
        wst = [Slot(sb(ctx, f"wst{i}", [P, KD, SC], F32), sem(f"s_wst{i}")) for i in range(2)]
        rbc = [Slot(sb(ctx, f"rbc{i}", [P, L], F16), sem(f"s_rbc{i}")) for i in range(2)]
        rjunk = sb(ctx, "rjunk", [P, L], F16)
        slot_f = sb(ctx, "slot_f", [P, QT + KT], F32)
        slot_i = [Slot(sb(ctx, f"slot_i{i}", [P, QT + KT], I32)) for i in range(2)]
        gat = [Slot(sb(ctx, f"gat{i}", [P, ROW], F32), sem(f"s_gat{i}")) for i in range(QT + KT)]
        KW = NK + 2
        kb = [Slot(sb(ctx, f"kb{i}", [P, H, NK], F16)) for i in range(2)]
        vhi = [Slot(sb(ctx, f"vhi{i}", [P, KT, H, DH + 1], F16)) for i in range(2)]
        nkf = [Slot(sb(ctx, f"nkf{i}", [DH, H], F32), sem(f"s_nkf{i}")) for i in range(2)]
        nkl = [Slot(sb(ctx, f"nkl{i}", [DH, 2, H], F16)) for i in range(2)]
        nvf = [Slot(sb(ctx, f"nvf{i}", [H, DH + 1], F32), sem(f"s_nvf{i}")) for i in range(2)]
        nvd = sb(ctx, "nvd", [H, H, DH + 1], F32)
        nvb = [Slot(sb(ctx, f"nvb{i}", [96, H, DH + 1], F16)) for i in range(2)]
        pnm = sb(ctx, "pnm", [P, QT, 104], F16)
        res = [Slot(sb(ctx, f"res{i}", [P, D], F32), sem(f"s_res{i}")) for i in range(2)]
        SCALE = DH ** -0.5
        m = Q.done(po.memset(pnm[:], 0.0))
        for i in range(2):
            m = Q.done(po.memset(nvb[i].t[:], 0.0))
            m = Q.done(po.memset(vhi[i].t[:], 1.0))
            m_ms = A.done(ac.mul(kb[i].t[DH:DH + H, :, :], cst[0:H, C_ID:C_ID + H].unsqueeze(2).to_broadcast([H, H, NK]), MS))
            m = Q.done(po.memset(nvf[i].t[:], 1.0))
        m_z = Q.done(po.memset(res[0].t[:], 0.0))
        zero_rows = Slot(None, sem("s_zero_rows"))
        SP.after(m_z)
        SP.after(load_null.landed(sp.dma_start(res[0].t[1:2, :], null_tok)))
        for b in range(NB):
            m_zero = zero_rows.landed(sp.dma_start(res_d[b][0:RES0, :], res[0].t[:]))
        res[0].free = [m_zero]
        for e in (PE, V, A, Q):
            e.after(m_z, m_ms)

        def split_weights(g):
            wh, wl = wts[g % 2]
            for n in range(NW // SC):
                s = wst[n % 2]
                c0_ = n * SC
                src = (wq[g][:, c0_:c0_ + SC] if c0_ < D else wkv[g][:, c0_ - D:c0_ - D + SC] if c0_ < 3 * D
                       else wo[g][:, c0_ - 3 * D:c0_ - 3 * D + SC])
                SP.after(s.free)
                got = s.landed(sp.dma_start(s.t[:], src.rearrange("(k p) n -> p k n", p=P)))
                cs = slice(n * SC, (n + 1) * SC)
                A.after(got, wh.free if n == 0 else None)
                A.done(ac.mul(wh.t[:, :, cs], s.t[:], WS))
                m = A.done(ac.mul(s.t[:], s.t[:], WS))
                Q.after(m, wl.free if n == 0 else None)
                m = Q.done(po.tensor_tensor(wl.t[:, :, cs], s.t[:], wh.t[:, :, cs], ALU.subtract))
                s.free = [m]
                yield 1
            wl.ready = m
            nk, nv, nl, nb = nkf[g % 2], nvf[g % 2], nkl[g % 2], nvb[g % 2]
            SP.after(nk.free, nv.free)
            m_k = nk.landed(sp.dma_start(nk.t[:], null_k[g], allow_slow_non_contiguous=True))
            m_v = nv.landed(sp.dma_start(nv.t[:, 0:DH], null_v[g]))
            V.after(m_k, m_v, nl.free, nb.free)
            m = V.done(ve.tensor_copy(nl.t[:, 0, :], nk.t[:]))
            V.after(m)
            m = V.done(ve.tensor_tensor(nl.t[:, 1, :], nk.t[:], nl.t[:, 0, :], ALU.subtract))
            nk.free = [m]
            m = V.done(ve.tensor_tensor(nvd[:], nv.t[:].unsqueeze(1).to_broadcast([H, H, DH + 1]),
                                        cst[0:H, C_ID:C_ID + H].unsqueeze(2).to_broadcast([H, H, DH + 1]), ALU.mult))
            nv.free = [m]
            V.after(m)
            m = V.done(ve.tensor_copy(nb.t[0:H], nvd[:]))
            V.after(m)
            V.done(ve.tensor_copy(nb.t[32:32 + H], nvd[:]))
            m = V.done(ve.tensor_tensor(nb.t[64:64 + H], nvd[:], nb.t[0:H], ALU.subtract))
            nb.ready = m
            yield 1


        def route(n):
            g, b = divmod(n, NB)
            si = slot_i[n % 2]
            for kind, r, nt, off in (("q", b * 2 * G + g, QT, 0), ("k", b * 2 * G + G + g, KT, QT)):
                s = rbc[0 if kind == "q" else 1]
                SP.after(s.free)
                got = s.landed(sp.dma_start(s.t[:], rank_d[r].partition_broadcast(P)))
                yield 0.1
                V.after(got)
                for j in range(nt):
                    m = V.done(ve.tensor_scalar(rjunk[:], s.t[:], cst[:, C_J + j:C_J + j + 1], 0.0, ALU.is_le, ALU.add,
                                                accum_out=slot_f[:, off + j:off + j + 1]))
                    V.after(m)
                s.free = [m]
            V.after(si.free)
            m_si = V.done(ve.tensor_scalar(si.t[:], slot_f[:], float(b * L), None, ALU.add))
            yield 0.1
            got = []
            for j in range(QT + KT):
                t = gat[j]
                Q.after(m_si, t.free)
                t.got = t.landed(po.indirect_dma_start(
                    t.t[:], None, rows_d, bass.IndirectOffsetOnAxis(ap=si.t[:, j:j + 1], axis=0)))
                got.append(t.got)
                if j % 2:
                    yield 0.1
            si.free = got

        idx_tok = sb(ctx, "idx_tok", [P, TPS, NR], I32)
        cnt = sb(ctx, "cnt", [P, TPS, NB], F32)
        s_rank = Slot(None, sem("s_rank"))
        top = ExitStack()
        with top:
            lg = sb(top, "lg", [NR, L], F32)
            junk = sb(top, "junk", [NR, L], F32)
            gt = sb(top, "gt", [NR, L], F32)
            eq = sb(top, "eq", [NR, L], F32)
            rk = sb(top, "rk", [NR, L], F32)
            zero = sb(top, "zero", [NR, L], F32)
            rk16 = sb(top, "rk16", [NR, L], F16)
            key = sb(top, "key", [NR, 4], I32)
            num = sb(top, "num", [NR, 4], F32)
            idx_f = sb(top, "idx_f", [P, TPS, NR], F32)
            none = sb(top, "none", [P, TPS, NB], F32)
            selt = sb(top, "selt", [P, TPS, NR], F32)
            PE.after([(V.key, V.sem, V.n)])
            for c in range(TPS):
                bk = bank("single")
                m = PE.done(pe.transpose(bk.t[0:NR, 0:P], logit[:, c, :, :].rearrange("p b j -> p (b j)"), id32))
                V.after(m)
                m = V.done(ve.tensor_copy(lg[:, c * P:(c + 1) * P], bk.t[0:NR, 0:P]))
                bk.free = [m]
            V.done(ve.memset(zero[:], 0.0))
            V.done(ve.memset(key[:, 0:1], -1))
            m = V.done(ve.memset(key[:, 1:2], 0))
            found, cand, ok = (key[:, j:j + 1] for j in range(3))
            val = cand.bitcast(F32)
            ks = cst[0:NR, C_K:C_K + 1]

            first_weights = Feed(split_weights(0), NW // SC + 1)
            for bit in range(31, -1, -1):
                first_weights.to((31 - bit) / 24)
                V.after(m)
                if bit < 31:
                    m = V.done(ve.tensor_scalar(cand, found, 1 << bit, None, ALU.bitwise_xor))
                    V.after(m)
                m = V.done(ve.tensor_scalar(junk[:], lg[:], val, 0.0, ALU.is_ge, ALU.add, accum_out=num[:, 1:2]))
                V.after(m)
                m = V.done(ve.tensor_tensor(ok, num[:, 1:2], ks, ALU.is_ge))
                V.after(m)
                m = V.done(ve.copy_predicated(found, ok, cand))
            V.after(m)
            val = found.bitcast(F32)
            m = V.done(ve.tensor_scalar(gt[:], lg[:], val, 0.0, ALU.is_gt, ALU.add, accum_out=num[:, 1:2]))
            m2 = V.done(ve.tensor_scalar(eq[:], lg[:], val, None, ALU.is_equal))
            V.after(m2)
            m = V.done(ve.tensor_tensor(num[:, 2:3], ks, num[:, 1:2], ALU.subtract))
            m = V.done(ve.tensor_tensor_scan(rk[:], eq[:], zero[:], 0.0, ALU.add, ALU.add))
            V.after(m)
            m = V.done(ve.scalar_tensor_tensor(eq[:], rk[:], num[:, 2:3], eq[:], ALU.is_le, ALU.mult))
            V.after(m)
            m = V.done(ve.tensor_tensor(gt[:], gt[:], eq[:], ALU.add))
            V.after(m)
            m = V.done(ve.tensor_tensor_scan(rk[:], gt[:], zero[:], 0.0, ALU.add, ALU.add))
            V.after(m)
            m_rk = V.done(ve.tensor_copy(rk16[:], rk[:]))
            SP.after(m_rk)
            m_rank = s_rank.landed(sp.dma_start(rank_d, rk16[:]))
            SP.after(m_rank)
            first_route = Feed(route(0), 0.5)
            first_route.to(0.1)
            m = V.done(ve.scalar_tensor_tensor(eq[:], rk[:], cst[0:NR, C_BASE:C_BASE + 1], gt[:], ALU.add, ALU.mult))
            V.after(m)
            PE.after(m)
            for c in range(TPS):
                bk = bank("single")
                pe.transpose(bk.t[:, 0:NR], eq[:, c * P:(c + 1) * P], cst[0:NR, C_ID:C_ID + NR])
                m = PE.done(pe.transpose(bk.t[:, NR:2 * NR], gt[:, c * P:(c + 1) * P], cst[0:NR, C_ID:C_ID + NR]))
                V.after(m)
                m_ix = V.done(ve.tensor_copy(idx_f[:, c, :], bk.t[:, 0:NR]))
                m = V.done(ve.tensor_copy(selt[:, c, :], bk.t[:, NR:2 * NR]))
                bk.free = [m]
            V.after(m)
            m = V.done(ve.tensor_reduce(cnt[:], selt[:].rearrange("p c (b j) -> p c b j", b=NB)[:, :, :, 0:G], AX.X, ALU.add))
            V.after(m)
            m = V.done(ve.tensor_scalar(none[:], cnt[:], 0.0, None, ALU.is_equal))
            V.after(m)
            idx0 = idx_f[:].rearrange("p c (b j) -> p c b j", b=NB)[:, :, :, 0]
            m = V.done(ve.tensor_tensor(idx0, idx0, none[:], ALU.add))
            V.after(m)
            V.done(ve.tensor_copy(idx_tok[:], idx_f[:]))
            m = V.done(ve.tensor_scalar(cnt[:], cnt[:], 1.0, None, ALU.max))
            V.after(m)
            m_cnt = V.done(ve.reciprocal(cnt[:], cnt[:]))
            top_end = [m_cnt, m_rank]
            first_route.to(1)
        for e in (PE, V, A, Q, SP):
            e.after(top_end)

        kscore = Slot(sb(ctx, "kscore", [P, KT], F32))
        qscore = [Slot(sb(ctx, f"qscore{i}", [P, QT], F32)) for i in range(2)]
        xq = Slot(sb(ctx, "xq", [P, 2 * KD, NQ], F16))
        xk = Slot(sb(ctx, "xk", [P, 2 * KD, NK], F16))
        qa = [Slot(sb(ctx, f"qa{i}", [P, H, NQ], F16)) for i in range(2)]
        qb = [Slot(sb(ctx, f"qb{i}", [P, H, NQ], F16)) for i in range(1)]
        ka = [Slot(sb(ctx, f"ka{i}", [P, H, KW], F16)) for i in range(2)]
        vlo = [Slot(sb(ctx, f"vlo{i}", [P, KT, H, DH], F16)) for i in range(2)]
        smx = sb(ctx, "smx", [P, QT, H], F32)
        snl = sb(ctx, "snl", [P, QT, H], F32)
        pnl = sb(ctx, "pnl", [P, QT, H], F32)
        pnT = sb(ctx, "pnT", [104, NQ], F16)
        pf = [Slot(sb(ctx, f"pf{i}", [P, KT, NQ], F32)) for i in range(2)]
        ph = [Slot(sb(ctx, f"ph{i}", [P, 2, KT, NQ], F16)) for i in range(LAG + 1)]
        rden = sb(ctx, "rden", [P, H, QT], F32)
        of = [Slot(sb(ctx, f"of{i}", [P, QT, DH], F32)) for i in range(2)]
        ohl = Slot(sb(ctx, "ohl", [P, 2, QT, D], F16))
        oT = [Slot(sb(ctx, f"oT{i}", [P, 2 * KD, P], F16)) for i in range(2)]
        accb = [Slot(sb(ctx, f"accb{i}", [P, D], F32), sem(f"s_accb{i}")) for i in range(2)]
        stored = [Slot(None, sem(f"s_out{i}")) for i in range(2)]
        spare = [h.t[:].rearrange("p k n -> p (k n)").bitcast(F32) for h in wts[G % 2]]
        gres = [[Slot(spare[0][:, (i * G + g) * D:(i * G + g + 1) * D], sem(f"s_gres{i}{g}")) for g in range(G)]
                for i in range(2)]
        held = [spare[1][:, c * D:(c + 1) * D] for c in range(TPS)]
        made = {}

        made = {}

        rows_of = {}

        def turn_rows(n):
            g, u = n // NB, n % 2
            for j in range(QT + KT):
                t = gat[j]
                g16 = t.t[:].bitcast(F16)
                PE.after(t.got)
                bk = bank("single")
                b16 = bk.t[:].bitcast(F16)
                for c in range(2 * KD):
                    ins = pe.transpose(b16[:, c * P:(c + 1) * P], g16[:, c * P:(c + 1) * P], id16[:])
                m_t = PE.done(ins)
                V.after(t.got, qscore[u].free if j == 0 else None, kscore.free if j == QT else None)
                if j < QT:
                    m_qs = V.done(ve.tensor_copy(qscore[u].t[:, j:j + 1], t.t[:, D + g:D + g + 1]))
                else:
                    m_qs = V.done(ve.tensor_scalar(kscore.t[:, j - QT:j - QT + 1], t.t[:, D + G + g:D + G + g + 1],
                                                   1.0 / WS, None, ALU.mult))
                t.free = [m_t, m_qs]
                dst, s0 = (xq, j) if j < QT else (xk, j - QT)
                A.after(m_t, dst.free if s0 == 0 else None)
                m_x = A.done(ac.copy(dst.t[:].bitcast(F32)[:, :, s0 * P // 2:(s0 + 1) * P // 2],
                                     bk.t[:].rearrange("p (c t) -> p c t", c=2 * KD)))
                bk.free = [m_x]
                yield 0.43
            rows_of[n] = (m_x, m_qs)

        def prepare(n):
            g, b = divmod(n, NB)
            u = n % 2
            wh, wl = wts[g % 2]
            m_x, m_qs = rows_of[n]
            PE.after(m_x, wl.ready)
            qa_, ka_, kb_, vh, vl = qa[u], ka[u], kb[u], vhi[u], vlo[u]
            nl = nkl[g % 2]
            ahead = Feed(route(n + 1), 0.5) if n + 1 < G * NB else None
            def low_queries(e, bk, m_a):
                V.after(m_a)
                for a in range(2):
                    m_q = V.done(ve.scalar_tensor_tensor(qa_.t[DH:P, 2 * e + a, :], bk.t[a * DH:(a + 1) * DH, :], 1.0 / WS,
                                                         qa_.t[0:DH, 2 * e + a, :], ALU.mult, ALU.subtract))
                bk.free = [m_q]
                return m_q

            part = None
            for e in range(KD):
                bk = bank("single")
                n_ = 0
                for k in range(KD):
                    ws = slice(e * P, (e + 1) * P)
                    for w, ha in ((wh, 0), (wh, 1), (wl, 0)):
                        ins = pe.matmul(bk.t[:], w.t[:, k, ws], xq.t[:, ha * KD + k, :], start=n_ == 0, stop=n_ == 3 * KD - 1)
                        n_ += 1
                m = PE.done(ins)
                A.after(m, qa_.free if e == 0 else None)
                for a in range(2):
                    m_a = A.done(ac.mul(qa_.t[0:DH, 2 * e + a, :], bk.t[a * DH:(a + 1) * DH, :], 1.0 / WS))
                if part:
                    low_queries(*part)
                part = (e, bk, m_a)
                if ahead and e % 2:
                    ahead.to((e // 2 + 1) / 4)
                yield 2.6
            xq.free = [m]
            def low_keys(e2, bk, m_a):
                V.after(m_a, kb_.free if e2 == 0 else None)
                for a in range(2):
                    src = bk.t[a * DH:(a + 1) * DH, :].rearrange("p (e t) -> p e t", e=2)
                    hs = slice(4 * e2 + a, 4 * e2 + a + 3, 2)
                    m_kb = V.done(ve.scalar_tensor_tensor(kb_.t[0:DH, hs, :], src, 1.0 / WS, ka_.t[0:DH, hs, 0:NK],
                                                          ALU.mult, ALU.subtract))
                bk.free = [m_kb]
                return m_kb

            for e2 in range(KD // 2):
                bk = bank("single")
                for e in (2 * e2, 2 * e2 + 1):
                    n_ = 0
                    for k in range(KD):
                        ws = slice(D + e * P, D + (e + 1) * P)
                        for w, ha in ((wh, 0), (wh, 1), (wl, 0)):
                            ins = pe.matmul(bk.t[:, (e % 2) * NK:(e % 2 + 1) * NK], w.t[:, k, ws], xk.t[:, ha * KD + k, :],
                                            start=n_ == 0, stop=n_ == 3 * KD - 1)
                            n_ += 1
                m = PE.done(ins)
                A.after(m, ka_.free if e2 == 0 else None)
                for a in range(2):
                    m_a = A.done(ac.mul(ka_.t[0:DH, 4 * e2 + a:4 * e2 + a + 3:2, 0:NK],
                                        bk.t[a * DH:(a + 1) * DH, :].rearrange("p (e t) -> p e t", e=2), 1.0 / WS))
                if e2 == 0:
                    m_q = low_queries(*part)
                else:
                    low_keys(*part)
                part = (e2, bk, m_a)
                if ahead:
                    ahead.to((e2 + 3) / 4)
                yield 2.6
            m_kb = low_keys(*part)
            V.after(m_kb)
            m_k2 = V.done(ve.tensor_copy(ka_.t[DH:P, :, 0:NK], ka_.t[0:DH, :, 0:NK]))
            V.after(ka_.free)
            V.done(ve.tensor_copy(ka_.t[0:DH, :, NK], nl.t[:, 0, :]))
            m_nk = V.done(ve.tensor_copy(ka_.t[DH:P, :, NK], nl.t[:, 0, :]))
            for j in range(KT):
                bk = bank("single")
                n_ = 0
                for k in range(KD):
                    for ha, w in ((0, wh), (0, wl), (1, wh)):
                        ins = pe.matmul(bk.t[:], xk.t[:, ha * KD + k, j * P:(j + 1) * P], w.t[:, k, 2 * D:3 * D],
                                        start=n_ == 0, stop=n_ == 3 * KD - 1)
                        n_ += 1
                m_mm = PE.done(ins)
                src = bk.t[:].rearrange("p (h d) -> p h d", h=H)
                vsc = kscore.t[:, j:j + 1]
                A.after(m_mm, m_qs, vh.free if j == 0 else None)
                m = A.done(ac.activation(vh.t[:, j, :, 0:DH], src, ACT.Copy, scale=vsc))
                yield 2.6
                V.after(m, vl.free if j == 0 else None)
                m_v = V.done(ve.scalar_tensor_tensor(vl.t[:, j, :, :], src, vsc, vh.t[:, j, :, 0:DH], ALU.mult, ALU.subtract))
                bk.free = [m_v]
            kscore.free = [m, m_v]
            xk.free = [m_mm]
            made[n] = (m_q, m_kb, m_k2, m_nk, m_v, m_qs)

        def maxima(n):
            u = n % 2
            qa_, ka_ = qa[u], ka[u]
            nl, qb_ = nkl[n // NB % 2], qb[0]
            PE.after(*made[n])
            for qt in range(QT):
                qs = slice(qt * P, (qt + 1) * P)
                for h2 in range(H // 2):
                    bk = bank("pair")
                    for a in range(2):
                        h = 2 * h2 + a
                        pe.matmul(bk.t[:, a * 512:a * 512 + NK + 1], qa_.t[:, h, qs], ka_.t[:, h, 0:NK + 1], start=True, stop=False,
                                  skip_group_check=True)
                        ins = pe.matmul(bk.t[:, a * 512 + NK:a * 512 + NK + 1], qa_.t[0:DH, h, qs], nl.t[:, 1, h:h + 1],
                                        start=False, stop=True, skip_group_check=True)
                    m = PE.done(ins)
                    sc = bk.t[:].rearrange("p (a t) -> p a t", a=2)
                    V.after(m)
                    m_mx = V.done(ve.tensor_reduce(smx[:, qt, 2 * h2:2 * h2 + 2], sc[:, :, 0:NK + 1], AX.X, ALU.max))
                    m_sn = V.done(ve.tensor_copy(snl[:, qt, 2 * h2:2 * h2 + 2], sc[:, :, NK]))
                    bk.free = [m_sn]
                    if (qt, h2) == (QT - 1, 0):
                        V.after(qb_.free, made[n][0])
                        V.done(ve.tensor_copy(qb_.t[0:DH], qa_.t[0:DH]))
                    yield 0.5
            shift = pnm[:, :, 96:96 + H]
            V.after(m_sn)
            m = V.done(ve.tensor_scalar(shift, smx[:], -1.0 / MS, None, ALU.mult))
            V.after(m)
            m = V.done(ve.scalar_tensor_tensor(pnl[:], shift, MS, snl[:], ALU.mult, ALU.add))
            A.after(m)
            m = A.done(ac.activation(pnl[:], pnl[:], ACT.Exp, scale=SCALE))
            V.after(m)
            m = V.done(ve.tensor_copy(pnm[:, :, 0:H], pnl[:]))
            V.after(m)
            V.done(ve.tensor_copy(pnm[:, :, 64:64 + H], pnl[:]))
            m = V.done(ve.tensor_tensor(pnm[:, :, 32:32 + H], pnl[:], pnm[:, :, 0:H], ALU.subtract))
            yield 1.5
            PE.after(m)
            bk = bank("single")
            b16 = bk.t[:].bitcast(F16)
            for qt in range(QT):
                ins = pe.transpose(b16[0:104, qt * P:(qt + 1) * P], pnm[:, qt, :], id16[:])
            m = PE.done(ins)
            V.after(m)
            m_pT = V.done(ve.tensor_copy(pnT[:], b16[0:104, 0:NQ]))
            bk.free = [m_pT]
            V.after(m_pT)
            m_qb = [V.done(ve.tensor_copy(qb_.t[DH:DH + H, h], pnT[96:96 + H, :])) for h in range(H)]
            turned[n] = (m_qb, m_pT)
            yield 0.2

        turned = {}

        def heads_of(n):
            g, b = divmod(n, NB)
            u = n % 2
            qa_, ka_, kb_, vh, vl = qa[u], ka[u], kb[u], vhi[u], vlo[u]
            nb, qb_ = nvb[g % 2], qb[0]
            m_qb, m_pT = turned[n]

            def scores(h):
                PE.after(m_qb[h])
                bk = bank("pair")
                for j in range(KT):
                    o = bk.t[:, j * NQ:(j + 1) * NQ]
                    pe.matmul(o, ka_.t[:, h, j * P:(j + 1) * P], qa_.t[:, h, :], start=True, stop=False)
                    ins = pe.matmul(o, kb_.t[0:DH + H, h, j * P:(j + 1) * P], qb_.t[0:DH + H, h, :], start=False, stop=True)
                m_s = PE.done(ins)
                f, p_ = pf[h % 2], ph[h % (LAG + 1)]
                A.after(m_s, f.free)
                m = A.done(ac.activation(f.t[:].rearrange("p k q -> p (k q)"), bk.t[:], ACT.Exp, scale=SCALE))
                bk.free = [m]
                A.after(m, p_.free)
                m_h = A.done(ac.copy(p_.t[:, 0], f.t[:]))
                m_l = []
                for j, E, e in ((0, V, ve), (1, Q, po)):
                    E.after(m_h)
                    m_l.append(E.done(e.tensor_tensor(p_.t[:, 1, j], f.t[:, j], p_.t[:, 0, j], ALU.subtract)))
                f.free = m_l
                return m_s, m_l

            def values(h, m_l):
                p_ = ph[h % (LAG + 1)]
                PE.after(m_l, m_pT, nb.ready)
                bk = bank("single")
                for qt in range(QT):
                    qs = slice(qt * P, (qt + 1) * P)
                    o = bk.t[:, qt * (DH + 1):(qt + 1) * (DH + 1)]
                    pe.matmul(o, pnT[0:96, qs], nb.t[:, h, :], start=True, stop=False, skip_group_check=True)
                    for j in range(KT):
                        pe.matmul(o, p_.t[:, 0, j, qs], vh.t[:, j, h, :], start=False, stop=False, skip_group_check=True)
                        pe.matmul(o[:, 0:DH], p_.t[:, 0, j, qs], vl.t[:, j, h, :], start=False, stop=False, skip_group_check=True)
                        ins = pe.matmul(o, p_.t[:, 1, j, qs], vh.t[:, j, h, :], start=False, stop=j == KT - 1, skip_group_check=True)
                m = PE.done(ins)
                p_.free = [m]
                o3 = bk.t[:, 0:QT * (DH + 1)].rearrange("p (q d) -> p q d", q=QT)
                V.after(m)
                m1 = V.done(ve.reciprocal(rden[:, h, :], o3[:, :, DH]))
                V.after(m1)
                m1 = V.done(ve.tensor_tensor(rden[:, h, :], rden[:, h, :], qscore[u].t[:], ALU.mult))
                f = of[h % 2]
                V.after(m1, f.free)
                m1 = V.done(ve.tensor_tensor(f.t[:], o3[:, :, 0:DH], rden[:, h, :].unsqueeze(2).to_broadcast([P, QT, DH]), ALU.mult))
                bk.free = [m1]
                A.after(m1, ohl.free if h == 0 else None)
                m2 = A.done(ac.copy(ohl.t[:, 0, :, h * DH:(h + 1) * DH], f.t[:]))
                Q.after(m2)
                m2 = Q.done(po.tensor_tensor(ohl.t[:, 1, :, h * DH:(h + 1) * DH], f.t[:],
                                             ohl.t[:, 0, :, h * DH:(h + 1) * DH], ALU.subtract))
                f.free = [m2]
                return m, m1, m2

            wait = []
            for h in range(H + LAG):
                if h < H:
                    wait.append(scores(h))
                    yield 0.85
                if h >= LAG:
                    m_pv, m_on, m_ohl = values(h - LAG, wait[h - LAG][1])
                    yield 0.76
            m_s = wait[-1][0]
            qa_.free = [m_s]
            qb_.free = [m_s]
            ka_.free = [m_s]
            kb_.free = [m_s]
            vh.free = [m_pv]
            vl.free = [m_pv]
            qscore[u].free = [m_on]
            if b == NB - 1:
                nkl[g % 2].free = [m_pv]
                nvb[g % 2].free = [m_pv]
            ohl.ready = m_ohl

        def finish(n):
            g, b = divmod(n, NB)
            wh, wl = wts[g % 2]
            PE.after(ohl.ready)
            for qt in range(QT + 1):
                if qt < QT:
                    bk = bank("single")
                    b16 = bk.t[:].bitcast(F16)
                    for j in range(2 * KD):
                        ins = pe.transpose(b16[:, j * P:(j + 1) * P], ohl.t[:, j // KD, qt, (j % KD) * P:(j % KD + 1) * P], id16[:])
                    m = PE.done(ins)
                    if qt == QT - 1:
                        ohl.free = [m]
                    o_ = oT[qt % 2]
                    A.after(m, o_.free)
                    o_.ready = A.done(ac.copy(o_.t[:].bitcast(F32).rearrange("p j t -> p (j t)"), bk.t[:]))
                    bk.free = [o_.ready]
                    yield 0.43
                if qt == 0:
                    continue
                qt -= 1
                o_ = oT[qt % 2]
                PE.after(o_.ready)
                bk = bank("single")
                n_ = 0
                for k in range(KD):
                    for ha, w in ((0, wh), (0, wl), (1, wh)):
                        ins = pe.matmul(bk.t[:], o_.t[:, ha * KD + k, :], w.t[:, k, 3 * D:4 * D], start=n_ == 0, stop=n_ == 3 * KD - 1)
                        n_ += 1
                    if k == KD // 2 - 1:
                        yield 1.3
                m = PE.done(ins)
                o_.free = [m]
                r_ = res[qt % 2]
                A.after(m, r_.free)
                m1 = A.done(ac.mul(r_.t[:], bk.t[:], 1.0 / WS))
                bk.free = [m1]
                SP.after(m1)
                r0 = RES0 + g * NQ + qt * P
                m2 = r_.landed(sp.dma_start(res_d[b][r0:r0 + P, :], r_.t[:]))
                r_.free = [m2]
                last[qt % 2] = m2
                yield 1.3
            if b == NB - 1:
                wh.free = [m]
                wl.free = [m]

        last = [m_zero, m_zero]

        def fetch(b, s, c, g, ready=G):
            Q.after(s.free, *last, [w.free for w in wts[G % 2]])
            s.got = s.landed(po.indirect_dma_start(
                s.t, None, res_d[b][0:RES0 + ready * NQ, :], bass.IndirectOffsetOnAxis(ap=idx_tok[:, c, b * 2 * G + g:b * 2 * G + g + 1], axis=0)))

        def load_acc(b, c):
            a_ = accb[c % 2]
            SP.after(a_.free)
            r0 = (b * TPS + c) * P
            a_.got = a_.landed(sp.dma_start(a_.t[:], acc_d[r0:r0 + P, :]))

        def store_out(b, c, total, m):
            a_, o_ = accb[c % 2], stored[c % 2]
            V.after(a_.got, m)
            m = V.done(ve.scalar_tensor_tensor(a_.t[:], total, cnt[:, c, b:b + 1], a_.t[:], ALU.mult, ALU.add))
            SP.after(m)
            r0 = (b * TPS + c) * P
            o_.got = o_.landed(sp.dma_start(out[r0:r0 + P, :], a_.t[:]))
            a_.free = [o_.got]
            return m

        def combine(b):
            for c in range(TPS + 1):
                if c < TPS:
                    for g in range(G):
                        fetch(b, gres[c % 2][g], c, g)
                        if g % 2:
                            yield 1
                    load_acc(b, c)
                if c > 0:
                    s = gres[(c - 1) % 2]
                    a0, a1, a2, a3 = (r.t for r in s)
                    V.after([r.got for r in s])
                    V.done(ve.tensor_tensor(a0, a0, a1, ALU.add))
                    m = V.done(ve.tensor_tensor(a2, a2, a3, ALU.add))
                    V.after(m)
                    m = V.done(ve.tensor_tensor(a0, a0, a2, ALU.add))
                    m = store_out(b, c - 1, a0, m)
                    for r in s:
                        r.free = [m]
                    yield 1

        def hold(b):
            for c in range(TPS + 1):
                if c < TPS:
                    for g in range(G - 1):
                        fetch(b, gres[c % 2][g], c, g, G - 1)
                        yield 1
                if c > 0:
                    s = gres[(c - 1) % 2]
                    V.after([r.got for r in s[:G - 1]])
                    m = V.done(ve.tensor_tensor(held[c - 1], s[0].t, s[1].t, ALU.add))
                    V.after(m)
                    m = V.done(ve.tensor_tensor(held[c - 1], held[c - 1], s[2].t, ALU.add))
                    for r in s[:G - 1]:
                        r.free = [m]
                    yield 1

        def combine_held(b):
            rows = [gres[c // G][c % G] for c in range(TPS)]
            for c in range(TPS):
                fetch(b, rows[c], c, G - 1)
            for c in range(TPS):
                load_acc(b, c)
                V.after(rows[c].got)
                m = V.done(ve.tensor_tensor(held[c], held[c], rows[c].t, ALU.add))
                rows[c].free = [store_out(b, c, held[c], m)]

        items = G * NB
        SPLIT, LEAD = 0.7, 1.2
        for gen in (turn_rows(0), prepare(0), turn_rows(1), maxima(0)):
            Feed(gen, 1).to(1)
        for n in range(items):
            heads, ends = [], []
            if n % NB == 2 and n // NB + 1 < G:
                heads.append(Feed(split_weights(n // NB + 1), NW // SC + 1))
            if n + 1 < items:
                following = Feed(chain(prepare(n + 1), maxima(n + 1)), 30.5)
                heads.append(Part(following, 0, SPLIT))
                ends.append(Part(following, SPLIT, LEAD))
            if n // NB == G - 1:
                merge = (Feed(combine(n % NB - 1), 3 * TPS) if n % NB else Feed(hold(NB - 1), G * TPS))
                heads.append(Part(merge, 0, 0.6))
                ends.append(Part(merge, 0.6, 1))
            if n + 2 < items:
                ends.append(Feed(turn_rows(n + 2), (QT + KT) * 0.43))
            weave(Feed(heads_of(n), 12.9), *heads)
            weave(Feed(finish(n), 12.1), *ends)
        combine_held(NB - 1)
        SP.after(*[o.got for o in stored], *last)


def kernel(L0_attn_x, L0_attn_ln_w, L0_attn_ln_b, L0_attn_in_proj_w, L0_attn_conv_w, L0_attn_conv_b,
           L0_attn_A_log, L0_attn_D, L0_attn_dt_bias, L0_attn_gamma, L0_attn_out_proj_w, L0_ffn_w_qr,
           L0_ffn_w_kvr, L0_ffn_w_q, L0_ffn_w_kv, L0_ffn_w_out, L0_ffn_null_kv, L0_ffn_null_token):
    import numpy as np
    import concourse.bacc as bacc
    from concourse.bass_utils import run_bass_kernel_spmd

    c = np.zeros((P, C_N), np.float32)
    c[:, C_ID:C_ID + P] = np.eye(P)
    c[:, C_U:C_U + P] = np.triu(np.ones((P, P)))
    for j in range(QT):
        c[:, C_J + j] = j * P + np.arange(P)
    for r in range(NR):
        b, j = divmod(r, 2 * G)
        c[r, C_K] = NQ if j < G else NK
        c[r, C_BASE] = RES0 + j * NQ - 1 if j < G else 0.0
    a = np.asarray
    arrays = {
        "x": a(L0_attn_x).reshape(T, D),
        "w_in": a(L0_attn_in_proj_w).T,
        "ln_w": a(L0_attn_ln_w),
        "ln_b": a(L0_attn_ln_b),
        "conv_w": a(L0_attn_conv_w),
        "conv_b": a(L0_attn_conv_b),
        "a_log": a(L0_attn_A_log),
        "d_skip": a(L0_attn_D),
        "dt_bias": a(L0_attn_dt_bias),
        "gamma": a(L0_attn_gamma),
        "w_out": a(L0_attn_out_proj_w).T,
        "w_route": np.concatenate([a(L0_ffn_w_qr), a(L0_ffn_w_kvr)], 0).T,
        "wq": a(L0_ffn_w_q).transpose(0, 2, 1),
        "wkv": a(L0_ffn_w_kv).transpose(0, 2, 1),
        "wo": a(L0_ffn_w_out).transpose(0, 2, 1),
        "null_k": a(L0_ffn_null_kv)[0, :, :, 0, :].transpose(0, 2, 1),
        "null_v": a(L0_ffn_null_kv)[1, :, :, 0, :],
        "null_tok": a(L0_ffn_null_token).reshape(D),
        "consts": c,
    }
    nc = bacc.Bacc("TRN2", target_bir_lowering=False, num_devices=1)
    feeds, args = {}, []
    for name, v in arrays.items():
        v = np.ascontiguousarray(v)
        feeds[name] = v
        args.append(nc.dram_tensor(name, v.shape, mybir.dt.from_np(v.dtype), kind="ExternalInput").ap())
    out = nc.dram_tensor("y", (T, D), F32, kind="ExternalOutput").ap()
    program(nc, *args, out)
    r = run_bass_kernel_spmd(nc, [feeds], core_ids=[0])
    return r.results[0]["y"].reshape(NB, L, D)
```
